# Optimizing a Trainium2 kernel written in Bass

```python
import numpy as np
import jax
import jax.numpy as jnp

def _softmax(x, axis=-1):
    return jax.nn.softmax(x, axis=axis)

def _gelu(x):
    return jax.nn.gelu(x, approximate=True)

def _silu(x):
    return jax.nn.silu(x)

def _sigmoid(x):
    return jax.nn.sigmoid(x)

def _layernorm(x, axis=-1, eps=1e-05):
    m = jnp.mean(x, axis=axis, keepdims=True)
    v = jnp.var(x, axis=axis, keepdims=True)
    return (x - m) / jnp.sqrt(v + eps)

def _scatter_add(tgt, idx, src, axis=0):
    return tgt.at[idx].add(src)

def _segment_sum(src, seg, n):
    return jax.ops.segment_sum(src, seg, n)
kernel_name = 'mk_recurrent_d2_jaxref_r8_7bc5c5'

def setup_inputs(seed: int=0):
    np.random.seed(seed)
    _w = jnp.asarray

    def _L0_attn_setup():
        import jax, jax.numpy as jnp
        import numpy as np
        import math
        DIM = 128
        NUM_HEADS = 16
        HEAD_DIM = DIM // NUM_HEADS
        MAX_BIAS = 8.0
        SCALE = HEAD_DIM ** (-0.5)

        def _alibi_slopes(n):

            def pow2(n):
                start = 2.0 ** (-2.0 ** (-(math.log2(n) - 3)))
                return [start * start ** i for i in range(n)]
            if math.log2(n).is_integer():
                return pow2(n)
            c = 2 ** math.floor(math.log2(n))
            return pow2(c) + _alibi_slopes(2 * c)[0::2][:n - c]

        def _rotate_half(t):
            t1, t2 = jnp.split(t, 2, axis=-1)
            return jnp.concatenate([-t2, t1], axis=-1)
        key = jax.random.key(seed)
        k1, k2, k3, k4 = jax.random.split(key, 4)
        B, N, C = (2, 256, DIM)
        x = jax.random.normal(k1, (B, N, C), dtype=jnp.float32)
        qkv_w = jax.random.normal(k2, (3 * C, C), dtype=jnp.float32) * C ** (-0.5)
        proj_w = jax.random.normal(k3, (C, C), dtype=jnp.float32) * C ** (-0.5)
        proj_b = jax.random.normal(k4, (C,), dtype=jnp.float32) * 0.01
        slopes = jnp.asarray(np.array(_alibi_slopes(NUM_HEADS), dtype=np.float32))
        return {'x': x, 'qkv_w': qkv_w, 'proj_w': proj_w, 'proj_b': proj_b, 'slopes': slopes}
    _L0_attn_in = _L0_attn_setup()

    def _L0_ffn_setup():
        import jax, jax.numpy as jnp
        import numpy as np
        DIM = 128
        HIDDEN = 384
        SCALE = 1.0 / 127.0

        def _dequant(w_int, dtype):
            return w_int.astype(dtype) * jnp.asarray(SCALE, dtype)
        key = jax.random.key(seed)
        k_x, k_g, k_u, k_d = jax.random.split(key, 4)
        x = jax.random.normal(k_x, (4, 256, DIM), dtype=jnp.float32)
        w_gate = jax.random.randint(k_g, (HIDDEN, DIM), -127, 128, dtype=jnp.int32)
        w_up = jax.random.randint(k_u, (HIDDEN, DIM), -127, 128, dtype=jnp.int32)
        w_down = jax.random.randint(k_d, (DIM, HIDDEN), -127, 128, dtype=jnp.int32)
        return {'x': x, 'w_gate': w_gate, 'w_up': w_up, 'w_down': w_down}
    _L0_ffn_in = _L0_ffn_setup()

    def _L1_attn_setup():
        import jax, jax.numpy as jnp
        import numpy as np
        DIM = 128
        DEPTH = 4
        D_STATE = 16
        D_CONV = 4
        D_INNER = 2 * DIM
        DT_RANK = (DIM + 15) // 16
        B_SZ, L = (4, 256)

        def _selective_scan(u, delta, A, Bm, Cm, D):

            def step(h, inp):
                u_t, d_t, b_t, c_t = inp
                dA = jnp.exp(d_t[:, :, None] * A)
                h = dA * h + (d_t * u_t)[:, :, None] * b_t[:, None, :]
                y = jnp.einsum('bds,bs->bd', h, c_t)
                return (h, y)
            h0 = jnp.zeros((u.shape[0], u.shape[2], A.shape[1]), u.dtype)
            xs = (u.transpose(1, 0, 2), delta.transpose(1, 0, 2), Bm.transpose(1, 0, 2), Cm.transpose(1, 0, 2))
            _, ys = jax.lax.scan(step, h0, xs)
            return ys.transpose(1, 0, 2) + u * D

        def _mamba_layer(x, in_w, cw, cb, xp_w, dtw, dtb, A_log, D, ow):
            xz = jnp.einsum('bld,ed->ble', x, in_w)
            xi, z = jnp.split(xz, 2, axis=-1)
            xc = jax.lax.conv_general_dilated(xi.transpose(0, 2, 1), cw[:, None, :], window_strides=(1,), padding=[(D_CONV - 1, 0)], feature_group_count=D_INNER, dimension_numbers=('NCH', 'OIH', 'NCH'))
            xc = jax.nn.silu(xc.transpose(0, 2, 1) + cb)
            dbc = jnp.einsum('bld,ed->ble', xc, xp_w)
            dt, Bm, Cm = jnp.split(dbc, [DT_RANK, DT_RANK + D_STATE], axis=-1)
            delta = jax.nn.softplus(jnp.einsum('blr,dr->bld', dt, dtw) + dtb)
            A = -jnp.exp(A_log)
            y = _selective_scan(xc, delta, A, Bm, Cm, D)
            y = y * jax.nn.silu(z)
            return jnp.einsum('bld,od->blo', y, ow)
        key = jax.random.key(seed)
        ks = jax.random.split(key, 10)
        s = 0.02
        x = jax.random.normal(ks[0], (B_SZ, L, DIM), jnp.float32)
        in_proj_w = jax.random.normal(ks[1], (DEPTH, 2 * D_INNER, DIM), jnp.float32) * s
        conv_w = jax.random.normal(ks[2], (DEPTH, D_INNER, D_CONV), jnp.float32) * 0.2
        conv_b = jnp.zeros((DEPTH, D_INNER), jnp.float32)
        x_proj_w = jax.random.normal(ks[3], (DEPTH, DT_RANK + 2 * D_STATE, D_INNER), jnp.float32) * s
        dt_proj_w = jax.random.normal(ks[4], (DEPTH, D_INNER, DT_RANK), jnp.float32) * s
        dt_proj_b = jnp.full((DEPTH, D_INNER), float(np.log(np.expm1(0.01))), jnp.float32)
        A_log = jnp.broadcast_to(jnp.log(jnp.arange(1, D_STATE + 1, dtype=jnp.float32)), (D_INNER, D_STATE))
        A_log = jnp.broadcast_to(A_log, (DEPTH, D_INNER, D_STATE))
        D = jnp.ones((DEPTH, D_INNER), jnp.float32)
        out_proj_w = jax.random.normal(ks[5], (DEPTH, DIM, D_INNER), jnp.float32) * s
        return {'x': x, 'in_proj_w': in_proj_w, 'conv_w': conv_w, 'conv_b': conv_b, 'x_proj_w': x_proj_w, 'dt_proj_w': dt_proj_w, 'dt_proj_b': dt_proj_b, 'A_log': A_log, 'D': D, 'out_proj_w': out_proj_w}
    _L1_attn_in = _L1_attn_setup()

    def _L1_ffn_setup():
        import jax, jax.numpy as jnp
        import numpy as np
        D_MODEL = 128
        D_FF = 512
        NUM_M = 2
        E_ROUTER = 8 * NUM_M - 1
        D_FF_R = D_FF // NUM_M
        TOP_K = NUM_M * 2 - 1
        B, T = (2, 256)

        def _expert_stack(x, W1, b1, W2, b2):
            h = jax.nn.gelu(jnp.einsum('btd,edf->ebtf', x, W1) + b1[:, None, None, :], approximate=False)
            return jnp.einsum('ebtf,efd->ebtd', h, W2) + b2[:, None, None, :]
        key = jax.random.key(seed)
        ks = jax.random.split(key, 12)
        s = lambda fan_in: 1.0 / np.sqrt(fan_in)
        x = jax.random.normal(ks[0], (B, T, D_MODEL), dtype=jnp.float32)
        sW1 = jax.random.uniform(ks[1], (1, D_MODEL, D_FF), jnp.float32, -s(D_MODEL), s(D_MODEL))
        sb1 = jax.random.uniform(ks[2], (1, D_FF), jnp.float32, -s(D_MODEL), s(D_MODEL))
        sW2 = jax.random.uniform(ks[3], (1, D_FF, D_MODEL), jnp.float32, -s(D_FF), s(D_FF))
        sb2 = jax.random.uniform(ks[4], (1, D_MODEL), jnp.float32, -s(D_FF), s(D_FF))
        rW1 = jax.random.uniform(ks[5], (E_ROUTER, D_MODEL, D_FF_R), jnp.float32, -s(D_MODEL), s(D_MODEL))
        rb1 = jax.random.uniform(ks[6], (E_ROUTER, D_FF_R), jnp.float32, -s(D_MODEL), s(D_MODEL))
        rW2 = jax.random.uniform(ks[7], (E_ROUTER, D_FF_R, D_MODEL), jnp.float32, -s(D_FF_R), s(D_FF_R))
        rb2 = jax.random.uniform(ks[8], (E_ROUTER, D_MODEL), jnp.float32, -s(D_FF_R), s(D_FF_R))
        gW = jax.random.uniform(ks[9], (D_MODEL, E_ROUTER), jnp.float32, -s(D_MODEL), s(D_MODEL))
        gb = jax.random.uniform(ks[10], (E_ROUTER,), jnp.float32, -s(D_MODEL), s(D_MODEL))
        return {'x': x, 'sW1': sW1, 'sb1': sb1, 'sW2': sW2, 'sb2': sb2, 'rW1': rW1, 'rb1': rb1, 'rW2': rW2, 'rb2': rb2, 'gW': gW, 'gb': gb}
    _L1_ffn_in = _L1_ffn_setup()
    _d = {'L0_attn_x': _L0_attn_in['x'], 'L0_attn_qkv_w': _L0_attn_in['qkv_w'], 'L0_attn_proj_w': _L0_attn_in['proj_w'], 'L0_attn_proj_b': _L0_attn_in['proj_b'], 'L0_attn_slopes': _L0_attn_in['slopes'], 'L0_ffn_w_gate': _L0_ffn_in['w_gate'], 'L0_ffn_w_up': _L0_ffn_in['w_up'], 'L0_ffn_w_down': _L0_ffn_in['w_down'], 'L1_attn_in_proj_w': _L1_attn_in['in_proj_w'], 'L1_attn_conv_w': _L1_attn_in['conv_w'], 'L1_attn_conv_b': _L1_attn_in['conv_b'], 'L1_attn_x_proj_w': _L1_attn_in['x_proj_w'], 'L1_attn_dt_proj_w': _L1_attn_in['dt_proj_w'], 'L1_attn_dt_proj_b': _L1_attn_in['dt_proj_b'], 'L1_attn_A_log': _L1_attn_in['A_log'], 'L1_attn_D': _L1_attn_in['D'], 'L1_attn_out_proj_w': _L1_attn_in['out_proj_w'], 'L1_ffn_sW1': _L1_ffn_in['sW1'], 'L1_ffn_sb1': _L1_ffn_in['sb1'], 'L1_ffn_sW2': _L1_ffn_in['sW2'], 'L1_ffn_sb2': _L1_ffn_in['sb2'], 'L1_ffn_rW1': _L1_ffn_in['rW1'], 'L1_ffn_rb1': _L1_ffn_in['rb1'], 'L1_ffn_rW2': _L1_ffn_in['rW2'], 'L1_ffn_rb2': _L1_ffn_in['rb2'], 'L1_ffn_gW': _L1_ffn_in['gW'], 'L1_ffn_gb': _L1_ffn_in['gb']}
    _x0 = _d['L0_attn_x']
    _d['L0_attn_x'] = jax.random.normal(jax.random.fold_in(jax.random.key(seed), 1), (2, 1024, 128), dtype=_x0.dtype)
    del _x0
    return _d

def reference(L0_attn_x, L0_attn_qkv_w, L0_attn_proj_w, L0_attn_proj_b, L0_attn_slopes, L0_ffn_w_gate, L0_ffn_w_up, L0_ffn_w_down, L1_attn_in_proj_w, L1_attn_conv_w, L1_attn_conv_b, L1_attn_x_proj_w, L1_attn_dt_proj_w, L1_attn_dt_proj_b, L1_attn_A_log, L1_attn_D, L1_attn_out_proj_w, L1_ffn_sW1, L1_ffn_sb1, L1_ffn_sW2, L1_ffn_sb2, L1_ffn_rW1, L1_ffn_rb1, L1_ffn_rW2, L1_ffn_rb2, L1_ffn_gW, L1_ffn_gb):

    def _L0_attn_ref(x, qkv_w, proj_w, proj_b, slopes):
        import jax, jax.numpy as jnp
        import numpy as np
        import math
        DIM = 128
        NUM_HEADS = 16
        HEAD_DIM = DIM // NUM_HEADS
        MAX_BIAS = 8.0
        SCALE = HEAD_DIM ** (-0.5)

        def _alibi_slopes(n):

            def pow2(n):
                start = 2.0 ** (-2.0 ** (-(math.log2(n) - 3)))
                return [start * start ** i for i in range(n)]
            if math.log2(n).is_integer():
                return pow2(n)
            c = 2 ** math.floor(math.log2(n))
            return pow2(c) + _alibi_slopes(2 * c)[0::2][:n - c]

        def _rotate_half(t):
            t1, t2 = jnp.split(t, 2, axis=-1)
            return jnp.concatenate([-t2, t1], axis=-1)
        B, N, C = x.shape
        H, D = (NUM_HEADS, HEAD_DIM)
        qkv = (x @ qkv_w.T).reshape(B, N, 3, H, D).transpose(2, 0, 3, 1, 4)
        q, k, v = (qkv[0], qkv[1], qkv[2])
        inv_freq = 1.0 / 10000.0 ** (jnp.arange(0, D, 2, dtype=jnp.float32) / D)
        freqs = jnp.arange(N, dtype=jnp.float32)[:, None] * inv_freq[None, :]
        sin = jnp.tile(jnp.sin(freqs), (1, 2))
        cos = jnp.tile(jnp.cos(freqs), (1, 2))
        q = q * cos + _rotate_half(q) * sin
        k = k * cos + _rotate_half(k) * sin
        attn = jnp.einsum('bhqd,bhkd->bhqk', q, k) * SCALE
        pos = jnp.arange(N, dtype=jnp.float32)
        diff = pos[None, :] - pos[:, None]
        diff = jnp.where(diff > 0, 0.0, diff)
        alibi = diff[None, :, :] * slopes[:, None, None] * MAX_BIAS
        attn = attn + alibi[None]
        w = jax.nn.softmax(attn, axis=-1)
        out = jnp.einsum('bhqk,bhkd->bhqd', w, v)
        out = out.transpose(0, 2, 1, 3).reshape(B, N, C)
        return out @ proj_w.T + proj_b

    def _L0_ffn_ref(x, w_gate, w_up, w_down):
        import jax, jax.numpy as jnp
        import numpy as np
        DIM = 128
        HIDDEN = 384
        SCALE = 1.0 / 127.0

        def _dequant(w_int, dtype):
            return w_int.astype(dtype) * jnp.asarray(SCALE, dtype)
        wg = _dequant(w_gate, x.dtype)
        wu = _dequant(w_up, x.dtype)
        wd = _dequant(w_down, x.dtype)
        gate = jnp.einsum('bsd,hd->bsh', x, wg)
        up = jnp.einsum('bsd,hd->bsh', x, wu)
        h = jax.nn.silu(gate) * up
        return jnp.einsum('bsh,dh->bsd', h, wd)

    def _L1_attn_ref(x, in_proj_w, conv_w, conv_b, x_proj_w, dt_proj_w, dt_proj_b, A_log, D, out_proj_w):
        import jax, jax.numpy as jnp
        import numpy as np
        DIM = 128
        DEPTH = 4
        D_STATE = 16
        D_CONV = 4
        D_INNER = 2 * DIM
        DT_RANK = (DIM + 15) // 16
        B_SZ, L = (4, 256)

        def _selective_scan(u, delta, A, Bm, Cm, D):

            def step(h, inp):
                u_t, d_t, b_t, c_t = inp
                dA = jnp.exp(d_t[:, :, None] * A)
                h = dA * h + (d_t * u_t)[:, :, None] * b_t[:, None, :]
                y = jnp.einsum('bds,bs->bd', h, c_t)
                return (h, y)
            h0 = jnp.zeros((u.shape[0], u.shape[2], A.shape[1]), u.dtype)
            xs = (u.transpose(1, 0, 2), delta.transpose(1, 0, 2), Bm.transpose(1, 0, 2), Cm.transpose(1, 0, 2))
            _, ys = jax.lax.scan(step, h0, xs)
            return ys.transpose(1, 0, 2) + u * D

        def _mamba_layer(x, in_w, cw, cb, xp_w, dtw, dtb, A_log, D, ow):
            xz = jnp.einsum('bld,ed->ble', x, in_w)
            xi, z = jnp.split(xz, 2, axis=-1)
            xc = jax.lax.conv_general_dilated(xi.transpose(0, 2, 1), cw[:, None, :], window_strides=(1,), padding=[(D_CONV - 1, 0)], feature_group_count=D_INNER, dimension_numbers=('NCH', 'OIH', 'NCH'))
            xc = jax.nn.silu(xc.transpose(0, 2, 1) + cb)
            dbc = jnp.einsum('bld,ed->ble', xc, xp_w)
            dt, Bm, Cm = jnp.split(dbc, [DT_RANK, DT_RANK + D_STATE], axis=-1)
            delta = jax.nn.softplus(jnp.einsum('blr,dr->bld', dt, dtw) + dtb)
            A = -jnp.exp(A_log)
            y = _selective_scan(xc, delta, A, Bm, Cm, D)
            y = y * jax.nn.silu(z)
            return jnp.einsum('bld,od->blo', y, ow)
        for i in range(DEPTH):
            x = _mamba_layer(x, in_proj_w[i], conv_w[i], conv_b[i], x_proj_w[i], dt_proj_w[i], dt_proj_b[i], A_log[i], D[i], out_proj_w[i])
        return x

    def _L1_ffn_ref(x, sW1, sb1, sW2, sb2, rW1, rb1, rW2, rb2, gW, gb):
        import jax, jax.numpy as jnp
        import numpy as np
        D_MODEL = 128
        D_FF = 512
        NUM_M = 2
        E_ROUTER = 8 * NUM_M - 1
        D_FF_R = D_FF // NUM_M
        TOP_K = NUM_M * 2 - 1
        B, T = (2, 256)

        def _expert_stack(x, W1, b1, W2, b2):
            h = jax.nn.gelu(jnp.einsum('btd,edf->ebtf', x, W1) + b1[:, None, None, :], approximate=False)
            return jnp.einsum('ebtf,efd->ebtd', h, W2) + b2[:, None, None, :]
        shared_enc = _expert_stack(x, sW1, sb1, sW2, sb2).sum(0)
        weights = jax.nn.softmax(x @ gW + gb, axis=-1)
        topv, topi = jax.lax.top_k(weights, TOP_K)
        gated = (jax.nn.one_hot(topi, E_ROUTER, dtype=weights.dtype) * topv[..., None]).sum(axis=-2)
        router_out = _expert_stack(x, rW1, rb1, rW2, rb2)
        router_enc = jnp.einsum('ebtd,bte->btd', router_out, gated)
        return shared_enc + router_enc + x
    x = L0_attn_x
    xn = _layernorm(x, axis=-1)
    s = _L0_attn_ref(xn, L0_attn_qkv_w, L0_attn_proj_w, L0_attn_proj_b, L0_attn_slopes)
    g = _silu(_L0_ffn_ref(xn, L0_ffn_w_gate, L0_ffn_w_up, L0_ffn_w_down))
    x = x + s * g
    xn = _layernorm(x, axis=-1)
    s = _L1_attn_ref(xn, L1_attn_in_proj_w, L1_attn_conv_w, L1_attn_conv_b, L1_attn_x_proj_w, L1_attn_dt_proj_w, L1_attn_dt_proj_b, L1_attn_A_log, L1_attn_D, L1_attn_out_proj_w)
    g = _silu(_L1_ffn_ref(xn, L1_ffn_sW1, L1_ffn_sb1, L1_ffn_sW2, L1_ffn_sb2, L1_ffn_rW1, L1_ffn_rb1, L1_ffn_rW2, L1_ffn_rb2, L1_ffn_gW, L1_ffn_gb))
    x = x + s * g
    return x

_drawn_inputs = setup_inputs


def setup_inputs(seed=0):
    import zlib

    import numpy as np

    out = dict(_drawn_inputs(seed))
    spreads = {'L1_attn_conv_b': (0.0, 0.1),
     'L1_attn_dt_proj_b': (-4.600165843963623, 0.2),
     'L1_attn_D': (1.0, 0.2)}
    factors = {}
    for name, (base, spread) in spreads.items():
        noise = np.random.default_rng([zlib.crc32(name.encode()), seed]).standard_normal(out[name].shape)
        drawn = base * np.exp(spread * noise) if base else spread * noise
        out[name] = jnp.asarray(drawn.astype(out[name].dtype))
    for name, factor in factors.items():
        out[name] = (out[name] * factor).astype(out[name].dtype)
    return out
```

```python
from contextlib import ExitStack

import concourse.bass as bass
from concourse import mybir

F32 = mybir.dt.float32
BF16 = mybir.dt.bfloat16
I32 = mybir.dt.int32
ALU = mybir.AluOpType
ACT = mybir.ActivationFunctionType
AX = mybir.AxisListType

P = 128
BATCH, SEQ, DIM = 2, 1024, 128
TOK = BATCH * SEQ
TILES = TOK // P
HALF = 512
HEADS, HEAD_DIM = 16, 8
HEADS_PER_GROUP = 4
HEAD_GROUPS = HEADS // HEADS_PER_GROUP
GROUPS = BATCH * HEAD_GROUPS
QT = SEQ // P
PAIR_ROWS = 9 * HEAD_DIM
BIAS_R = 2 * (QT - 1)
BIAS_ROWS = 3 * BIAS_R
MAX_ROW = PAIR_ROWS + BIAS_ROWS
PACK_ROWS = MAX_ROW + 3
RING = 4
MAX_BIAS = 8.0
LN_EPS = 1e-5
HIDDEN = 384
QSCALE = 1.0 / 127.0
EXPERTS = 15
TOP_K = 3


class Core:

    def __init__(self, nc, stack):
        self.nc, self.stack = nc, stack

    def sb(self, name, shape, dt=F32):
        return self.stack.enter_context(self.nc.sbuf_tensor(name, shape, dt))

    def ps(self, name, shape, dt=F32):
        return self.stack.enter_context(self.nc.psum_tensor(name, shape, dt))

    def sem(self, name):
        return self.stack.enter_context(self.nc.semaphore(name))


def layer_norm(nc, whole, tag, x, xn, xnT, ident, loads):
    loaded, stats_done, mv_done, var_done = (whole.sem(f"{tag}_{n}") for n in ("loaded", "stats_done", "mv_done", "var_done"))
    rstd_done, norm_done, turned, copied = (whole.sem(f"{tag}_{n}") for n in ("rstd_done", "norm_done", "turned", "copied"))
    with ExitStack() as st:
        c = Core(nc, st)
        stats = c.sb(f"{tag}_stats", [P, TILES, 6])
        mv = c.sb(f"{tag}_mv", [P, TILES, 2])
        var = c.sb(f"{tag}_var", [P, TILES])
        power = c.sb(f"{tag}_power", [P, TILES])
        rstd = c.sb(f"{tag}_rstd", [P, TILES])
        psT = c.ps(f"{tag}_psT", [P, TOK])
        block = st.enter_context(nc.Block())

        @block.sync
        def _(sp):
            for dst, src in loads:
                sp.dma_start(dst, src).then_inc(loaded, 16)

        @block.gpsimd
        def _(pool):
            pool.memset(power[:, :], -0.5).then_inc(var_done, 1)
            pool.wait_ge(var_done, 2)
            pool.tensor_tensor(rstd[:, :], var[:, :], power[:, :], ALU.pow).then_inc(rstd_done, 1)

        @block.vector
        def _(dve):
            if loads:
                dve.wait_ge(loaded, 16 * len(loads))
            for t in range(TILES):
                dve.bn_stats(stats[:, t, :], x[:, t, :]).then_inc(stats_done, 1)
            for t in range(TILES):
                dve.wait_ge(stats_done, t + 1)
                dve.bn_aggr(mv[:, t, :], stats[:, t, :]).then_inc(mv_done, 1)
            dve.wait_ge(mv_done, TILES)
            dve.tensor_scalar(var[:, :], mv[:, :, 1], LN_EPS, None, ALU.add).then_inc(var_done, 1)
            dve.wait_ge(rstd_done, 1)
            for t in range(TILES):
                dve.tensor_scalar(xn[:, t, :], x[:, t, :], mv[:, t, 0:1], rstd[:, t:t + 1],
                                  ALU.subtract, ALU.mult).then_inc(norm_done, 1)

        @block.tensor
        def _(pe):
            if loads:
                pe.wait_ge(loaded, 16 * len(loads))
            for t in range(TILES):
                pe.wait_ge(norm_done, t + 1)
                pe.transpose(psT[:, t * P:(t + 1) * P], xn[:, t, :], ident[:, :]).then_inc(turned, 1)

        @block.scalar
        def _(act):
            for n in range(TOK // HALF):
                act.wait_ge(turned, 4 * (n + 1))
                act.activation(xnT[:, n * HALF:(n + 1) * HALF], psT[:, n * HALF:(n + 1) * HALF],
                               ACT.Copy).then_inc(copied, 1)


def project_qkv(nc, whole, d, xnT, ident, v_all, tri_all, s8, parts_scr, bias_scr):
    loaded, proj_done, rot_cos, rot_sin, rot_add = (whole.sem(n) for n in ("b_loaded", "b_proj_done", "b_rot_cos", "b_rot_sin", "b_rot_add"))
    part0, rest0, part1, part2 = (whole.sem(n) for n in ("b_part0", "b_rest0", "b_part1", "b_part2"))
    v_done, v_copied, kb_full, kb_part0, kb_rest, kb_part1, kb_part2 = (
        whole.sem(n) for n in ("b_v_done", "b_v_copied", "b_kb_full", "b_kb_part0", "b_kb_rest", "b_kb_part1", "b_kb_part2"))
    tri_done, stored, s8_done = whole.sem("b_tri_done"), whole.sem("b_stored"), whole.sem("b_s8_done")
    with ExitStack() as st:
        c = Core(nc, st)
        w = c.sb("b_w", [P, 5, P])
        cs = c.sb("b_cs", [P, 4, SEQ])
        f = c.sb("b_f", [P, 2, TOK])
        sin_part = c.sb("b_sin_part", [P, 2, HALF])
        parts = c.sb("b_parts", [P, 2, 3, TOK], BF16)
        triT = c.sb("b_triT", [P, P])
        slopes = c.sb("b_slopes", [P, HEADS])
        kb_rows = 8 * BIAS_R
        kc = c.sb("b_kc", [kb_rows, SEQ])
        ks = c.sb("b_ks", [kb_rows, 2])
        kb = c.sb("b_kb", [kb_rows, 2, SEQ])
        kbp = c.sb("b_kbp", [kb_rows, 3, 2, SEQ], BF16)
        pq = c.ps("b_pq", [P, 2, 2, HALF])
        pv = c.ps("b_pv", [P, TILES, P])
        block = st.enter_context(nc.Block())
        N = TOK // HALF

        @block.sync
        def _(sp):
            sp.dma_start(w[:, :, :], d["w_qkv"]).then_inc(loaded, 16)
            sp.dma_start(cs[:, :, :], d["rotation"]).then_inc(loaded, 16)
            sp.dma_start(triT[:, :], d["tri_kq"]).then_inc(loaded, 16)
            sp.dma_start(slopes[:, :], d["slopes"].partition_broadcast(P)).then_inc(loaded, 16)
            sp.dma_start(kc[:, :], d["bias_keys"]).then_inc(loaded, 16)
            sp.dma_start(ks[:, :], d["slopes_rows"]).then_inc(loaded, 16)
            for z in range(2):
                for i, ready in enumerate((part0, part1, part2)):
                    sp.wait_ge(ready, z + 1)
                    for b in range(BATCH):
                        sp.dma_start(parts_scr[z, i, b], parts[:, z, i, b * SEQ:(b + 1) * SEQ]).then_inc(stored, 16)
            for i, ready in enumerate((kb_part0, kb_part1, kb_part2)):
                sp.wait_ge(ready, 1)
                for hh in range(2):
                    for b in range(BATCH):
                        g0 = b * HEAD_GROUPS + 2 * hh
                        sp.dma_start(bias_scr[i, g0:g0 + 2].rearrange("g h r k -> (g h r) k"),
                                     kbp[:, i, hh, :]).then_inc(stored, 16)
            sp.wait_ge(stored, 16 * (12 + 12))

        @block.tensor
        def _(pe):
            pe.wait_ge(loaded, 96)
            for s in range(2 * N):
                n, z = s // 2, s % 2
                if s >= 2:
                    pe.wait_ge(rot_sin, s - 1)
                for j in range(2):
                    mm = pe.matmul(pq[:, s % 2, j, :], w[:, 2 * z + j, :], xnT[:, n * HALF:(n + 1) * HALF],
                                   start=True, stop=True)
                mm.then_inc(proj_done, 1)
                for t in range(2 * s, 2 * s + 2):
                    mm = pe.matmul(pv[:, t, :], xnT[:, t * P:(t + 1) * P], w[:, 4, :], start=True, stop=True)
                mm.then_inc(v_done, 1)

        @block.vector
        def _(dve):
            dve.wait_ge(loaded, 96)
            dve.tensor_scalar(s8[:, :], slopes[:, :], MAX_BIAS, None, ALU.mult).then_inc(s8_done, 1)
            for hh in range(2):
                dve.tensor_scalar(kb[:, hh, :], kc[:, :], ks[:, hh:hh + 1], MAX_BIAS,
                                  ALU.mult, ALU.mult).then_inc(kb_full, 1)
            for s in range(2 * N):
                n, z = s // 2, s % 2
                at = slice((n % 2) * HALF, (n % 2 + 1) * HALF)
                dst = f[:, z, n * HALF:(n + 1) * HALF]
                dve.wait_ge(proj_done, s + 1)
                dve.tensor_tensor(dst, pq[:, s % 2, 0, :], cs[:, 2 * z, at], ALU.mult).then_inc(rot_cos, 1)
                if s >= 2:
                    dve.wait_ge(rot_add, s - 1)
                dve.tensor_tensor(sin_part[:, s % 2, :], pq[:, s % 2, 1, :], cs[:, 2 * z + 1, at],
                                  ALU.mult).then_inc(rot_sin, 1)
                dve.wait_ge(rot_cos, s + 1)
                dve.wait_ge(rot_sin, s + 1)
                dve.tensor_tensor(dst, dst, sin_part[:, s % 2, :], ALU.add).then_inc(rot_add, 1)
            for z in range(2):
                dve.wait_ge(part0, z + 1)
                dve.tensor_tensor(f[:, z, :], f[:, z, :], parts[:, z, 0, :], ALU.subtract).then_inc(rest0, 1)
                dve.wait_ge(part1, z + 1)
                dve.tensor_tensor(parts[:, z, 2, :], f[:, z, :], parts[:, z, 1, :], ALU.subtract).then_inc(part2, 1)

        @block.scalar
        def _(act):
            act.wait_ge(kb_full, 2)
            act.activation(kbp[:, 0, :, :], kb[:, :, :], ACT.Copy).then_inc(kb_part0, 1)
            act.wait_ge(kb_rest, 1)
            act.activation(kbp[:, 1, :, :], kb[:, :, :], ACT.Copy).then_inc(kb_part1, 1)
            for n in range(N):
                act.wait_ge(v_done, 2 * (n + 1))
                b, k0 = 4 * n // QT, 4 * n % QT
                act.activation(v_all[:, b * HEAD_GROUPS:(b + 1) * HEAD_GROUPS, k0:k0 + 4, :].rearrange("p g k x -> p k g x"),
                               pv[:, 4 * n:4 * n + 4, :].rearrange("p k (g x) -> p k g x", g=HEAD_GROUPS),
                               ACT.Copy).then_inc(v_copied, 1)
            for z in range(2):
                act.wait_ge(rot_add, 2 * N)
                act.activation(parts[:, z, 0, :], f[:, z, :], ACT.Copy).then_inc(part0, 1)
                act.wait_ge(rest0, z + 1)
                act.activation(parts[:, z, 1, :], f[:, z, :], ACT.Copy).then_inc(part1, 1)

        @block.gpsimd
        def _(pool):
            pool.wait_ge(loaded, 96)
            pool.wait_ge(s8_done, 1)
            pool.wait_ge(kb_part0, 1)
            pool.tensor_tensor(kb[:, :, :], kb[:, :, :], kbp[:, 0, :, :], ALU.subtract).then_inc(kb_rest, 1)
            pool.wait_ge(kb_part1, 1)
            pool.tensor_tensor(kbp[:, 2, :, :], kb[:, :, :], kbp[:, 1, :, :], ALU.subtract).then_inc(kb_part2, 1)
            for h in range(HEADS):
                pool.tensor_scalar(tri_all[:, h, :], triT[:, :], s8[:, h:h + 1], None, ALU.mult).then_inc(tri_done, 1)


def attention(nc, whole, d, ident, v_all, tri_all, s8, parts_scr, bias_scr, o_all):
    names = ("pack_loaded", "ones_loaded", "scores_ready", "exp_done", "pv_done", "o_copied", "v_ready", "v_fixed",
             "maxs_ready", "maxs_free", "center_done", "max_done", "neg_done", "mp0", "mr0", "mp1", "mr1", "mp2", "m_turned",
             "m_copied", "m_stored", "w_zero", "gtri_loaded", "begun", "sp_begun")
    s = {n: whole.sem("c_" + n) for n in names}
    with ExitStack() as st:
        c = Core(nc, st)
        qpack = c.sb("c_qpack", [PACK_ROWS, RING, HEADS_PER_GROUP, SEQ], BF16)
        kpack = c.sb("c_kpack", [PACK_ROWS, RING, HEADS_PER_GROUP, SEQ], BF16)
        probs = c.sb("c_probs", [P, 8, SEQ])
        v_cur = c.sb("c_v_cur", [P, QT, HEADS_PER_GROUP, 32])
        window = c.sb("c_window", [P, HEADS_PER_GROUP, 7 * P])
        tri = c.sb("c_tri", [P, P])
        identb = c.sb("c_identb", [P, P], BF16)
        junk = c.sb("c_junk", [P, 2, HALF], BF16)
        mx = c.sb("c_mx", [P, 32, 2])
        neg = c.sb("c_neg", [P, 32])
        negp = c.sb("c_negp", [P, 3, 32], BF16)
        neg_rows = c.sb("c_neg_rows", [96, P], BF16)
        pst = c.ps("c_pst", [P, 2, SEQ])
        pmax = c.ps("c_pmax", [P, 2, HALF])
        po = c.ps("c_po", [P, SEQ])
        block = st.enter_context(nc.Block())

        LOADS = 9 + 9 + 3
        LEAD = 28

        def load_group(q, g, ring):
            for z, pack in enumerate((qpack, kpack)):
                for i in range(3):
                    for j in range(3):
                        src = parts_scr[z, (i, j)[z]].rearrange("b (g h d) t -> (b g) d h t", g=HEAD_GROUPS, d=HEAD_DIM)
                        r0 = HEAD_DIM * (3 * i + j)
                        src = src[bass.ds(g, 1)].rearrange("o d h t -> (o d) h t")
                        dst = pack[r0:r0 + HEAD_DIM, bass.ds(ring, 1)].rearrange("d o h t -> d (o h) t")
                        q.dma_start(dst, src).then_inc(s["pack_loaded"], 16)
            for i in range(3):
                r0 = PAIR_ROWS + BIAS_R * i
                src = bias_scr[i][bass.ds(g, 1)].rearrange("o h r k -> r (o h) k")
                q.dma_start(kpack[r0:r0 + BIAS_R, bass.ds(ring, 1)].rearrange("r o h k -> r (o h) k"),
                            src).then_inc(s["pack_loaded"], 16)
            q.wait_ge(s["pack_loaded"], (g + 1) * (16 * LOADS))
            q.sem_inc(s["sp_begun"], 1)

        @block.sync
        def _(sp):
            sp.sem_inc(s["m_stored"], 16)
            sp.dma_start(tri[:, :], d["tri_qk"]).then_inc(s["gtri_loaded"], 16)
            sp.dma_start(identb[:, :], d["ident_bf16"]).then_inc(s["gtri_loaded"], 16)
            for r in range(RING):
                sp.dma_start(qpack[PAIR_ROWS:MAX_ROW, r], d["bias_queries"]).then_inc(s["ones_loaded"], 16)
                sp.dma_start(kpack[MAX_ROW:PACK_ROWS, r], d["ones_rows"]).then_inc(s["ones_loaded"], 16)
            for g in range(RING):
                load_group(sp, g, g)

            def store_max(g):
                sp.wait_ge(s["m_copied"], g + 1)
                sp.sem_inc(s["sp_begun"], 1)
                for i in range(3):
                    dst = qpack[MAX_ROW + i:MAX_ROW + i + 1, bass.ds(g % RING, 1)].rearrange("r o h (t q) -> r (o h t) q", q=P)
                    sp.dma_start(dst, neg_rows[32 * i:32 * i + 32, :]).then_inc(s["m_stored"], 16)

            store_max(0)
            with sp.Fori(0, GROUPS - RING) as g:
                store_max(g + 1)
                sp.wait_ge(s["pv_done"], (g + 1) * QT + 1)
                sp.sem_inc(s["sp_begun"], 1)
                load_group(sp, g + RING, g)
            with sp.Fori(GROUPS - RING, GROUPS - 1) as g:
                store_max(g + 1)
            sp.wait_ge(s["m_stored"], 48 * GROUPS + 16)

        @block.gpsimd
        def _(pool):
            pool.memset(window[:, :, :], 0.0).then_inc(s["w_zero"], 1)
            pool.memset(v_cur[:, :, :, :], 0.0).then_inc(s["v_fixed"], 1)
            pool.wait_ge(s["v_fixed"], 1)
            pool.memset(v_cur[:, :, :, HEAD_DIM:HEAD_DIM + 1], 1.0).then_inc(s["v_fixed"], 1)
            pool.wait_ge(s["v_fixed"], 2)
            with pool.Fori(0, GROUPS) as g:
                pool.wait_ge(s["pv_done"], g * QT + 1)
                pool.tensor_copy(v_cur[:, :, :, 0:HEAD_DIM],
                                 v_all[:, bass.ds(g, 1)].rearrange("p o k (h x) -> p (o k) h x", x=HEAD_DIM)).then_inc(s["v_ready"], 1)

        def max_tiles(pe, g, n0, n1, first):
            for n in range(n0, n1):
                h, qt, half = n // 16, n // 2 % 8, n % 2
                if not (first and n < 2):
                    pe.wait_ge(s["maxs_free"], g * 65 + max(n - 1, 0))
                ring = g % RING
                q = qpack[0:MAX_ROW, bass.ds(ring, 1), h, qt * P:(qt + 1) * P].rearrange("r o q -> r (o q)")
                k = kpack[0:MAX_ROW, bass.ds(ring, 1), h, half * HALF:(half + 1) * HALF].rearrange("r o k -> r (o k)")
                pe.matmul(pmax[:, n % 2, :], q, k, start=True, stop=True).then_inc(s["maxs_ready"], 1)

        def turn_max(pe, g):
            pe.wait_ge(s["mp2"], g + 1)
            pe.transpose(pmax[0:96, 0, 0:P // 2].bitcast(BF16), negp[:, :, :].rearrange("p i x -> p (i x)"),
                         identb[:, :]).then_inc(s["m_turned"], 1)

        def second_pass(pe, g, with_next):
            ring = g % RING
            pe.wait_ge(s["m_stored"], (g + 1) * 48 + 16)
            if with_next:
                pe.wait_ge(s["pack_loaded"], (g + 2) * (16 * LOADS))
            for j in range(32):
                kt, h = j // 4, j % 4
                pe.wait_ge(s["exp_done"], g * 32 + (j + 1))
                k = kpack[:, bass.ds(ring, 1), h, kt * P:(kt + 1) * P].rearrange("r o k -> r (o k)")
                n0, n1 = (64 * j // LEAD, 64 * (j + 1) // LEAD) if with_next and j < LEAD else (0, 0)
                for half in range(2):
                    q = qpack[:, bass.ds(ring, 1), h, half * HALF:(half + 1) * HALF].rearrange("r o q -> r (o q)")
                    diag = kt // 4 == half
                    mm = pe.matmul(pst[:, j % 2, half * HALF:(half + 1) * HALF], k, q, start=True, stop=True,
                                   skip_group_check=diag)
                    if diag:
                        t = tri_all[:, bass.ds((g % HEAD_GROUPS) * HEADS_PER_GROUP + h, 1), :].rearrange("p o q -> p (o q)")
                        mm = pe.matmul(pst[:, j % 2, kt * P:(kt + 1) * P], ident[:, :], t, start=False, stop=True,
                                       skip_group_check=True)
                    if half == 0:
                        max_tiles(pe, g + 1, n0, min(n0 + 1, n1), False)
                mm.then_inc(s["scores_ready"], 1)
                max_tiles(pe, g + 1, n0 + 1, n1, False)
                if j >= 5 and (j - 5) % 4 == 0:
                    weigh(pe, g, (j - 5) // 4)
                if with_next and j == 31:
                    turn_max(pe, g + 1)
            weigh(pe, g, 7)

        def weigh(pe, g, kt):
            pe.wait_ge(s["exp_done"], g * 32 + (4 * kt + 6))
            if kt == 0:
                pe.wait_ge(s["v_ready"], g + 1)
                pe.wait_ge(s["o_copied"], g + 1)
            for half in range(2):
                for h in range(HEADS_PER_GROUP):
                    mm = pe.matmul(po[32 * h:32 * h + 32, half * HALF:(half + 1) * HALF], v_cur[:, kt, h, :],
                                   probs[:, 4 * (kt % 2) + h, half * HALF:(half + 1) * HALF],
                                   start=(kt == 0), stop=(kt == QT - 1))
            mm.then_inc(s["pv_done"], 1)

        @block.tensor
        def _(pe):
            pe.sem_inc(s["pv_done"], 1)
            pe.wait_ge(s["gtri_loaded"], 32)
            pe.wait_ge(s["ones_loaded"], 16 * 2 * RING)
            pe.wait_ge(s["pack_loaded"], 16 * LOADS)
            max_tiles(pe, 0, 0, 64, True)
            turn_max(pe, 0)
            with pe.Fori(0, GROUPS - 1) as g:
                second_pass(pe, g, True)
            second_pass(pe, GROUPS - 1, False)

        @block.scalar
        def _(act):
            act.sem_inc(s["o_copied"], 1)
            act.sem_inc(s["exp_done"], 2)
            with act.Fori(0, GROUPS) as g:
                for j in range(32):
                    kt = j // 4
                    act.wait_ge(s["scores_ready"], g * 32 + (j + 1))
                    if j % 4 == 0:
                        if kt >= 2:
                            act.wait_ge(s["pv_done"], g * QT + kt)
                    act.activation(probs[:, j % 8, :], pst[:, j % 2, :], ACT.Exp).then_inc(s["exp_done"], 1)
                act.wait_ge(s["pv_done"], (g + 1) * QT + 1)
                act.activation(o_all[:, bass.ds(g, 1), :].rearrange("p o q -> p (o q)"), po[:, :], ACT.Copy).then_inc(s["o_copied"], 1)

        def maxima(dve, g):
            for h in range(HEADS_PER_GROUP):
                dve.tensor_scalar(window[:, h, 3 * P:4 * P], tri[:, :],
                                  s8[:, bass.ds((g % HEAD_GROUPS) * HEADS_PER_GROUP + h, 1)], None, ALU.mult).then_inc(s["center_done"], 1)
            dve.wait_ge(s["center_done"], (g + 1) * 4)
            for n in range(64):
                h, qt, half = n // 16, n // 2 % 8, n % 2
                dve.wait_ge(s["maxs_ready"], g * 64 + (n + 1))
                if qt // 4 == half:
                    if n >= 2:
                        dve.wait_ge(s["maxs_free"], g * 65 + (n - 1))
                    dve.sem_inc(s["begun"], 1)
                    o = 3 * P - P * (qt % 4)
                    dve.tensor_tensor_reduce(junk[:, half, :], pmax[:, n % 2, :], window[:, h, o:o + HALF], 1.0, -3e38,
                                             ALU.add, ALU.max, mx[:, n // 2, half:half + 1]).then_inc(s["maxs_free"], 1)
                else:
                    dve.tensor_reduce(mx[:, n // 2, half:half + 1], pmax[:, n % 2, :], AX.X, ALU.max).then_inc(s["maxs_free"], 1)
            dve.wait_ge(s["maxs_free"], g * 65 + 64)
            dve.tensor_reduce(neg[:, :], mx[:, :, :], AX.X, ALU.max, negate=True).then_inc(s["neg_done"], 1)
            dve.wait_ge(s["neg_done"], g + 1)
            dve.tensor_copy(negp[:, 0, :], neg[:, :]).then_inc(s["mp0"], 1)
            dve.wait_ge(s["mp0"], g + 1)
            dve.tensor_tensor(neg[:, :], neg[:, :], negp[:, 0, :], ALU.subtract).then_inc(s["mr0"], 1)
            dve.wait_ge(s["mr0"], g + 1)
            dve.tensor_copy(negp[:, 1, :], neg[:, :]).then_inc(s["mp1"], 1)
            dve.wait_ge(s["mp1"], g + 1)
            dve.tensor_tensor(negp[:, 2, :], neg[:, :], negp[:, 1, :], ALU.subtract).then_inc(s["mp2"], 1)
            dve.wait_ge(s["m_turned"], g + 1)
            dve.wait_ge(s["m_stored"], g * 48 + 16)
            dve.tensor_copy(neg_rows[:, :], pmax[0:96, 0, 0:P // 2].bitcast(BF16)).then_inc(s["m_copied"], 1)
            dve.wait_ge(s["m_copied"], g + 1)
            dve.sem_inc(s["maxs_free"], 1)

        @block.vector
        def _(dve):
            dve.wait_ge(s["w_zero"], 1)
            dve.wait_ge(s["gtri_loaded"], 32)
            with dve.Fori(0, GROUPS) as g:
                maxima(dve, g)


def ffn_and_mix(nc, whole, d, ident, o_all, x, xnT):
    names = ("loaded", "wg_cast", "w_scaled", "gu_ready", "silu_done", "gu_read", "turned", "recip", "o_read", "o_turned", "oT_copied",
             "row_ready", "proj_read", "gate_done", "mul_done", "x_done")
    s = {n: whole.sem("d_" + n) for n in names}
    KH = HIDDEN // P
    N = TOK // HALF
    with ExitStack() as st:
        c = Core(nc, st)
        w_int = c.sb("d_w_int", [P, 3, HIDDEN], I32)
        w = c.sb("d_w", [P, 3, HIDDEN])
        w_proj = c.sb("d_w_proj", [P, DIM])
        bias = c.sb("d_bias", [P, DIM])
        act_gate = c.sb("d_act_gate", [P, 2, HALF])
        hT = c.sb("d_hT", [P, KH, TOK])
        recip = c.sb("d_recip", [P, TILES, HEADS])
        o_tok = c.sb("d_o_tok", [P, TILES, DIM])
        oT = c.sb("d_oT", [P, TOK])
        mix = c.sb("d_mix", [P, TILES, DIM])
        gate = c.sb("d_gate", [P, TILES, DIM])
        pgu = c.ps("d_pgu", [P, 2, 2, HALF])
        pturn = c.ps("d_pturn", [P, 2, HALF])
        prow = c.ps("d_prow", [P, 2, HALF])
        block = st.enter_context(nc.Block())

        @block.sync
        def _(sp):
            sp.dma_start(w_int[:, :, :], d["w_ffn"]).then_inc(s["loaded"], 16)
            sp.dma_start(w_proj[:, :], d["w_proj"]).then_inc(s["loaded"], 16)
            sp.dma_start(bias[:, :], d["proj_b"].partition_broadcast(P)).then_inc(s["loaded"], 16)

        @block.gpsimd
        def _(pool):
            pool.wait_ge(s["loaded"], 48)
            pool.tensor_copy(w[:, :, :], w_int[:, :, :]).then_inc(s["wg_cast"], 1)
            pool.wait_ge(s["wg_cast"], 1)
            pool.tensor_scalar(w[:, :, :], w[:, :, :], QSCALE, None, ALU.mult).then_inc(s["w_scaled"], 1)

        @block.tensor
        def _(pe):
            for t in range(TILES):
                b, qt = t // QT, t % QT
                if t >= 2:
                    pe.wait_ge(s["o_read"], t - 1)
                for hg in range(HEAD_GROUPS):
                    mm = pe.transpose(pturn[:, t % 2, hg * P:(hg + 1) * P],
                                      o_all[:, b * HEAD_GROUPS + hg, qt * P:(qt + 1) * P], ident[:, :])
                mm.then_inc(s["turned"], 1)
            pe.wait_ge(s["w_scaled"], 1)
            for r in range(KH * N):
                m, n = r // N, r % N
                if r >= 2:
                    pe.wait_ge(s["gu_read"], r - 1)
                for j in range(2):
                    mm = pe.matmul(pgu[:, r % 2, j, :], w[:, j, m * P:(m + 1) * P], xnT[:, n * HALF:(n + 1) * HALF],
                                   start=True, stop=True)
                mm.then_inc(s["gu_ready"], 1)
            for t in range(TILES):
                n = t // 4
                if t % 4 == 0:
                    pe.wait_ge(s["o_read"], TILES)
                    if n >= 2:
                        pe.wait_ge(s["oT_copied"], n - 1)
                mm = pe.transpose(pturn[:, n % 2, t % 4 * P:(t % 4 + 1) * P], o_tok[:, t, :], ident[:, :])
                if t % 4 == 3:
                    mm.then_inc(s["o_turned"], 1)
            pe.wait_ge(s["gu_read"], KH * N)
            for r in range(2 * N):
                if r >= 2:
                    pe.wait_ge(s[("proj_read", "gate_done")[r % 2]], r // 2)
                if r % 2 == 0:
                    pe.wait_ge(s["oT_copied"], r // 2 + 1)
                for t in range(4 * (r // 2), 4 * (r // 2) + 4):
                    dst = prow[:, r % 2, t % 4 * P:(t % 4 + 1) * P]
                    if r % 2 == 0:
                        mm = pe.matmul(dst, oT[:, t * P:(t + 1) * P], w_proj[:, :], start=True, stop=True)
                    else:
                        for k in range(KH):
                            mm = pe.matmul(dst, hT[:, k, t * P:(t + 1) * P], w[:, 2, k * P:(k + 1) * P],
                                           start=(k == 0), stop=(k == KH - 1))
                mm.then_inc(s["row_ready"], 1)

        @block.scalar
        def _(act):
            for r in range(KH * N):
                act.wait_ge(s["gu_ready"], r + 1)
                if r >= 2:
                    act.wait_ge(s["gu_read"], r - 1)
                act.activation(act_gate[:, r % 2, :], pgu[:, r % 2, 0, :], ACT.Silu).then_inc(s["silu_done"], 1)
            for n in range(N):
                act.wait_ge(s["o_turned"], n + 1)
                act.activation(oT[:, n * HALF:(n + 1) * HALF], pturn[:, n % 2, :], ACT.Copy).then_inc(s["oT_copied"], 1)
            for n in range(N):
                act.wait_ge(s["row_ready"], 2 * n + 2)
                act.activation(gate[:, 4 * n:4 * n + 4, :], prow[:, 1, :].rearrange("p (t c) -> p t c", t=4),
                               ACT.Silu).then_inc(s["gate_done"], 1)

        @block.vector
        def _(dve):
            for t in range(TILES):
                v = pturn[:, t % 2, :].rearrange("p (h x) -> p h x", h=HEADS)
                dve.wait_ge(s["turned"], t + 1)
                dve.reciprocal(recip[:, t, :], v[:, :, HEAD_DIM]).then_inc(s["recip"], 1)
                dve.wait_ge(s["recip"], t + 1)
                dve.tensor_tensor(o_tok[:, t, :].rearrange("p (h x) -> p h x", h=HEADS), v[:, :, 0:HEAD_DIM],
                                  recip[:, t, :].unsqueeze(2).to_broadcast([P, HEADS, HEAD_DIM]), ALU.mult).then_inc(s["o_read"], 1)
            for r in range(KH * N):
                m, n = r // N, r % N
                dve.wait_ge(s["silu_done"], r + 1)
                dve.tensor_tensor(hT[:, m, n * HALF:(n + 1) * HALF], act_gate[:, r % 2, :], pgu[:, r % 2, 1, :],
                                  ALU.mult).then_inc(s["gu_read"], 1)
            for n in range(N):
                tt = slice(4 * n, 4 * n + 4)
                dve.wait_ge(s["row_ready"], 2 * n + 1)
                dve.wait_ge(s["loaded"], 48)
                dve.tensor_tensor(mix[:, tt, :], prow[:, 0, :].rearrange("p (t c) -> p t c", t=4),
                                  bias[:, :].unsqueeze(1).to_broadcast([P, 4, DIM]), ALU.add).then_inc(s["proj_read"], 1)
                dve.wait_ge(s["gate_done"], n + 1)
                dve.wait_ge(s["proj_read"], n + 1)
                dve.tensor_tensor(mix[:, tt, :], mix[:, tt, :], gate[:, tt, :], ALU.mult).then_inc(s["mul_done"], 1)
                dve.wait_ge(s["mul_done"], n + 1)
                dve.tensor_tensor(x[:, tt, :], x[:, tt, :], mix[:, tt, :], ALU.add).then_inc(s["x_done"], 1)


ALL_EXPERTS = EXPERTS + 2
EXP_HID = 256


def experts(nc, whole, d, ident, xn, xnT, gate_out):
    names = ("gate_loaded", "b_loaded", "logit_ready", "logit", "top", "shift", "expo", "total", "inv", "weight", "best", "gt", "eq", "ngt", "room",
             "cum", "allow", "both", "pick", "ones", "gated", "g_turned", "g_copied", "b2_ready", "acc_ready", "h_ready", "h_done",
             "y_ready", "y_read", "silu_done", "begun")
    s = {n: whole.sem("e_" + n) for n in names}
    w1_loaded = [whole.sem(f"e_w1_loaded{i}") for i in range(2)]
    w2_loaded = [whole.sem(f"e_w2_loaded{i}") for i in range(2)]
    E, A = EXPERTS, ALL_EXPERTS
    with ExitStack() as st:
        c = Core(nc, st)
        w_gate = c.sb("e_w_gate", [P, E])
        b_gate = c.sb("e_b_gate", [P, E])
        restart = c.sb("e_restart", [P, TILES, E])
        b1 = c.sb("e_b1", [P, A, 2])
        b2 = c.sb("e_b2", [A, DIM])
        w1 = c.sb("e_w1", [P, 2, EXP_HID])
        w2 = c.sb("e_w2", [P, 2, 2, DIM])
        hT = c.sb("e_hT", [P, 2, 2, TOK])
        wt = c.sb("e_wt", [P, TILES, E])
        small = c.sb("e_small", [P, 5, TILES])
        best = c.sb("e_best", [P, TILES, 8])
        gt = c.sb("e_gt", [P, TILES, E])
        eq = c.sb("e_eq", [P, TILES, E])
        cum = c.sb("e_cum", [P, TILES, E])
        gates = c.sb("e_gates", [P, A, TILES])
        gates_tok = c.sb("e_gates_tok", [P, TILES, A])
        gT = c.sb("e_gT", [A, TOK])
        ph = c.ps("e_ph", [P, 2, SEQ])
        py = c.ps("e_py", [P, 2, HALF])
        pg = c.ps("e_pg", [P, 2, HALF])
        block = st.enter_context(nc.Block())
        wide = lambda v: v.unsqueeze(2).to_broadcast([P, TILES, E])

        def load_w1(sp, e, par):
            sp.dma_start(w1[:, par, :], d["experts_w1"][bass.ds(e, 1)].rearrange("o c f -> (o c) f")).then_inc(w1_loaded[par], 16)

        def load_w2(sp, e, par):
            sp.dma_start(w2[:, par, :, :], d["experts_w2"][bass.ds(e, 1)].rearrange("o f k c -> (o f) k c")).then_inc(w2_loaded[par], 16)

        @block.sync
        def _(sp):
            sp.dma_start(w_gate[:, :], d["gate_w"]).then_inc(s["gate_loaded"], 16)
            sp.dma_start(b_gate[:, :], d["gate_b"].partition_broadcast(P)).then_inc(s["gate_loaded"], 16)
            sp.dma_start(restart[:, :, :], d["restart"]).then_inc(s["gate_loaded"], 16)
            for par in range(2):
                load_w1(sp, par, par)
                load_w2(sp, par, par)
            sp.dma_start(b1[:, :, :], d["experts_b1"]).then_inc(s["b_loaded"], 16)
            sp.dma_start(b2[:, :], d["experts_b2"]).then_inc(s["b_loaded"], 16)
            with sp.Fori(0, (A - 3) // 2) as i:
                for par in range(2):
                    sp.wait_ge(s["h_ready"], i * 8 + 4 * (par + 1))
                    load_w1(sp, i * 2 + (par + 2), par)
                    sp.wait_ge(s["y_ready"], i * 8 + 4 * (par + 1))
                    load_w2(sp, i * 2 + (par + 2), par)
            sp.wait_ge(s["h_ready"], 4 * (A - 2))
            load_w1(sp, A - 1, 0)
            sp.wait_ge(s["y_ready"], 4 * (A - 2))
            load_w2(sp, A - 1, 0)

        def hidden(pe, e, par, uses):
            pe.wait_ge(w1_loaded[par], uses * 16)
            for u in range(4):
                m, half = u // 2, u % 2
                pe.wait_ge(s["h_done"], e * 4 + (u + 1))
                for j in range(2):
                    at = half * SEQ + j * HALF
                    mm = pe.matmul(ph[:, u % 2, j * HALF:(j + 1) * HALF], w1[:, par, m * P:(m + 1) * P], xnT[:, at:at + HALF],
                                   start=True, stop=True)
                mm.then_inc(s["h_ready"], 1)

        def output(pe, e, par, uses):
            pe.wait_ge(w2_loaded[par], uses * 16)
            pe.wait_ge(s["h_done"], e * 4 + 6)
            for r in range(4):
                pe.wait_ge(s["y_read"], e * 16 + (4 * r + 12))
                for t in range(4 * r, 4 * r + 4):
                    for k in range(2):
                        mm = pe.matmul(py[:, r % 2, t % 4 * P:(t % 4 + 1) * P], hT[:, par, k, t * P:(t + 1) * P],
                                       w2[:, par, k, :], start=(k == 0), stop=(k == 1))
                mm.then_inc(s["y_ready"], 1)

        @block.tensor
        def _(pe):
            pe.wait_ge(s["gate_loaded"], 48)
            for t in range(TILES):
                mm = pe.matmul(pg[:, 0, t * 16:t * 16 + E], xnT[:, t * P:(t + 1) * P], w_gate[:, :], start=True, stop=True)
            mm.then_inc(s["logit_ready"], 1)
            hidden(pe, 0, 0, 1)
            pe.wait_ge(s["gated"], 1)
            for n in range(TILES // 4):
                if n >= 1:
                    pe.wait_ge(s["g_copied"], n)
                for t in range(4 * n, 4 * n + 4):
                    mm = pe.transpose(pg[0:A, 1, t % 4 * P:(t % 4 + 1) * P], gates_tok[:, t, :], ident[:, :])
                mm.then_inc(s["g_turned"], 1)
            pe.wait_ge(s["g_copied"], TILES // 4)
            pe.wait_ge(s["b_loaded"], 32)
            for n in range(TILES // 4):
                if n >= 1:
                    pe.wait_ge(s["acc_ready"], n)
                for t in range(4 * n, 4 * n + 4):
                    mm = pe.matmul(pg[:, 0, t % 4 * P:(t % 4 + 1) * P], gT[:, t * P:(t + 1) * P], b2[:, :], start=True, stop=True)
                mm.then_inc(s["b2_ready"], 1)
            with pe.Fori(0, (A - 1) // 2) as i:
                hidden(pe, i * 2 + 1, 1, i + 1)
                output(pe, i * 2, 0, i + 1)
                hidden(pe, i * 2 + 2, 0, i + 2)
                output(pe, i * 2 + 1, 1, i + 1)
            output(pe, A - 1, 0, (A + 1) // 2)

        @block.scalar
        def _(act):
            act.sem_inc(s["h_done"], 2)
            act.wait_ge(s["shift"], 1)
            act.activation(wt[:, :, :], wt[:, :, :], ACT.Exp).then_inc(s["expo"], 1)
            act.wait_ge(s["b_loaded"], 32)

            def transposed():
                for n in range(TILES // 4):
                    act.wait_ge(s["g_turned"], n + 1)
                    act.activation(gT[:, n * HALF:(n + 1) * HALF], pg[0:A, 1, :], ACT.Copy).then_inc(s["g_copied"], 1)

            def first(e, par):
                for u in range(4):
                    m, half = u // 2, u % 2
                    act.wait_ge(s["h_ready"], e * 4 + u + 1)
                    act.activation(hT[:, par, m, half * SEQ:(half + 1) * SEQ], ph[:, u % 2, :], ACT.Gelu,
                                   bias=b1[:, e, m:m + 1]).then_inc(s["h_done"], 1)

            first(0, 0)
            transposed()
            first(1, 1)
            with act.Fori(1, (A - 1) // 2) as i:
                for par in range(2):
                    for u in range(4):
                        m, half = u // 2, u % 2
                        if u == 0:
                            act.wait_ge(s["y_ready"], i * 8 + 4 * (par - 1))
                        act.wait_ge(s["h_ready"], i * 8 + (4 * par + u + 1))
                        act.sem_inc(s["begun"], 1)
                        bias = b1[:, bass.ds(i * 2 + par, 1), m:m + 1].rearrange("p o m -> p (o m)")
                        act.activation(hT[:, par, m, half * SEQ:(half + 1) * SEQ], ph[:, u % 2, :], ACT.Gelu,
                                       bias=bias).then_inc(s["h_done"], 1)
            act.wait_ge(s["y_ready"], 4 * (A - 2))
            first(A - 1, 0)
            for n in range(4):
                act.wait_ge(s["y_read"], TILES * A + 4 * n + 4)
                act.activation(gate_out[:, 4 * n:4 * n + 4, :], gate_out[:, 4 * n:4 * n + 4, :], ACT.Silu).then_inc(s["silu_done"], 1)

        @block.vector
        def _(dve):
            inc = lambda ins, name: (ins.then_inc(s[name], 1), dve.wait_ge(s[name], 1))
            dve.wait_ge(s["gate_loaded"], 48)
            dve.wait_ge(s["logit_ready"], 1)
            mx, total, inv, ngt, room = (small[:, n, :] for n in range(5))
            inc(dve.tensor_tensor(wt[:, :, :], pg[:, 0, 0:16 * TILES].rearrange("p (t e) -> p t e", e=16)[:, :, 0:E],
                                  b_gate[:, :].unsqueeze(1).to_broadcast([P, TILES, E]), ALU.add), "logit")
            inc(dve.tensor_reduce(mx, wt[:, :, :], AX.X, ALU.max), "top")
            dve.tensor_tensor(wt[:, :, :], wt[:, :, :], wide(mx), ALU.subtract).then_inc(s["shift"], 1)
            dve.wait_ge(s["expo"], 1)
            inc(dve.tensor_reduce(total, wt[:, :, :], AX.X, ALU.add), "total")
            inc(dve.reciprocal(inv, total), "inv")
            inc(dve.tensor_tensor(wt[:, :, :], wt[:, :, :], wide(inv), ALU.mult), "weight")
            for t in range(TILES):
                dve.max(best[:, t, :], wt[:, t, :]).then_inc(s["best"], 1)
            dve.wait_ge(s["best"], TILES)
            third = wide(best[:, :, TOP_K - 1])
            inc(dve.tensor_tensor(gt[:, :, :], wt[:, :, :], third, ALU.is_gt), "gt")
            inc(dve.tensor_tensor(eq[:, :, :], wt[:, :, :], third, ALU.is_equal), "eq")
            inc(dve.tensor_reduce(ngt, gt[:, :, :], AX.X, ALU.add), "ngt")
            inc(dve.tensor_scalar(room, ngt, -1.0, float(TOP_K), ALU.mult, ALU.add), "room")
            inc(dve.tensor_tensor_scan(cum[:, :, :].rearrange("p t e -> p (t e)"), restart[:, :, :].rearrange("p t e -> p (t e)"),
                                       eq[:, :, :].rearrange("p t e -> p (t e)"), 0.0, ALU.mult, ALU.add), "cum")
            inc(dve.tensor_tensor(cum[:, :, :], cum[:, :, :], wide(room), ALU.is_le), "allow")
            inc(dve.tensor_tensor(eq[:, :, :], eq[:, :, :], cum[:, :, :], ALU.mult), "both")
            inc(dve.tensor_tensor(gt[:, :, :], gt[:, :, :], eq[:, :, :], ALU.add), "pick")
            dve.memset(gates_tok[:, :, E:A], 1.0).then_inc(s["ones"], 1)
            dve.memset(gates[:, E:A, :], 1.0).then_inc(s["ones"], 1)
            dve.tensor_tensor(gates[:, 0:E, :].rearrange("p e t -> p t e"), wt[:, :, :], gt[:, :, :], ALU.mult).then_inc(s["ones"], 1)
            dve.wait_ge(s["ones"], 3)
            dve.tensor_tensor(gates_tok[:, :, 0:E], wt[:, :, :], gt[:, :, :], ALU.mult).then_inc(s["gated"], 1)
            for n in range(TILES // 4):
                dve.wait_ge(s["b2_ready"], n + 1)
                dve.tensor_tensor(gate_out[:, 4 * n:4 * n + 4, :], pg[:, 0, :].rearrange("p (t c) -> p t c", t=4),
                                  xn[:, 4 * n:4 * n + 4, :], ALU.add).then_inc(s["acc_ready"], 1)
            dve.wait_ge(s["acc_ready"], TILES // 4)
            dve.sem_inc(s["y_read"], TILES)

            with dve.Fori(0, A) as e:
                for t in range(TILES):
                    if t % 4 == 0:
                        dve.wait_ge(s["y_ready"], e * 4 + (t // 4 + 1))
                        dve.wait_ge(s["y_read"], e * 16 + (t + 4))
                    dve.scalar_tensor_tensor(out=gate_out[:, t, :], in0=py[:, t // 4 % 2, t % 4 * P:(t % 4 + 1) * P],
                                             scalar=gates[:, bass.ds(e, 1), t:t + 1].rearrange("p o t -> p (o t)"),
                                             in1=gate_out[:, t, :], op0=ALU.mult, op1=ALU.add).then_inc(s["y_read"], 1)


LAYERS, INNER, STATE, RANK, TAPS = 4, 256, 16, 8, 4
NH = INNER // P
COLS = TAPS + 1 + 1 + STATE + 1
X_ROWS = 3 * 2 * STATE + RANK


def mamba(nc, whole, d, ident, u, decay):
    names = ("w_loaded", "wo_loaded", "sel_loaded", "pad_zero", "xz_ready", "xz_read", "tap0", "taps", "xc_done", "xp_ready", "bc0", "dt_copied",
             "bc_rest", "bc1", "bc_ready", "dl_ready", "dl_abs", "dl_relu", "dl_exp", "dl_ln", "delta", "du_done", "a_exp", "a_neg",
             "diag", "b_ready", "b_copied", "c_ready", "exp_done", "drive_done", "scan_done", "prod_done", "y_done",
             "yg_done", "out_ready", "u_done", "pre_done", "begun", "act_begun")
    s = {n: whole.sem("m_" + n) for n in names}
    with ExitStack() as st:
        c = Core(nc, st)
        sel = c.sb("m_sel", [6 * STATE, 2 * STATE, P], BF16)
        w = c.sb("m_w", [P, 2 * INNER + NH * X_ROWS + NH * COLS])
        w_in = w[:, 0:2 * INNER]
        w_x = w[:, 2 * INNER:2 * INNER + NH * X_ROWS].rearrange("p (k r) -> p k r", k=NH)
        cols = w[:, 2 * INNER + NH * X_ROWS:].rearrange("p (k r) -> p k r", k=NH)
        w_dt = c.sb("m_w_dt", [X_ROWS, INNER])
        w_out = c.sb("m_w_out", [P, NH, DIM])
        pad = c.sb("m_pad", [P, NH, BATCH, TAPS - 1 + SEQ])
        zs = c.sb("m_zs", [P, NH, TOK])
        cv = c.sb("m_cv", [P, NH, TOK])
        xc = c.sb("m_xc", [P, NH, TOK])
        delta = c.sb("m_delta", [P, NH, TOK])
        du = c.sb("m_du", [P, NH, TOK])
        bcp = c.sb("m_bcp", [6 * STATE, TOK], BF16)
        bcq = c.sb("m_bcq", [6 * STATE, TOK], BF16)
        bcr = c.sb("m_bcr", [6 * STATE, TOK])
        dts = c.sb("m_dts", [X_ROWS, TOK])
        neg_a = c.sb("m_neg_a", [P, NH, STATE])
        diag = c.sb("m_diag", [P, NH, P])
        b_sb = c.sb("m_b_sb", [P, 4, SEQ])
        drive = c.sb("m_drive", [P, 2, SEQ])
        state = c.sb("m_state", [P, 2, SEQ])
        prod = c.sb("m_prod", [P, 2, SEQ])
        pa = c.ps("m_pa", [P, 4, HALF])
        pb = c.ps("m_pb", [P, 4, HALF])
        block = st.enter_context(nc.Block())
        N = TOK // HALF
        pb_wide = pb[:, :, :].rearrange("p n c -> p (n c)")
        pa_wide = pa[:, :, :].rearrange("p n c -> p (n c)")
        p_b, p_c = pb_wide[:, 0:SEQ], pb_wide[:, SEQ:2 * SEQ]
        PER_LAYER = BATCH * STATE

        @block.sync
        def _(sp):
            sp.dma_start(sel[:, :, :], d["select"]).then_inc(s["sel_loaded"], 16)
            with sp.Fori(0, LAYERS) as l:
                sp.wait_ge(s["pre_done"], l + 1)
                sp.dma_start(w[:, :], d["mamba_w"][bass.ds(l, 1)].rearrange("o p f -> (o p) f")).then_inc(s["w_loaded"], 16)
                sp.dma_start(w_dt[X_ROWS - RANK:X_ROWS, :], d["mamba_w_dt"][bass.ds(l, 1)].rearrange("o r f -> (o r) f")).then_inc(s["w_loaded"], 16)
                sp.wait_ge(s["u_done"], l * BATCH + 1)
                sp.dma_start(w_out[:, :, :], d["mamba_w_out"][bass.ds(l, 1)].rearrange("o p k f -> (o p) k f")).then_inc(s["wo_loaded"], 16)

        @block.tensor
        def _(pe):
            def b_rows(S, si, b):
                pe.wait_ge(s["b_copied"], S + 1)
                row(si, b, p_b).then_inc(s["b_ready"], 1)

            def c_rows(S, si, b):
                pe.wait_ge(s["prod_done"], S * 2 + 2)
                row(si + STATE, b, p_c).then_inc(s["c_ready"], 1)

            def row(j, b, dst):
                pick = sel[:, bass.ds(j, 1), :].rearrange("r o p -> r (o p)")
                for n in range(2):
                    mm = pe.matmul(dst[:, n * HALF:(n + 1) * HALF], pick, bcp[:, b * SEQ + n * HALF:b * SEQ + (n + 1) * HALF],
                                   start=True, stop=True)
                return mm

            def add_y(U, h):
                pe.wait_ge(s["prod_done"], U + 3)
                for n in range(2):
                    mm = pe.matmul(pa[:, 2 * h + n, :], ident[:, :], prod[:, h, n * HALF:(n + 1) * HALF],
                                   start=False, stop=True, skip_group_check=True)
                mm.then_inc(s["y_done"], 1)

            pe.sem_inc(s["y_done"], 2)
            pe.wait_ge(s["sel_loaded"], 16)
            with pe.Fori(0, LAYERS) as l:
                pe.wait_ge(s["w_loaded"], l * 32 + 32)
                pe.wait_ge(s["u_done"], l * BATCH + 1)
                for r in range(4 * N):
                    m, n = r // N, r % N
                    if r >= 4:
                        pe.wait_ge(s["xz_read"], l * 16 + (r - 3))
                    pe.matmul(pa[:, r % 4, :], w_in[:, m * P:(m + 1) * P], u[:, n * HALF:(n + 1) * HALF],
                              start=True, stop=True).then_inc(s["xz_ready"], 1)
                for k in range(NH):
                    pe.wait_ge(s["xc_done"], l * NH + (k + 1))
                    for n in range(N):
                        mm = pe.matmul(pb[0:X_ROWS, n, :], w_x[:, k, :], xc[:, k, n * HALF:(n + 1) * HALF],
                                       start=(k == 0), stop=(k == NH - 1))
                mm.then_inc(s["xp_ready"], 1)
                pe.wait_ge(s["dt_copied"], l + 1)
                pe.wait_ge(s["xz_read"], l * 16 + 16)
                for h in range(NH):
                    if h == 1:
                        pe.wait_ge(s["bc0"], l + 1)
                        pe.wait_ge(s["bc_rest"], l + 1)
                    for n in range(N):
                        mm = pe.matmul((pa, pb)[h][:, n, :], w_dt[X_ROWS - RANK:X_ROWS, h * P:(h + 1) * P],
                                       dts[X_ROWS - RANK:X_ROWS, n * HALF:(n + 1) * HALF], start=True, stop=True)
                    mm.then_inc(s["dl_ready"], 1)
                pe.wait_ge(s["bc_ready"], l * 2 + 2)
                pe.wait_ge(s["dl_relu"], l * NH + NH)
                pe.wait_ge(s["dl_abs"], l * NH + NH)
                pe.wait_ge(s["diag"], l * NH + NH)
                for b in range(BATCH):
                    S0 = l * PER_LAYER + b * STATE
                    pe.wait_ge(s["u_done"], l * BATCH + (b + 1))
                    b_rows(S0, 0, b)
                    b_rows(S0 + 1, 1, b)
                    for h in range(NH):
                        for n in range(2):
                            mm = pe.matmul(pa[:, 2 * h + n, :], diag[:, h, :], xc[:, h, b * SEQ + n * HALF:b * SEQ + (n + 1) * HALF],
                                           start=True, stop=True, skip_group_check=True)
                    c_rows(S0, 0, b)
                    b_rows(S0 + 2, 2, b)
                    add_y(S0 * 2, 0)
                    with pe.Fori(1, STATE - 2) as si:
                        S = S0 + si
                        c_rows(S, si, b)
                        add_y(S * 2 - 1, 1)
                        b_rows(S + 2, si + 2, b)
                        add_y(S * 2, 0)
                    for si in (STATE - 2, STATE - 1):
                        S = S0 + si
                        c_rows(S, si, b)
                        add_y(S * 2 - 1, 1)
                        add_y(S * 2, 0)
                    add_y(S * 2 + 1, 1)
                    pe.wait_ge(s["yg_done"], l * BATCH + (b + 1))
                    pe.wait_ge(s["wo_loaded"], l * 16 + 16)
                    pe.wait_ge(s["b_copied"], S0 + (STATE + 1))
                    for n in range(2):
                        for k in range(NH):
                            mm = pe.matmul(p_b[:, n * HALF:(n + 1) * HALF], w_out[:, k, :],
                                           cv[:, k, b * SEQ + n * HALF:b * SEQ + (n + 1) * HALF], start=(k == 0), stop=(k == NH - 1))
                    mm.then_inc(s["out_ready"], 1)

        @block.scalar
        def _(act):
            act.sem_inc(s["exp_done"], 2)
            act.sem_inc(s["u_done"], 1)
            act.sem_inc(s["b_copied"], 1)
            with act.Fori(0, LAYERS) as l:
                act.wait_ge(s["pad_zero"], 1)
                act.wait_ge(s["w_loaded"], l * 32 + 32)
                for r in range(4 * N):
                    m, n = r // N, r % N
                    act.wait_ge(s["xz_ready"], l * 16 + (r + 1))
                    if m < NH:
                        b, at = n // 2, TAPS - 1 + n % 2 * HALF
                        act.activation(pad[:, m, b, at:at + HALF], pa[:, r % 4, :], ACT.Copy).then_inc(s["xz_read"], 1)
                        if n == N - 1:
                            act.wait_ge(s["xz_read"], l * 16 + 4 * (m + 1))
                            act.activation(cv[:, m, :].rearrange("p (b t) -> p b t", b=BATCH), pad[:, m, :, 0:SEQ], ACT.Identity,
                                           scale=cols[:, m, 0:1], bias=cols[:, m, TAPS:TAPS + 1]).then_inc(s["tap0"], 1)
                    else:
                        act.activation(zs[:, m - NH, n * HALF:(n + 1) * HALF], pa[:, r % 4, :], ACT.Silu).then_inc(s["xz_read"], 1)
                for h in range(NH):
                    act.wait_ge(s["taps"], l * 6 + 3 * (h + 1))
                    act.activation(xc[:, h, :], cv[:, h, :], ACT.Silu).then_inc(s["xc_done"], 1)
                act.wait_ge(s["xp_ready"], l + 1)
                act.activation(dts[X_ROWS - RANK:X_ROWS, :], pb_wide[X_ROWS - RANK:X_ROWS, :], ACT.Copy).then_inc(s["dt_copied"], 1)
                act.activation(bcp[:, :], pb_wide[0:6 * STATE, :], ACT.Copy).then_inc(s["bc0"], 1)
                act.wait_ge(s["bc_rest"], l + 1)
                act.activation(bcq[:, :], bcr[:, :], ACT.Copy).then_inc(s["bc1"], 1)
                for h in range(NH):
                    act.wait_ge(s["dl_ready"], l * NH + (h + 1))
                    act.activation(cv[:, h, :], (pa_wide, pb_wide)[h], ACT.Abs, bias=cols[:, h, TAPS + 1:TAPS + 2]).then_inc(s["dl_abs"], 1)
                for h in range(NH):
                    act.wait_ge(s["dl_abs"], l * NH + (h + 1))
                    act.activation(cv[:, h, :], cv[:, h, :], ACT.Exp, scale=-1.0).then_inc(s["dl_exp"], 1)
                for h in range(NH):
                    act.wait_ge(s["dl_exp"], l * NH + (h + 1))
                    act.activation(cv[:, h, :], cv[:, h, :], ACT.Ln, bias=1.0).then_inc(s["dl_ln"], 1)
                act.activation(neg_a[:, :, :], cols[:, :, TAPS + 2:TAPS + 2 + STATE], ACT.Exp).then_inc(s["a_exp"], 1)
                act.wait_ge(s["a_neg"], l + 1)
                act.wait_ge(s["delta"], l * NH + NH)
                for b in range(BATCH):
                    S0 = l * PER_LAYER + b * STATE

                    def copy_b(S, ring):
                        act.wait_ge(s["b_ready"], S + 1)
                        act.wait_ge(s["drive_done"], S * 2 + 1)
                        act.sem_inc(s["act_begun"], 1)
                        act.activation(b_sb[:, bass.ds(ring, 1), :].rearrange("p o t -> p (o t)"), p_b, ACT.Copy).then_inc(s["b_copied"], 1)

                    def decays(S, si):
                        for h in range(NH):
                            act.wait_ge(s["scan_done"], S * 2 + (h + 1))
                            act.sem_inc(s["act_begun"], 1)
                            act.activation(decay[:, h, :], delta[:, h, b * SEQ:(b + 1) * SEQ], ACT.Exp,
                                           scale=neg_a[:, h, bass.ds(si, 1)]).then_inc(s["exp_done"], 1)

                    copy_b(S0, 0)
                    copy_b(S0 + 1, 1)
                    with act.Fori(0, STATE - 2) as si:
                        decays(S0 + si, si)
                        copy_b(S0 + si + 2, (si + 2) % 4)
                    with act.Fori(STATE - 2, STATE) as si:
                        decays(S0 + si, si)
                    act.wait_ge(s["out_ready"], l * BATCH + (b + 1))
                    act.activation(u[:, b * SEQ:(b + 1) * SEQ], p_b, ACT.Copy).then_inc(s["u_done"], 1)

        @block.gpsimd
        def _(pool):
            pool.memset(pad[:, :, :, 0:TAPS - 1], 0.0).then_inc(s["pad_zero"], 1)
            pool.sem_inc(s["drive_done"], 7)
            with pool.Fori(0, LAYERS) as l:
                pool.wait_ge(s["w_loaded"], l * 32 + 32)
                for h in range(NH):
                    pool.wait_ge(s["u_done"], l * BATCH + 1)
                    pool.sem_inc(s["begun"], 1)
                    pool.tensor_scalar(diag[:, h, :], ident[:, :], cols[:, h, COLS - 1:COLS], None, ALU.mult).then_inc(s["diag"], 1)
                pool.wait_ge(s["du_done"], l * NH + NH)
                pool.sem_inc(s["begun"], 1)
                for b in range(BATCH):
                    S0 = l * PER_LAYER + b * STATE
                    with pool.Fori(0, STATE) as si:
                        S = S0 + si
                        pool.wait_ge(s["b_copied"], S + 2)
                        for h in range(NH):
                            pool.wait_ge(s["scan_done"], S * 2 + (h + 1))
                            pool.sem_inc(s["begun"], 1)
                            pool.tensor_tensor(drive[:, h, :], du[:, h, b * SEQ:(b + 1) * SEQ],
                                               b_sb[:, bass.ds(si % 4, 1), :].rearrange("p o t -> p (o t)"), ALU.mult).then_inc(s["drive_done"], 1)

        @block.vector
        def _(dve):
            dve.sem_inc(s["scan_done"], 2)
            dve.sem_inc(s["prod_done"], 2)
            dve.sem_inc(s["pre_done"], 1)
            with dve.Fori(0, LAYERS) as l:
                for h in range(NH):
                    dve.wait_ge(s["tap0"], l * NH + (h + 1))
                    v = cv[:, h, :].rearrange("p (b t) -> p b t", b=BATCH)
                    for j in range(1, TAPS):
                        if j > 1:
                            dve.wait_ge(s["taps"], l * 6 + (3 * h + j - 1))
                        dve.scalar_tensor_tensor(out=v, in0=pad[:, h, :, j:j + SEQ], scalar=cols[:, h, j:j + 1], in1=v,
                                                 op0=ALU.mult, op1=ALU.add).then_inc(s["taps"], 1)
                dve.wait_ge(s["bc0"], l + 1)
                dve.tensor_tensor(bcr[:, :], pb_wide[0:6 * STATE, :], bcp[:, :], ALU.subtract).then_inc(s["bc_rest"], 1)
                dve.wait_ge(s["bc1"], l + 1)
                dve.tensor_copy(bcp[32:64, :], bcq[32:64, :]).then_inc(s["bc_ready"], 1)
                dve.tensor_tensor(bcp[64:96, :], bcr[64:96, :], bcq[64:96, :], ALU.subtract).then_inc(s["bc_ready"], 1)
                for h in range(NH):
                    dve.wait_ge(s["dl_abs"], l * NH + (h + 1))
                    dve.tensor_scalar(delta[:, h, :], (pa_wide, pb_wide)[h], cols[:, h, TAPS + 1:TAPS + 2], 0.0,
                                      ALU.add, ALU.max).then_inc(s["dl_relu"], 1)
                for h in range(NH):
                    dve.wait_ge(s["dl_ln"], l * NH + (h + 1))
                    dve.wait_ge(s["dl_relu"], l * NH + (h + 1))
                    dve.tensor_tensor(delta[:, h, :], delta[:, h, :], cv[:, h, :], ALU.add).then_inc(s["delta"], 1)
                    dve.wait_ge(s["delta"], l * NH + (h + 1))
                    dve.tensor_tensor(du[:, h, :], delta[:, h, :], xc[:, h, :], ALU.mult).then_inc(s["du_done"], 1)
                dve.wait_ge(s["a_exp"], l + 1)
                dve.tensor_scalar(neg_a[:, :, :], neg_a[:, :, :], -1.0, None, ALU.mult).then_inc(s["a_neg"], 1)
                dve.wait_ge(s["diag"], l * NH + NH)
                dve.wait_ge(s["dl_abs"], l * NH + NH)
                dve.wait_ge(s["bc_ready"], l * 2 + 2)
                dve.wait_ge(s["du_done"], l * NH + NH)
                dve.sem_inc(s["pre_done"], 1)
                for b in range(BATCH):
                    S0 = l * PER_LAYER + b * STATE
                    with dve.Fori(0, STATE) as si:
                        S = S0 + si
                        for h in range(NH):
                            dve.wait_ge(s["exp_done"], S * 2 + (h + 3))
                            dve.wait_ge(s["drive_done"], S * 2 + (h + 8))
                            dve.wait_ge(s["prod_done"], S * 2 + (h + 1))
                            dve.tensor_tensor_scan(state[:, h, :], decay[:, h, :], drive[:, h, :], 0.0, ALU.mult, ALU.add).then_inc(s["scan_done"], 1)
                            dve.wait_ge(s["scan_done"], S * 2 + (h + 3))
                            dve.wait_ge(s["c_ready"], S + 1)
                            dve.wait_ge(s["y_done"], S * 2 + (h + 1))
                            dve.tensor_tensor(prod[:, h, :], state[:, h, :], p_c, ALU.mult).then_inc(s["prod_done"], 1)
                    dve.wait_ge(s["y_done"], S0 * 2 + (2 * STATE + 2))
                    dve.tensor_tensor(cv[:, :, b * SEQ:(b + 1) * SEQ], pa_wide.rearrange("p (h t) -> p h t", h=NH),
                                      zs[:, :, b * SEQ:(b + 1) * SEQ], ALU.mult).then_inc(s["yg_done"], 1)


def finish(nc, whole, d, ident, x, gate, u, out):
    turned, mixed, added, stored = (whole.sem(f"f_{n}") for n in ("turned", "mixed", "added", "stored"))
    out = out.rearrange("b (t p) c -> p (b t) c", p=P)
    with ExitStack() as st:
        c = Core(nc, st)
        res = c.sb("f_res", [P, TILES, DIM])
        pt = c.ps("f_pt", [P, TILES, P])
        block = st.enter_context(nc.Block())

        @block.tensor
        def _(pe):
            for t in range(TILES):
                pe.transpose(pt[:, t, :], u[:, t * P:(t + 1) * P], ident[:, :]).then_inc(turned, 1)

        @block.vector
        def _(dve):
            for n in range(TILES // 4):
                tt = slice(4 * n, 4 * n + 4)
                dve.wait_ge(turned, 4 * n + 4)
                dve.tensor_tensor(res[:, tt, :], pt[:, tt, :], gate[:, tt, :], ALU.mult).then_inc(mixed, 1)
                dve.wait_ge(mixed, n + 1)
                dve.tensor_tensor(res[:, tt, :], res[:, tt, :], x[:, tt, :], ALU.add).then_inc(added, 1)

        @block.sync
        def _(sp):
            for n in range(TILES // 4):
                tt = slice(4 * n, 4 * n + 4)
                sp.wait_ge(added, n + 1)
                sp.dma_start(out[:, tt, :], res[:, tt, :]).then_inc(stored, 16)
            sp.wait_ge(stored, 16 * (TILES // 4))


def program(nc, d, out, debug=None):
    with ExitStack() as stack:
        whole = Core(nc, stack)
        dram = lambda name, shape, dt=F32: nc.dram_tensor(name, shape, dt, kind="Internal").ap()
        parts_scr = dram("parts_scr", (2, 3, BATCH, DIM, SEQ), BF16)
        bias_scr = dram("bias_scr", (3, GROUPS, HEADS_PER_GROUP, BIAS_R, SEQ), BF16)
        x = whole.sb("x", [P, TILES, DIM])
        xn = whole.sb("xn", [P, TILES, DIM])
        xnT = whole.sb("xnT", [P, TOK])
        ident = whole.sb("ident", [P, P])

        layer_norm(nc, whole, "a", x, xn, xnT, ident,
                   [(x[:, :, :], d["x"].rearrange("(t p) c -> p t c", p=P)), (ident[:, :], d["ident"])])
        with ExitStack() as st:
            c = Core(nc, st)
            o_all = c.sb("o_all", [P, GROUPS, SEQ])
            with ExitStack() as st2:
                c = Core(nc, st2)
                v_all = c.sb("v_all", [P, GROUPS, QT, 32])
                tri_all = c.sb("tri_all", [P, HEADS, P])
                s8 = c.sb("s8", [P, HEADS])
                project_qkv(nc, whole, d, xnT, ident, v_all, tri_all, s8, parts_scr, bias_scr)
                attention(nc, whole, d, ident, v_all, tri_all, s8, parts_scr, bias_scr, o_all)
            if debug == "attention":
                dump(nc, whole, out, o_all[:, 0, :])
                return
            ffn_and_mix(nc, whole, d, ident, o_all, x, xnT)
        layer_norm(nc, whole, "n", x, xn, xnT, ident, [])
        if debug == "ffn":
            dump(nc, whole, out, x[:, :, :])
            return
        gate = whole.sb("gate", [P, TILES, DIM])
        experts(nc, whole, d, ident, xn, xnT, gate)
        if debug == "experts":
            dump(nc, whole, out, gate[:, :, :])
            return
        mamba(nc, whole, d, ident, xnT, xn[:, :, :].rearrange("p t c -> p (t c)").rearrange("p (h t) -> p h t", h=2))
        if debug == "mamba":
            dump(nc, whole, out, xnT[:, :])
            return
        finish(nc, whole, d, ident, x, gate, xnT, out)


def dump(nc, whole, out, src):
    done = whole.sem("dumped")
    with nc.Block() as block:
        @block.sync
        def _(sp):
            sp.dma_start(out, src).then_inc(done, 16)
            sp.wait_ge(done, 16)


def layout(a):
    import numpy as np

    f32 = np.float32
    w = np.asarray(a["L0_attn_qkv_w"])
    swap = np.arange(DIM).reshape(HEADS, 2, HEAD_DIM // 2)[:, ::-1].reshape(DIM)
    q, k, v = w[0:DIM], w[DIM:2 * DIM], w[2 * DIM:]
    m = {"x": np.asarray(a["L0_attn_x"]).reshape(TOK, DIM),
         "w_qkv": np.ascontiguousarray(np.stack([q, q[swap], k, k[swap], v]).transpose(2, 0, 1)),
         "slopes": np.asarray(a["L0_attn_slopes"]),
         "slopes_rows": np.ascontiguousarray(np.repeat(np.asarray(a["L0_attn_slopes"]).reshape(2, 8), BIAS_R, axis=1).T)}
    inv = f32(1.0) / np.power(f32(10000.0), np.arange(0, HEAD_DIM, 2, dtype=f32) / f32(HEAD_DIM)).astype(f32)
    ang = (np.arange(SEQ, dtype=f32)[:, None] * inv[None, :]).astype(f32).astype(np.float64)
    cos = np.tile(np.cos(ang).T, (2 * HEADS, 1))
    sin = np.tile(np.concatenate([-np.sin(ang).T, np.sin(ang).T]), (HEADS, 1))
    scale = HEAD_DIM ** -0.5
    m["rotation"] = np.ascontiguousarray(np.stack([cos * scale, sin * scale, cos, sin], axis=1).astype(f32))
    m["ident"] = np.eye(P, dtype=f32)

    bf = mybir.dt.np(BF16)
    m["ident_bf16"] = np.eye(P).astype(bf)
    i = np.arange(P)
    m["tri_qk"] = np.minimum(i[None, :] - i[:, None], 0).astype(f32)
    m["tri_kq"] = np.ascontiguousarray(m["tri_qk"].T)
    pos = np.arange(SEQ)
    rows_k, rows_q = [], []
    for b in range(1, QT):
        rows_k.append(np.where(pos < P * b, pos - P * b, 0))
        rows_q.append(pos // P == b)
    for b in range(1, QT):
        rows_k.append(np.where(pos < P * b, -1, 0))
        rows_q.append(np.where(pos // P == b, pos % P, 0))
    m["bias_keys"] = np.tile(np.stack(rows_k).astype(f32), (8, 1))
    m["bias_queries"] = np.ascontiguousarray(np.repeat(np.tile(np.stack(rows_q).astype(f32), (3, 1))[:, None, :], HEADS_PER_GROUP, axis=1)).astype(bf)
    m["ones_rows"] = np.ones((3, HEADS_PER_GROUP, SEQ), bf)
    down = np.asarray(a["L0_ffn_w_down"]).T.reshape(HIDDEN // P, P, DIM).transpose(1, 0, 2).reshape(P, HIDDEN)
    m["w_ffn"] = np.ascontiguousarray(np.stack([np.asarray(a["L0_ffn_w_gate"]).T, np.asarray(a["L0_ffn_w_up"]).T, down], axis=1))
    m["w_proj"] = np.ascontiguousarray(np.asarray(a["L0_attn_proj_w"]).T)
    m["proj_b"] = np.asarray(a["L0_attn_proj_b"])
    g = {n: np.asarray(a["L1_ffn_" + n]) for n in ("sW1", "sb1", "sW2", "sb2", "rW1", "rb1", "rW2", "rb2", "gW", "gb")}
    m["experts_w1"] = np.concatenate([g["rW1"], g["sW1"].reshape(DIM, 2, EXP_HID).transpose(1, 0, 2)])
    w2 = np.concatenate([g["rW2"], g["sW2"].reshape(2, EXP_HID, DIM)])
    m["experts_w2"] = np.ascontiguousarray(w2.reshape(ALL_EXPERTS, 2, P, DIM).transpose(0, 2, 1, 3))
    b1 = np.concatenate([g["rb1"], g["sb1"].reshape(2, EXP_HID)])
    m["experts_b1"] = np.ascontiguousarray(b1.reshape(ALL_EXPERTS, 2, P).transpose(2, 0, 1))
    m["experts_b2"] = np.concatenate([g["rb2"], g["sb2"], np.zeros((1, DIM), f32)])
    m["gate_w"], m["gate_b"] = g["gW"], g["gb"]
    restart = np.ones((P, TILES, EXPERTS), f32)
    restart[:, :, 0] = 0
    m["restart"] = restart
    t = {n: np.asarray(a["L1_attn_" + n]) for n in ("in_proj_w", "conv_w", "conv_b", "x_proj_w", "dt_proj_w", "dt_proj_b", "A_log", "D", "out_proj_w")}
    halves = lambda v: v.reshape(LAYERS, NH, P, -1).transpose(0, 2, 1, 3)
    w_x = t["x_proj_w"].transpose(0, 2, 1)
    bc, dt = w_x[:, :, RANK:], w_x[:, :, :RANK]
    m["mamba_w"] = np.ascontiguousarray(np.concatenate(
        [t["in_proj_w"].transpose(0, 2, 1)]
        + [halves(np.concatenate([bc, bc, bc, dt], axis=2)).reshape(LAYERS, P, -1)]
        + [halves(np.concatenate([t["conv_w"], t["conv_b"][:, :, None], t["dt_proj_b"][:, :, None], t["A_log"], t["D"][:, :, None]],
                                 axis=2)).reshape(LAYERS, P, -1)], axis=2))
    m["mamba_w_dt"] = np.ascontiguousarray(t["dt_proj_w"].transpose(0, 2, 1))
    m["mamba_w_out"] = np.ascontiguousarray(halves(t["out_proj_w"].transpose(0, 2, 1)))
    m["select"] = np.ascontiguousarray(np.tile(np.repeat(np.eye(2 * STATE)[:, :, None], P, axis=2), (3, 1, 1))).astype(bf)
    return m


_OUT = (BATCH, SEQ, DIM)


def kernel(**inputs):
    import concourse.bacc as bacc
    import numpy as np
    from concourse.bass_utils import run_bass_kernel_spmd

    nc = bacc.Bacc("TRN2", target_bir_lowering=False, num_devices=1)
    arrays = {f"in_{n}": np.ascontiguousarray(v) for n, v in layout(inputs).items()}
    d = {n[3:]: nc.dram_tensor(n, v.shape, mybir.dt.from_np(v.dtype), kind="ExternalInput").ap() for n, v in arrays.items()}
    out = nc.dram_tensor("out", _OUT, F32, kind="ExternalOutput").ap()
    program(nc, d, out)
    r = run_bass_kernel_spmd(nc, [arrays], core_ids=[0])
    return r.results[0]["out"]
```

```python
from contextlib import ExitStack

import concourse.bass as bass
from concourse import mybir

F32 = mybir.dt.float32
BF16 = mybir.dt.bfloat16
I32 = mybir.dt.int32
ALU = mybir.AluOpType
ACT = mybir.ActivationFunctionType
AX = mybir.AxisListType

P = 128
BATCH, SEQ, DIM = 2, 1024, 128
TOK = BATCH * SEQ
TILES = TOK // P
HALF = 512
HEADS, HEAD_DIM = 16, 8
HEADS_PER_GROUP = 4
HEAD_GROUPS = HEADS // HEADS_PER_GROUP
GROUPS = BATCH * HEAD_GROUPS
QT = SEQ // P
PAIR_ROWS = 9 * HEAD_DIM
BIAS_R = 2 * (QT - 1)
BIAS_ROWS = 3 * BIAS_R
MAX_ROW = PAIR_ROWS + BIAS_ROWS
PACK_ROWS = MAX_ROW + 3
RING = 4
MAX_BIAS = 8.0
LN_EPS = 1e-5
HIDDEN = 384
QSCALE = 1.0 / 127.0
EXPERTS = 15
TOP_K = 3


STORES = 3 * BATCH * (2 + 2)


class Core:

    def __init__(self, nc, stack):
        self.nc, self.stack = nc, stack

    def sb(self, name, shape, dt=F32):
        return self.stack.enter_context(self.nc.sbuf_tensor(name, shape, dt))

    def ps(self, name, shape, dt=F32):
        return self.stack.enter_context(self.nc.psum_tensor(name, shape, dt))

    def sem(self, name):
        return self.stack.enter_context(self.nc.semaphore(name))


def layer_norm(nc, whole, tag, x, xn, xnT, ident, loads):
    loaded, stats_done, mv_done, var_done = (whole.sem(f"{tag}_{n}") for n in ("loaded", "stats_done", "mv_done", "var_done"))
    rstd_done, norm_done, turned, copied = (whole.sem(f"{tag}_{n}") for n in ("rstd_done", "norm_done", "turned", "copied"))
    with ExitStack() as st:
        c = Core(nc, st)
        stats = c.sb(f"{tag}_stats", [P, TILES, 6])
        mv = c.sb(f"{tag}_mv", [P, TILES, 2])
        var = c.sb(f"{tag}_var", [P, TILES])
        power = c.sb(f"{tag}_power", [P, TILES])
        rstd = c.sb(f"{tag}_rstd", [P, TILES])
        psT = c.ps(f"{tag}_psT", [P, TOK])
        block = st.enter_context(nc.Block())

        @block.sync
        def _(sp):
            for dst, src in loads:
                sp.dma_start(dst, src).then_inc(loaded, 16)

        @block.gpsimd
        def _(pool):
            pool.memset(power[:, :], -0.5).then_inc(var_done, 1)
            pool.wait_ge(var_done, 2)
            pool.tensor_tensor(rstd[:, :], var[:, :], power[:, :], ALU.pow).then_inc(rstd_done, 1)

        @block.vector
        def _(dve):
            if loads:
                dve.wait_ge(loaded, 16 * len(loads))
            for t in range(TILES):
                dve.bn_stats(stats[:, t, :], x[:, t, :]).then_inc(stats_done, 1)
            for t in range(TILES):
                dve.wait_ge(stats_done, t + 1)
                dve.bn_aggr(mv[:, t, :], stats[:, t, :]).then_inc(mv_done, 1)
            dve.wait_ge(mv_done, TILES)
            dve.tensor_scalar(var[:, :], mv[:, :, 1], LN_EPS, None, ALU.add).then_inc(var_done, 1)
            dve.wait_ge(rstd_done, 1)
            for t in range(TILES):
                dve.tensor_scalar(xn[:, t, :], x[:, t, :], mv[:, t, 0:1], rstd[:, t:t + 1],
                                  ALU.subtract, ALU.mult).then_inc(norm_done, 1)

        @block.tensor
        def _(pe):
            if loads:
                pe.wait_ge(loaded, 16 * len(loads))
            for t in range(TILES):
                pe.wait_ge(norm_done, t + 1)
                pe.transpose(psT[:, t * P:(t + 1) * P], xn[:, t, :], ident[:, :]).then_inc(turned, 1)

        @block.scalar
        def _(act):
            for n in range(TOK // HALF):
                act.wait_ge(turned, 4 * (n + 1))
                act.activation(xnT[:, n * HALF:(n + 1) * HALF], psT[:, n * HALF:(n + 1) * HALF],
                               ACT.Copy).then_inc(copied, 1)


def project_qkv(nc, whole, d, xnT, ident, v_all, tri_all, s8, w_ffn, parts_scr, bias_scr, stored):
    loaded, proj_done, rot_cos, rot_sin, rot_add = (whole.sem(n) for n in ("b_loaded", "b_proj_done", "b_rot_cos", "b_rot_sin", "b_rot_add"))
    part0, rest0, part1, part2 = (whole.sem(n) for n in ("b_part0", "b_rest0", "b_part1", "b_part2"))
    v_done, v_copied, kb_full, kb_part0, kb_rest, kb_part1, kb_part2 = (
        whole.sem(n) for n in ("b_v_done", "b_v_copied", "b_kb_full", "b_kb_part0", "b_kb_rest", "b_kb_part1", "b_kb_part2"))
    tri_done, s8_done = whole.sem("b_tri_done"), whole.sem("b_s8_done")
    int_loaded, w_cast, w_scaled = whole.sem("b_int_loaded"), whole.sem("b_w_cast"), whole.sem("b_w_scaled")
    with ExitStack() as st:
        c = Core(nc, st)
        kb_rows = 8 * BIAS_R
        parts = c.sb("b_parts", [P, 2, 3, TOK], BF16)
        kbp = c.sb("b_kbp", [kb_rows, 3, 2, SEQ], BF16)
        w = c.sb("b_w", [P, 5, P])
        cs = c.sb("b_cs", [P, 4, SEQ])
        f = c.sb("b_f", [P, 2, TOK])
        sin_part = c.sb("b_sin_part", [P, 2, HALF])
        triT = c.sb("b_triT", [P, P])
        slopes = c.sb("b_slopes", [P, HEADS])
        w_int = c.sb("b_w_int", [P, 3, HIDDEN], I32)
        kc = c.sb("b_kc", [kb_rows, SEQ])
        ks = c.sb("b_ks", [kb_rows, 2])
        kb = c.sb("b_kb", [kb_rows, 2, SEQ])
        pq = c.ps("b_pq", [P, 2, 2, HALF])
        pv = c.ps("b_pv", [P, TILES, P])
        block = st.enter_context(nc.Block())
        N = TOK // HALF

        @block.sync
        def _(sp):
            sp.dma_start(w[:, :, :], d["w_qkv"]).then_inc(loaded, 16)
            sp.dma_start(cs[:, :, :], d["rotation"]).then_inc(loaded, 16)
            sp.dma_start(triT[:, :], d["tri_kq"]).then_inc(loaded, 16)
            sp.dma_start(slopes[:, :], d["slopes"].partition_broadcast(P)).then_inc(loaded, 16)
            sp.dma_start(kc[:, :], d["bias_keys"]).then_inc(loaded, 16)
            sp.dma_start(ks[:, :], d["slopes_rows"]).then_inc(loaded, 16)
            sp.dma_start(w_int[:, :, :], d["w_ffn"]).then_inc(int_loaded, 16)
            for z in range(2):
                for i, ready in enumerate((part0, part1, part2)):
                    sp.wait_ge(ready, z + 1)
                    for b in range(BATCH):
                        sp.dma_start(parts_scr[z, i, b], parts[:, z, i, b * SEQ:(b + 1) * SEQ]).then_inc(stored, 16)
            for i, ready in enumerate((kb_part0, kb_part1, kb_part2)):
                sp.wait_ge(ready, 1)
                for hh in range(2):
                    for b in range(BATCH):
                        g0 = b * HEAD_GROUPS + 2 * hh
                        sp.dma_start(bias_scr[i, g0:g0 + 2].rearrange("g h r k -> (g h r) k"),
                                     kbp[:, i, hh, :]).then_inc(stored, 16)

        @block.tensor
        def _(pe):
            pe.wait_ge(loaded, 96)
            for s in range(2 * N):
                n, z = s // 2, s % 2
                if s >= 2:
                    pe.wait_ge(rot_sin, s - 1)
                for j in range(2):
                    mm = pe.matmul(pq[:, s % 2, j, :], w[:, 2 * z + j, :], xnT[:, n * HALF:(n + 1) * HALF],
                                   start=True, stop=True)
                mm.then_inc(proj_done, 1)
                for t in range(2 * s, 2 * s + 2):
                    mm = pe.matmul(pv[:, t, :], xnT[:, t * P:(t + 1) * P], w[:, 4, :], start=True, stop=True)
                mm.then_inc(v_done, 1)

        @block.vector
        def _(dve):
            dve.wait_ge(loaded, 96)
            dve.tensor_scalar(s8[:, :], slopes[:, :], MAX_BIAS, None, ALU.mult).then_inc(s8_done, 1)
            for hh in range(2):
                dve.tensor_scalar(kb[:, hh, :], kc[:, :], ks[:, hh:hh + 1], MAX_BIAS,
                                  ALU.mult, ALU.mult).then_inc(kb_full, 1)
            for s in range(2 * N):
                n, z = s // 2, s % 2
                at = slice((n % 2) * HALF, (n % 2 + 1) * HALF)
                dst = f[:, z, n * HALF:(n + 1) * HALF]
                dve.wait_ge(proj_done, s + 1)
                dve.tensor_tensor(dst, pq[:, s % 2, 0, :], cs[:, 2 * z, at], ALU.mult).then_inc(rot_cos, 1)
                if s >= 2:
                    dve.wait_ge(rot_add, s - 1)
                dve.tensor_tensor(sin_part[:, s % 2, :], pq[:, s % 2, 1, :], cs[:, 2 * z + 1, at],
                                  ALU.mult).then_inc(rot_sin, 1)
                dve.wait_ge(rot_cos, s + 1)
                dve.wait_ge(rot_sin, s + 1)
                dve.tensor_tensor(dst, dst, sin_part[:, s % 2, :], ALU.add).then_inc(rot_add, 1)
            for z in range(2):
                dve.wait_ge(part0, z + 1)
                dve.tensor_tensor(f[:, z, :], f[:, z, :], parts[:, z, 0, :], ALU.subtract).then_inc(rest0, 1)
                dve.wait_ge(part1, z + 1)
                dve.tensor_tensor(parts[:, z, 2, :], f[:, z, :], parts[:, z, 1, :], ALU.subtract).then_inc(part2, 1)

        @block.scalar
        def _(act):
            act.wait_ge(kb_full, 2)
            act.activation(kbp[:, 0, :, :], kb[:, :, :], ACT.Copy).then_inc(kb_part0, 1)
            act.wait_ge(kb_rest, 1)
            act.activation(kbp[:, 1, :, :], kb[:, :, :], ACT.Copy).then_inc(kb_part1, 1)
            for n in range(N):
                act.wait_ge(v_done, 2 * (n + 1))
                b, k0 = 4 * n // QT, 4 * n % QT
                act.activation(v_all[:, b * HEAD_GROUPS:(b + 1) * HEAD_GROUPS, k0:k0 + 4, :].rearrange("p g k x -> p k g x"),
                               pv[:, 4 * n:4 * n + 4, :].rearrange("p k (g x) -> p k g x", g=HEAD_GROUPS),
                               ACT.Copy).then_inc(v_copied, 1)
            for z in range(2):
                act.wait_ge(rot_add, 2 * N)
                act.activation(parts[:, z, 0, :], f[:, z, :], ACT.Copy).then_inc(part0, 1)
                act.wait_ge(rest0, z + 1)
                act.activation(parts[:, z, 1, :], f[:, z, :], ACT.Copy).then_inc(part1, 1)

        @block.gpsimd
        def _(pool):
            pool.wait_ge(loaded, 96)
            pool.wait_ge(s8_done, 1)
            pool.wait_ge(kb_part0, 1)
            pool.tensor_tensor(kb[:, :, :], kb[:, :, :], kbp[:, 0, :, :], ALU.subtract).then_inc(kb_rest, 1)
            pool.wait_ge(kb_part1, 1)
            pool.tensor_tensor(kbp[:, 2, :, :], kb[:, :, :], kbp[:, 1, :, :], ALU.subtract).then_inc(kb_part2, 1)
            for h in range(HEADS):
                pool.tensor_scalar(tri_all[:, h, :], triT[:, :], s8[:, h:h + 1], None, ALU.mult).then_inc(tri_done, 1)
            pool.wait_ge(int_loaded, 16)
            pool.tensor_copy(w_ffn[:, :, :], w_int[:, :, :]).then_inc(w_cast, 1)
            pool.wait_ge(w_cast, 1)
            pool.tensor_scalar(w_ffn[:, :, :], w_ffn[:, :, :], QSCALE, None, ALU.mult).then_inc(w_scaled, 1)


def attention(nc, whole, d, ident, v_all, tri_all, s8, parts_scr, bias_scr, o_all, xnT, w_ffn, mix_gate, stored):
    names = ("pack_loaded", "ones_loaded", "scores_ready", "exp_done", "pv_done", "o_copied", "v_ready", "v_fixed",
             "maxs_ready", "maxs_free", "center_done", "max_done", "neg_done", "mp0", "mr0", "mp1", "mr1", "mp2", "m_turned",
             "m_copied", "m_stored", "w_zero", "gtri_loaded", "begun", "sp_begun",
             "gu_ready", "silu_done", "gu_read", "down_ready", "gate_done")
    s = {n: whole.sem("c_" + n) for n in names}
    with ExitStack() as st:
        c = Core(nc, st)
        qpack = c.sb("c_qpack", [PACK_ROWS, RING, HEADS_PER_GROUP, SEQ], BF16)
        kpack = c.sb("c_kpack", [PACK_ROWS, RING, HEADS_PER_GROUP, SEQ], BF16)
        probs = c.sb("c_probs", [P, 8, SEQ])
        v_cur = c.sb("c_v_cur", [P, QT, HEADS_PER_GROUP, 32])
        window = c.sb("c_window", [P, HEADS_PER_GROUP, 7 * P])
        tri = c.sb("c_tri", [P, P])
        identb = c.sb("c_identb", [P, P], BF16)
        junk = c.sb("c_junk", [P, 2, HALF], BF16)
        mx = c.sb("c_mx", [P, 32, 2])
        neg = c.sb("c_neg", [P, 32])
        negp = c.sb("c_negp", [P, 3, 32], BF16)
        neg_rows = c.sb("c_neg_rows", [96, P], BF16)
        pst = c.ps("c_pst", [P, 2, SEQ])
        pmax = c.ps("c_pmax", [P, 2, HALF])
        po = c.ps("c_po", [P, SEQ])
        block = st.enter_context(nc.Block())
        KH = HIDDEN // P
        N = TOK // HALF
        hT = probs[:, 0:2 * KH, :].rearrange("p (m b) t -> p m (b t)", m=KH)
        act_gate = probs[:, 2 * KH, :].rearrange("p (i c) -> p i c", i=2)
        pgu = pst[:, :, :].rearrange("p i (j c) -> p i j c", j=2)
        pdown = po[:, :].rearrange("p (i c) -> p i c", i=2)

        LOADS = 9 + 9 + 3
        LEAD = 28

        def load_group(q, g, ring):
            for z, pack in enumerate((qpack, kpack)):
                for i in range(3):
                    for j in range(3):
                        src = parts_scr[z, (i, j)[z]].rearrange("b (g h d) t -> (b g) d h t", g=HEAD_GROUPS, d=HEAD_DIM)
                        r0 = HEAD_DIM * (3 * i + j)
                        src = src[bass.ds(g, 1)].rearrange("o d h t -> (o d) h t")
                        dst = pack[r0:r0 + HEAD_DIM, bass.ds(ring, 1)].rearrange("d o h t -> d (o h) t")
                        q.dma_start(dst, src).then_inc(s["pack_loaded"], 16)
            for i in range(3):
                r0 = PAIR_ROWS + BIAS_R * i
                src = bias_scr[i][bass.ds(g, 1)].rearrange("o h r k -> r (o h) k")
                q.dma_start(kpack[r0:r0 + BIAS_R, bass.ds(ring, 1)].rearrange("r o h k -> r (o h) k"),
                            src).then_inc(s["pack_loaded"], 16)
            q.wait_ge(s["pack_loaded"], (g + 1) * (16 * LOADS))
            q.sem_inc(s["sp_begun"], 1)

        @block.sync
        def _(sp):
            sp.sem_inc(s["m_stored"], 16)
            sp.dma_start(tri[:, :], d["tri_qk"]).then_inc(s["gtri_loaded"], 16)
            sp.dma_start(identb[:, :], d["ident_bf16"]).then_inc(s["gtri_loaded"], 16)
            sp.wait_ge(stored, 16 * STORES)
            for r in range(RING):
                sp.dma_start(qpack[PAIR_ROWS:MAX_ROW, r], d["bias_queries"]).then_inc(s["ones_loaded"], 16)
                sp.dma_start(kpack[MAX_ROW:PACK_ROWS, r], d["ones_rows"]).then_inc(s["ones_loaded"], 16)
            for g in range(RING):
                load_group(sp, g, g)

            def store_max(g):
                sp.wait_ge(s["m_copied"], g + 1)
                sp.sem_inc(s["sp_begun"], 1)
                for i in range(3):
                    dst = qpack[MAX_ROW + i:MAX_ROW + i + 1, bass.ds(g % RING, 1)].rearrange("r o h (t q) -> r (o h t) q", q=P)
                    sp.dma_start(dst, neg_rows[32 * i:32 * i + 32, :]).then_inc(s["m_stored"], 16)

            store_max(0)
            with sp.Fori(0, GROUPS - RING) as g:
                store_max(g + 1)
                sp.wait_ge(s["pv_done"], (g + 1) * QT + 1)
                sp.sem_inc(s["sp_begun"], 1)
                load_group(sp, g + RING, g)
            with sp.Fori(GROUPS - RING, GROUPS - 1) as g:
                store_max(g + 1)
            sp.wait_ge(s["m_stored"], 48 * GROUPS + 16)

        @block.gpsimd
        def _(pool):
            pool.memset(window[:, :, :], 0.0).then_inc(s["w_zero"], 1)
            pool.memset(v_cur[:, :, :, :], 0.0).then_inc(s["v_fixed"], 1)
            pool.wait_ge(s["v_fixed"], 1)
            pool.memset(v_cur[:, :, :, HEAD_DIM:HEAD_DIM + 1], 1.0).then_inc(s["v_fixed"], 1)
            pool.wait_ge(s["v_fixed"], 2)
            with pool.Fori(0, GROUPS) as g:
                pool.wait_ge(s["pv_done"], g * QT + 1)
                pool.tensor_copy(v_cur[:, :, :, 0:HEAD_DIM],
                                 v_all[:, bass.ds(g, 1)].rearrange("p o k (h x) -> p (o k) h x", x=HEAD_DIM)).then_inc(s["v_ready"], 1)

        def max_tiles(pe, g, n0, n1, first):
            for n in range(n0, n1):
                h, qt, half = n // 16, n // 2 % 8, n % 2
                if not (first and n < 2):
                    pe.wait_ge(s["maxs_free"], g * 65 + max(n - 1, 0))
                ring = g % RING
                q = qpack[0:MAX_ROW, bass.ds(ring, 1), h, qt * P:(qt + 1) * P].rearrange("r o q -> r (o q)")
                k = kpack[0:MAX_ROW, bass.ds(ring, 1), h, half * HALF:(half + 1) * HALF].rearrange("r o k -> r (o k)")
                pe.matmul(pmax[:, n % 2, :], q, k, start=True, stop=True).then_inc(s["maxs_ready"], 1)

        def turn_max(pe, g):
            pe.wait_ge(s["mp2"], g + 1)
            pe.transpose(pmax[0:96, 0, 0:P // 2].bitcast(BF16), negp[:, :, :].rearrange("p i x -> p (i x)"),
                         identb[:, :]).then_inc(s["m_turned"], 1)

        def second_pass(pe, g, with_next):
            ring = g % RING
            pe.wait_ge(s["m_stored"], (g + 1) * 48 + 16)
            if with_next:
                pe.wait_ge(s["pack_loaded"], (g + 2) * (16 * LOADS))
            for j in range(32):
                kt, h = j // 4, j % 4
                pe.wait_ge(s["exp_done"], g * 32 + (j + 1))
                k = kpack[:, bass.ds(ring, 1), h, kt * P:(kt + 1) * P].rearrange("r o k -> r (o k)")
                n0, n1 = (64 * j // LEAD, 64 * (j + 1) // LEAD) if with_next and j < LEAD else (0, 0)
                for half in range(2):
                    q = qpack[:, bass.ds(ring, 1), h, half * HALF:(half + 1) * HALF].rearrange("r o q -> r (o q)")
                    diag = kt // 4 == half
                    mm = pe.matmul(pst[:, j % 2, half * HALF:(half + 1) * HALF], k, q, start=True, stop=True,
                                   skip_group_check=diag)
                    if diag:
                        t = tri_all[:, bass.ds((g % HEAD_GROUPS) * HEADS_PER_GROUP + h, 1), :].rearrange("p o q -> p (o q)")
                        mm = pe.matmul(pst[:, j % 2, kt * P:(kt + 1) * P], ident[:, :], t, start=False, stop=True,
                                       skip_group_check=True)
                    if half == 0:
                        max_tiles(pe, g + 1, n0, min(n0 + 1, n1), False)
                mm.then_inc(s["scores_ready"], 1)
                max_tiles(pe, g + 1, n0 + 1, n1, False)
                if j >= 5 and (j - 5) % 4 == 0:
                    weigh(pe, g, (j - 5) // 4)
                if with_next and j == 31:
                    turn_max(pe, g + 1)
            weigh(pe, g, 7)

        def weigh(pe, g, kt):
            pe.wait_ge(s["exp_done"], g * 32 + (4 * kt + 6))
            if kt == 0:
                pe.wait_ge(s["v_ready"], g + 1)
                pe.wait_ge(s["o_copied"], g + 1)
            for half in range(2):
                for h in range(HEADS_PER_GROUP):
                    mm = pe.matmul(po[32 * h:32 * h + 32, half * HALF:(half + 1) * HALF], v_cur[:, kt, h, :],
                                   probs[:, 4 * (kt % 2) + h, half * HALF:(half + 1) * HALF],
                                   start=(kt == 0), stop=(kt == QT - 1))
            mm.then_inc(s["pv_done"], 1)

        @block.tensor
        def _(pe):
            pe.sem_inc(s["pv_done"], 1)
            for r in range(KH * N):
                n, m = r // KH, r % KH
                if r >= 2:
                    pe.wait_ge(s["gu_read"], r - 1)
                for j in range(2):
                    mm = pe.matmul(pgu[:, r % 2, j, :], w_ffn[:, j, m * P:(m + 1) * P], xnT[:, n * HALF:(n + 1) * HALF],
                                   start=True, stop=True)
                mm.then_inc(s["gu_ready"], 1)
            pe.wait_ge(s["gtri_loaded"], 32)
            pe.wait_ge(s["ones_loaded"], 16 * 2 * RING)
            pe.wait_ge(s["pack_loaded"], 16 * LOADS)
            for t in range(TILES):
                n = t // 4
                if t % 4 == 0:
                    pe.wait_ge(s["gu_read"], KH * (n + 1))
                    if n >= 2:
                        pe.wait_ge(s["gate_done"], n - 1)
                max_tiles(pe, 0, 4 * t, 4 * t + 4, True)
                for k in range(KH):
                    mm = pe.matmul(pdown[:, n % 2, t % 4 * P:(t % 4 + 1) * P], hT[:, k, t * P:(t + 1) * P],
                                   w_ffn[:, 2, k * P:(k + 1) * P], start=(k == 0), stop=(k == KH - 1))
                if t % 4 == 3:
                    mm.then_inc(s["down_ready"], 1)
            turn_max(pe, 0)
            with pe.Fori(0, GROUPS - 1) as g:
                second_pass(pe, g, True)
            second_pass(pe, GROUPS - 1, False)

        @block.scalar
        def _(act):
            act.sem_inc(s["o_copied"], 1)
            for r in range(KH * N):
                act.wait_ge(s["gu_ready"], r + 1)
                if r >= 2:
                    act.wait_ge(s["gu_read"], r - 1)
                act.activation(act_gate[:, r % 2, :], pgu[:, r % 2, 0, :], ACT.Silu).then_inc(s["silu_done"], 1)
            for n in range(N):
                act.wait_ge(s["down_ready"], n + 1)
                act.activation(mix_gate[:, 4 * n:4 * n + 4, :], pdown[:, n % 2, :].rearrange("p (t c) -> p t c", t=4),
                               ACT.Silu).then_inc(s["gate_done"], 1)
            act.sem_inc(s["exp_done"], 2)
            with act.Fori(0, GROUPS) as g:
                for j in range(32):
                    kt = j // 4
                    act.wait_ge(s["scores_ready"], g * 32 + (j + 1))
                    if j % 4 == 0:
                        if kt >= 2:
                            act.wait_ge(s["pv_done"], g * QT + kt)
                    act.activation(probs[:, j % 8, :], pst[:, j % 2, :], ACT.Exp).then_inc(s["exp_done"], 1)
                act.wait_ge(s["pv_done"], (g + 1) * QT + 1)
                act.activation(o_all[:, bass.ds(g, 1), :].rearrange("p o q -> p (o q)"), po[:, :], ACT.Copy).then_inc(s["o_copied"], 1)

        def maxima(dve, g):
            for h in range(HEADS_PER_GROUP):
                dve.tensor_scalar(window[:, h, 3 * P:4 * P], tri[:, :],
                                  s8[:, bass.ds((g % HEAD_GROUPS) * HEADS_PER_GROUP + h, 1)], None, ALU.mult).then_inc(s["center_done"], 1)
            dve.wait_ge(s["center_done"], (g + 1) * 4)
            for n in range(64):
                h, qt, half = n // 16, n // 2 % 8, n % 2
                dve.wait_ge(s["maxs_ready"], g * 64 + (n + 1))
                if qt // 4 == half:
                    if n >= 2:
                        dve.wait_ge(s["maxs_free"], g * 65 + (n - 1))
                    dve.sem_inc(s["begun"], 1)
                    o = 3 * P - P * (qt % 4)
                    dve.tensor_tensor_reduce(junk[:, half, :], pmax[:, n % 2, :], window[:, h, o:o + HALF], 1.0, -3e38,
                                             ALU.add, ALU.max, mx[:, n // 2, half:half + 1]).then_inc(s["maxs_free"], 1)
                else:
                    dve.tensor_reduce(mx[:, n // 2, half:half + 1], pmax[:, n % 2, :], AX.X, ALU.max).then_inc(s["maxs_free"], 1)
            dve.wait_ge(s["maxs_free"], g * 65 + 64)
            dve.tensor_reduce(neg[:, :], mx[:, :, :], AX.X, ALU.max, negate=True).then_inc(s["neg_done"], 1)
            dve.wait_ge(s["neg_done"], g + 1)
            dve.tensor_copy(negp[:, 0, :], neg[:, :]).then_inc(s["mp0"], 1)
            dve.wait_ge(s["mp0"], g + 1)
            dve.tensor_tensor(neg[:, :], neg[:, :], negp[:, 0, :], ALU.subtract).then_inc(s["mr0"], 1)
            dve.wait_ge(s["mr0"], g + 1)
            dve.tensor_copy(negp[:, 1, :], neg[:, :]).then_inc(s["mp1"], 1)
            dve.wait_ge(s["mp1"], g + 1)
            dve.tensor_tensor(negp[:, 2, :], neg[:, :], negp[:, 1, :], ALU.subtract).then_inc(s["mp2"], 1)
            dve.wait_ge(s["m_turned"], g + 1)
            dve.wait_ge(s["m_stored"], g * 48 + 16)
            dve.tensor_copy(neg_rows[:, :], pmax[0:96, 0, 0:P // 2].bitcast(BF16)).then_inc(s["m_copied"], 1)
            dve.wait_ge(s["m_copied"], g + 1)
            dve.sem_inc(s["maxs_free"], 1)

        @block.vector
        def _(dve):
            for r in range(KH * N):
                n, m = r // KH, r % KH
                dve.wait_ge(s["silu_done"], r + 1)
                dve.tensor_tensor(hT[:, m, n * HALF:(n + 1) * HALF], act_gate[:, r % 2, :], pgu[:, r % 2, 1, :],
                                  ALU.mult).then_inc(s["gu_read"], 1)
            dve.wait_ge(s["w_zero"], 1)
            dve.wait_ge(s["gtri_loaded"], 32)
            with dve.Fori(0, GROUPS) as g:
                maxima(dve, g)


def project_and_mix(nc, whole, d, ident, o_all, x, mix_gate):
    names = ("loaded", "turned", "recip", "o_read", "o_turned", "oT_copied", "proj_ready", "proj_read", "mul_done", "x_done")
    s = {n: whole.sem("d_" + n) for n in names}
    N = TOK // HALF
    with ExitStack() as st:
        c = Core(nc, st)
        w_proj = c.sb("d_w_proj", [P, DIM])
        bias = c.sb("d_bias", [P, DIM])
        recip = c.sb("d_recip", [P, TILES, HEADS])
        o_tok = c.sb("d_o_tok", [P, TILES, DIM])
        oT = c.sb("d_oT", [P, TOK])
        mix = c.sb("d_mix", [P, TILES, DIM])
        pturn = c.ps("d_pturn", [P, 4, HALF])
        pturn2 = c.ps("d_pturn2", [P, 2, HALF])
        prow = c.ps("d_prow", [P, 2, HALF])
        block = st.enter_context(nc.Block())

        @block.sync
        def _(sp):
            sp.dma_start(w_proj[:, :], d["w_proj"]).then_inc(s["loaded"], 16)
            sp.dma_start(bias[:, :], d["proj_b"].partition_broadcast(P)).then_inc(s["loaded"], 16)

        @block.tensor
        def _(pe):
            def rows_of(n):
                pe.wait_ge(s["o_read"], 4 * n + 4)
                if n >= 2:
                    pe.wait_ge(s["oT_copied"], n - 1)
                for t in range(4 * n, 4 * n + 4):
                    mm = pe.transpose(pturn2[:, n % 2, t % 4 * P:(t % 4 + 1) * P], o_tok[:, t, :], ident[:, :])
                mm.then_inc(s["o_turned"], 1)

            def project(n):
                pe.wait_ge(s["loaded"], 32)
                pe.wait_ge(s["oT_copied"], n + 1)
                if n >= 2:
                    pe.wait_ge(s["proj_read"], n - 1)
                for t in range(4 * n, 4 * n + 4):
                    mm = pe.matmul(prow[:, n % 2, t % 4 * P:(t % 4 + 1) * P], oT[:, t * P:(t + 1) * P], w_proj[:, :],
                                   start=True, stop=True)
                mm.then_inc(s["proj_ready"], 1)

            for t in range(TILES):
                b, qt = t // QT, t % QT
                if t >= 4:
                    pe.wait_ge(s["o_read"], t - 3)
                for hg in range(HEAD_GROUPS):
                    mm = pe.transpose(pturn[:, t % 4, hg * P:(hg + 1) * P],
                                      o_all[:, b * HEAD_GROUPS + hg, qt * P:(qt + 1) * P], ident[:, :])
                mm.then_inc(s["turned"], 1)
                if t >= 7 and t % 4 == 3:
                    rows_of(t // 4 - 1)
                    if t >= 11:
                        project(t // 4 - 2)
            rows_of(N - 1)
            project(N - 2)
            project(N - 1)

        @block.scalar
        def _(act):
            for n in range(N):
                act.wait_ge(s["o_turned"], n + 1)
                act.activation(oT[:, n * HALF:(n + 1) * HALF], pturn2[:, n % 2, :], ACT.Copy).then_inc(s["oT_copied"], 1)

        @block.gpsimd
        def _(pool):
            for n in range(N):
                tt = slice(4 * n, 4 * n + 4)
                pool.wait_ge(s["mul_done"], n + 1)
                pool.tensor_tensor(x[:, tt, :], x[:, tt, :], mix[:, tt, :], ALU.add).then_inc(s["x_done"], 1)

        @block.vector
        def _(dve):
            def mixed(n):
                tt = slice(4 * n, 4 * n + 4)
                dve.wait_ge(s["proj_ready"], n + 1)
                dve.wait_ge(s["loaded"], 32)
                dve.tensor_tensor(mix[:, tt, :], prow[:, n % 2, :].rearrange("p (t c) -> p t c", t=4),
                                  bias[:, :].unsqueeze(1).to_broadcast([P, 4, DIM]), ALU.add).then_inc(s["proj_read"], 1)
                dve.wait_ge(s["proj_read"], n + 1)
                dve.tensor_tensor(mix[:, tt, :], mix[:, tt, :], mix_gate[:, tt, :], ALU.mult).then_inc(s["mul_done"], 1)

            for t in range(TILES):
                v = pturn[:, t % 4, :].rearrange("p (h x) -> p h x", h=HEADS)
                dve.wait_ge(s["turned"], t + 1)
                dve.reciprocal(recip[:, t, :], v[:, :, HEAD_DIM]).then_inc(s["recip"], 1)
                dve.wait_ge(s["recip"], t + 1)
                dve.tensor_tensor(o_tok[:, t, :].rearrange("p (h x) -> p h x", h=HEADS), v[:, :, 0:HEAD_DIM],
                                  recip[:, t, :].unsqueeze(2).to_broadcast([P, HEADS, HEAD_DIM]), ALU.mult).then_inc(s["o_read"], 1)
            for n in range(N):
                mixed(n)


ALL_EXPERTS = EXPERTS + 2
EXP_HID = 256


def experts(nc, whole, d, ident, xn, xnT, gate_out):
    names = ("gate_loaded", "b_loaded", "logit_ready", "logit", "top", "shift", "expo", "total", "inv", "weight", "best", "gt", "eq", "ngt", "room",
             "cum", "allow", "both", "pick", "ones", "gated", "g_turned", "g_copied", "b2_ready", "acc_ready", "h_ready", "h_done",
             "y_ready", "y_read", "silu_done", "begun")
    s = {n: whole.sem("e_" + n) for n in names}
    w1_loaded = [whole.sem(f"e_w1_loaded{i}") for i in range(2)]
    w2_loaded = [whole.sem(f"e_w2_loaded{i}") for i in range(2)]
    E, A = EXPERTS, ALL_EXPERTS
    with ExitStack() as st:
        c = Core(nc, st)
        w_gate = c.sb("e_w_gate", [P, E])
        b_gate = c.sb("e_b_gate", [P, E])
        restart = c.sb("e_restart", [P, TILES, E])
        b1 = c.sb("e_b1", [P, A, 2])
        b2 = c.sb("e_b2", [A, DIM])
        w1 = c.sb("e_w1", [P, 2, EXP_HID])
        w2 = c.sb("e_w2", [P, 2, 2, DIM])
        hT = c.sb("e_hT", [P, 2, 2, TOK])
        wt = c.sb("e_wt", [P, TILES, E])
        small = c.sb("e_small", [P, 5, TILES])
        best = c.sb("e_best", [P, TILES, 8])
        gt = c.sb("e_gt", [P, TILES, E])
        eq = c.sb("e_eq", [P, TILES, E])
        cum = c.sb("e_cum", [P, TILES, E])
        gates = c.sb("e_gates", [P, A, TILES])
        gates_tok = c.sb("e_gates_tok", [P, TILES, A])
        gT = c.sb("e_gT", [A, TOK])
        ph = c.ps("e_ph", [P, 2, SEQ])
        py = c.ps("e_py", [P, 2, HALF])
        pg = c.ps("e_pg", [P, 2, HALF])
        block = st.enter_context(nc.Block())
        wide = lambda v: v.unsqueeze(2).to_broadcast([P, TILES, E])

        def load_w1(sp, e, par):
            sp.dma_start(w1[:, par, :], d["experts_w1"][bass.ds(e, 1)].rearrange("o c f -> (o c) f")).then_inc(w1_loaded[par], 16)

        def load_w2(sp, e, par):
            sp.dma_start(w2[:, par, :, :], d["experts_w2"][bass.ds(e, 1)].rearrange("o f k c -> (o f) k c")).then_inc(w2_loaded[par], 16)

        @block.sync
        def _(sp):
            sp.dma_start(w_gate[:, :], d["gate_w"]).then_inc(s["gate_loaded"], 16)
            sp.dma_start(b_gate[:, :], d["gate_b"].partition_broadcast(P)).then_inc(s["gate_loaded"], 16)
            sp.dma_start(restart[:, :, :], d["restart"]).then_inc(s["gate_loaded"], 16)
            for par in range(2):
                load_w1(sp, par, par)
                load_w2(sp, par, par)
            sp.dma_start(b1[:, :, :], d["experts_b1"]).then_inc(s["b_loaded"], 16)
            sp.dma_start(b2[:, :], d["experts_b2"]).then_inc(s["b_loaded"], 16)
            with sp.Fori(0, (A - 3) // 2) as i:
                for par in range(2):
                    sp.wait_ge(s["h_ready"], i * 8 + 4 * (par + 1))
                    load_w1(sp, i * 2 + (par + 2), par)
                    sp.wait_ge(s["y_ready"], i * 8 + 4 * (par + 1))
                    load_w2(sp, i * 2 + (par + 2), par)
            sp.wait_ge(s["h_ready"], 4 * (A - 2))
            load_w1(sp, A - 1, 0)
            sp.wait_ge(s["y_ready"], 4 * (A - 2))
            load_w2(sp, A - 1, 0)

        def hidden(pe, e, par, uses):
            pe.wait_ge(w1_loaded[par], uses * 16)
            for u in range(4):
                m, half = u // 2, u % 2
                pe.wait_ge(s["h_done"], e * 4 + (u + 1))
                for j in range(2):
                    at = half * SEQ + j * HALF
                    mm = pe.matmul(ph[:, u % 2, j * HALF:(j + 1) * HALF], w1[:, par, m * P:(m + 1) * P], xnT[:, at:at + HALF],
                                   start=True, stop=True)
                mm.then_inc(s["h_ready"], 1)

        def output(pe, e, par, uses):
            pe.wait_ge(w2_loaded[par], uses * 16)
            pe.wait_ge(s["h_done"], e * 4 + 6)
            for r in range(4):
                pe.wait_ge(s["y_read"], e * 16 + (4 * r + 12))
                for t in range(4 * r, 4 * r + 4):
                    for k in range(2):
                        mm = pe.matmul(py[:, r % 2, t % 4 * P:(t % 4 + 1) * P], hT[:, par, k, t * P:(t + 1) * P],
                                       w2[:, par, k, :], start=(k == 0), stop=(k == 1))
                mm.then_inc(s["y_ready"], 1)

        @block.tensor
        def _(pe):
            pe.wait_ge(s["gate_loaded"], 48)
            for t in range(TILES):
                mm = pe.matmul(pg[:, 0, t * 16:t * 16 + E], xnT[:, t * P:(t + 1) * P], w_gate[:, :], start=True, stop=True)
            mm.then_inc(s["logit_ready"], 1)
            hidden(pe, 0, 0, 1)
            pe.wait_ge(s["gated"], 1)
            for n in range(TILES // 4):
                if n >= 1:
                    pe.wait_ge(s["g_copied"], n)
                for t in range(4 * n, 4 * n + 4):
                    mm = pe.transpose(pg[0:A, 1, t % 4 * P:(t % 4 + 1) * P], gates_tok[:, t, :], ident[:, :])
                mm.then_inc(s["g_turned"], 1)
            pe.wait_ge(s["g_copied"], TILES // 4)
            pe.wait_ge(s["b_loaded"], 32)
            for n in range(TILES // 4):
                if n >= 1:
                    pe.wait_ge(s["acc_ready"], n)
                for t in range(4 * n, 4 * n + 4):
                    mm = pe.matmul(pg[:, 0, t % 4 * P:(t % 4 + 1) * P], gT[:, t * P:(t + 1) * P], b2[:, :], start=True, stop=True)
                mm.then_inc(s["b2_ready"], 1)
            with pe.Fori(0, (A - 1) // 2) as i:
                hidden(pe, i * 2 + 1, 1, i + 1)
                output(pe, i * 2, 0, i + 1)
                hidden(pe, i * 2 + 2, 0, i + 2)
                output(pe, i * 2 + 1, 1, i + 1)
            output(pe, A - 1, 0, (A + 1) // 2)

        @block.scalar
        def _(act):
            act.sem_inc(s["h_done"], 2)
            act.wait_ge(s["shift"], 1)
            act.activation(wt[:, :, :], wt[:, :, :], ACT.Exp).then_inc(s["expo"], 1)
            act.wait_ge(s["b_loaded"], 32)

            def transposed():
                for n in range(TILES // 4):
                    act.wait_ge(s["g_turned"], n + 1)
                    act.activation(gT[:, n * HALF:(n + 1) * HALF], pg[0:A, 1, :], ACT.Copy).then_inc(s["g_copied"], 1)

            def first(e, par):
                for u in range(4):
                    m, half = u // 2, u % 2
                    act.wait_ge(s["h_ready"], e * 4 + u + 1)
                    act.activation(hT[:, par, m, half * SEQ:(half + 1) * SEQ], ph[:, u % 2, :], ACT.Gelu,
                                   bias=b1[:, e, m:m + 1]).then_inc(s["h_done"], 1)

            first(0, 0)
            transposed()
            first(1, 1)
            with act.Fori(1, (A - 1) // 2) as i:
                for par in range(2):
                    for u in range(4):
                        m, half = u // 2, u % 2
                        if u == 0:
                            act.wait_ge(s["y_ready"], i * 8 + 4 * (par - 1))
                        act.wait_ge(s["h_ready"], i * 8 + (4 * par + u + 1))
                        act.sem_inc(s["begun"], 1)
                        bias = b1[:, bass.ds(i * 2 + par, 1), m:m + 1].rearrange("p o m -> p (o m)")
                        act.activation(hT[:, par, m, half * SEQ:(half + 1) * SEQ], ph[:, u % 2, :], ACT.Gelu,
                                       bias=bias).then_inc(s["h_done"], 1)
            act.wait_ge(s["y_ready"], 4 * (A - 2))
            first(A - 1, 0)
            for n in range(4):
                act.wait_ge(s["y_read"], TILES * A + 4 * n + 4)
                act.activation(gate_out[:, 4 * n:4 * n + 4, :], gate_out[:, 4 * n:4 * n + 4, :], ACT.Silu).then_inc(s["silu_done"], 1)

        @block.vector
        def _(dve):
            inc = lambda ins, name: (ins.then_inc(s[name], 1), dve.wait_ge(s[name], 1))
            dve.wait_ge(s["gate_loaded"], 48)
            dve.wait_ge(s["logit_ready"], 1)
            mx, total, inv, ngt, room = (small[:, n, :] for n in range(5))
            inc(dve.tensor_tensor(wt[:, :, :], pg[:, 0, 0:16 * TILES].rearrange("p (t e) -> p t e", e=16)[:, :, 0:E],
                                  b_gate[:, :].unsqueeze(1).to_broadcast([P, TILES, E]), ALU.add), "logit")
            inc(dve.tensor_reduce(mx, wt[:, :, :], AX.X, ALU.max), "top")
            dve.tensor_tensor(wt[:, :, :], wt[:, :, :], wide(mx), ALU.subtract).then_inc(s["shift"], 1)
            dve.wait_ge(s["expo"], 1)
            inc(dve.tensor_reduce(total, wt[:, :, :], AX.X, ALU.add), "total")
            inc(dve.reciprocal(inv, total), "inv")
            inc(dve.tensor_tensor(wt[:, :, :], wt[:, :, :], wide(inv), ALU.mult), "weight")
            for t in range(TILES):
                dve.max(best[:, t, :], wt[:, t, :]).then_inc(s["best"], 1)
            dve.wait_ge(s["best"], TILES)
            third = wide(best[:, :, TOP_K - 1])
            inc(dve.tensor_tensor(gt[:, :, :], wt[:, :, :], third, ALU.is_gt), "gt")
            inc(dve.tensor_tensor(eq[:, :, :], wt[:, :, :], third, ALU.is_equal), "eq")
            inc(dve.tensor_reduce(ngt, gt[:, :, :], AX.X, ALU.add), "ngt")
            inc(dve.tensor_scalar(room, ngt, -1.0, float(TOP_K), ALU.mult, ALU.add), "room")
            inc(dve.tensor_tensor_scan(cum[:, :, :].rearrange("p t e -> p (t e)"), restart[:, :, :].rearrange("p t e -> p (t e)"),
                                       eq[:, :, :].rearrange("p t e -> p (t e)"), 0.0, ALU.mult, ALU.add), "cum")
            inc(dve.tensor_tensor(cum[:, :, :], cum[:, :, :], wide(room), ALU.is_le), "allow")
            inc(dve.tensor_tensor(eq[:, :, :], eq[:, :, :], cum[:, :, :], ALU.mult), "both")
            inc(dve.tensor_tensor(gt[:, :, :], gt[:, :, :], eq[:, :, :], ALU.add), "pick")
            dve.memset(gates_tok[:, :, E:A], 1.0).then_inc(s["ones"], 1)
            dve.memset(gates[:, E:A, :], 1.0).then_inc(s["ones"], 1)
            dve.tensor_tensor(gates[:, 0:E, :].rearrange("p e t -> p t e"), wt[:, :, :], gt[:, :, :], ALU.mult).then_inc(s["ones"], 1)
            dve.wait_ge(s["ones"], 3)
            dve.tensor_tensor(gates_tok[:, :, 0:E], wt[:, :, :], gt[:, :, :], ALU.mult).then_inc(s["gated"], 1)
            for n in range(TILES // 4):
                dve.wait_ge(s["b2_ready"], n + 1)
                dve.tensor_tensor(gate_out[:, 4 * n:4 * n + 4, :], pg[:, 0, :].rearrange("p (t c) -> p t c", t=4),
                                  xn[:, 4 * n:4 * n + 4, :], ALU.add).then_inc(s["acc_ready"], 1)
            dve.wait_ge(s["acc_ready"], TILES // 4)
            dve.sem_inc(s["y_read"], TILES)

            with dve.Fori(0, A) as e:
                for t in range(TILES):
                    if t % 4 == 0:
                        dve.wait_ge(s["y_ready"], e * 4 + (t // 4 + 1))
                        dve.wait_ge(s["y_read"], e * 16 + (t + 4))
                    dve.scalar_tensor_tensor(out=gate_out[:, t, :], in0=py[:, t // 4 % 2, t % 4 * P:(t % 4 + 1) * P],
                                             scalar=gates[:, bass.ds(e, 1), t:t + 1].rearrange("p o t -> p (o t)"),
                                             in1=gate_out[:, t, :], op0=ALU.mult, op1=ALU.add).then_inc(s["y_read"], 1)


LAYERS, INNER, STATE, RANK, TAPS = 4, 256, 16, 8, 4
NH = INNER // P
COLS = TAPS + 1 + 1 + STATE + 1
X_ROWS = 3 * 2 * STATE + RANK


def mamba(nc, whole, d, ident, u, decay_xn):
    names = ("w_loaded", "wo_loaded", "sel_loaded", "pad_zero", "pre_ready", "pre_read", "tap0", "taps", "xc_done", "zs_done", "bc0",
             "bc1", "bc_ready", "dl_exp", "dl_ln", "delta", "du_done", "a_exp", "a_neg", "xd_done", "y_init",
             "b_ready", "b_copied", "c_ready", "exp_done", "drive_done", "scan_done", "prod_done", "y_done",
             "yg_done", "out_ready", "u_done", "begun", "act_begun", "sp_begun", "dve_begun")
    s = {n: whole.sem("m_" + n) for n in names}
    with ExitStack() as st:
        c = Core(nc, st)
        sel = c.sb("m_sel", [6 * STATE, 2 * STATE, P], BF16)
        w = c.sb("m_w", [P, 2 * INNER + NH * X_ROWS + NH * COLS])
        w_in = w[:, 0:2 * INNER]
        w_x = w[:, 2 * INNER:2 * INNER + NH * X_ROWS].rearrange("p (k r) -> p k r", k=NH)
        cols = w[:, 2 * INNER + NH * X_ROWS:].rearrange("p (k r) -> p k r", k=NH)
        w_dt = c.sb("m_w_dt", [X_ROWS, INNER])
        w_out = c.sb("m_w_out", [P, NH, DIM])
        pad = c.sb("m_pad", [P, NH, TAPS - 1 + SEQ])
        zs = c.sb("m_zs", [P, NH, BATCH, SEQ])
        cv = c.sb("m_cv", [P, NH, BATCH, SEQ])
        xc = c.sb("m_xc", [P, NH, BATCH, SEQ])
        delta = c.sb("m_delta", [P, NH, BATCH, SEQ])
        du = c.sb("m_du", [P, NH, BATCH, SEQ])
        bcp = c.sb("m_bcp", [6 * STATE, BATCH, SEQ], BF16)
        bcq = c.sb("m_bcq", [6 * STATE, SEQ], BF16)
        bcr = c.sb("m_bcr", [6 * STATE, SEQ])
        dts = c.sb("m_dts", [X_ROWS, SEQ])
        a_pos = c.sb("m_a_pos", [P, NH, STATE])
        neg_a = c.sb("m_neg_a", [P, 2, NH * STATE])
        b_sb = c.sb("m_b_sb", [P, 4, SEQ])
        decay_more = c.sb("m_decay_more", [P, 2, SEQ])
        decay = (decay_xn[:, 0, :], decay_xn[:, 1, :], decay_more[:, 0, :], decay_more[:, 1, :])
        drive = c.sb("m_drive", [P, 2, SEQ])
        state = c.sb("m_state", [P, 2, SEQ])
        prod = c.sb("m_prod", [P, 2, SEQ])
        y = c.ps("m_y", [P, NH, SEQ])
        p_c = c.ps("m_p_c", [P, SEQ])
        p_b = c.ps("m_p_b", [P, HALF])
        aside = c.ps("m_aside", [P, HALF])
        block = st.enter_context(nc.Block())
        UNITS = 2 * STATE
        PRE = 14
        PE_AT = (5, 6, 7, 8, 9, 10, 11, 12, 14, 17, 20, 21, 22, 23)
        LAG = 4
        B_LEAD = 4
        BIAS_COL, DT_COL, A_COL, D_COL = TAPS, TAPS + 1, TAPS + 2, COLS - 1
        cut = lambda n: slice(n * HALF, (n + 1) * HALF)

        def passes(e, first, one):
            first()
            one(0, 0, (0, 1), None)
            with e.Fori(0, LAYERS - 1) as l:
                one(l, 1, (l + 1, 0), (l, 0))
                one(l + 1, 0, (l + 1, 1), (l, 1))
            one(LAYERS - 1, 1, None, (LAYERS - 1, 0))

        @block.sync
        def _(sp):
            def weights(l):
                sp.dma_start(w[:, :], d["mamba_w"][bass.ds(l, 1)].rearrange("o p f -> (o p) f")).then_inc(s["w_loaded"], 16)
                sp.dma_start(w_dt[X_ROWS - RANK:X_ROWS, :], d["mamba_w_dt"][bass.ds(l, 1)].rearrange("o r f -> (o r) f")).then_inc(s["w_loaded"], 16)

            def out_weights(l):
                sp.dma_start(w_out[:, :, :], d["mamba_w_out"][bass.ds(l, 1)].rearrange("o p k f -> (o p) k f")).then_inc(s["wo_loaded"], 16)

            weights(0)
            sp.dma_start(sel[:, :, :], d["select"]).then_inc(s["sel_loaded"], 16)
            out_weights(0)
            with sp.Fori(0, LAYERS - 1) as l:
                sp.wait_ge(s["xd_done"], l * BATCH + 2)
                sp.sem_inc(s["sp_begun"], 1)
                weights(l + 1)
                sp.wait_ge(s["u_done"], (l * BATCH + 2) * 2 + 3)
                sp.sem_inc(s["sp_begun"], 1)
                out_weights(l + 1)

        @block.tensor
        def _(pe):
            def prepare(l, b, i):
                K = l * BATCH + b
                if i == 0:
                    pe.wait_ge(s["w_loaded"], l * 32 + 32)
                    pe.wait_ge(s["u_done"], K * 2 + 1)
                pe.wait_ge(s["pre_read"], K * PRE + (i + 1))
                if i < 8:
                    m, n = i // 2, i % 2
                    mm = pe.matmul(aside[:, :], w_in[:, m * P:(m + 1) * P], u[:, b * SEQ + n * HALF:b * SEQ + (n + 1) * HALF],
                                   start=True, stop=True)
                elif i < 10:
                    n = i - 8
                    pe.wait_ge(s["xc_done"], K + 1)
                    for k in range(NH):
                        mm = pe.matmul(aside[0:X_ROWS, :], w_x[:, k, :], xc[:, k, b, cut(n)], start=(k == 0), stop=(k == NH - 1))
                else:
                    h, n = (i - 10) % 2, (i - 10) // 2
                    pe.wait_ge(s["bc0"], K * 2 + 2)
                    mm = pe.matmul(aside[:, :], w_dt[X_ROWS - RANK:X_ROWS, h * P:(h + 1) * P], dts[X_ROWS - RANK:X_ROWS, cut(n)],
                                   start=True, stop=True)
                mm.then_inc(s["pre_ready"], 1)

            def output(l, b, n, prepared):
                K = l * BATCH + b
                if n == 0:
                    pe.wait_ge(s["yg_done"], K * NH + 4)
                    pe.wait_ge(s["wo_loaded"], l * 16 + 16)
                    pe.wait_ge(s["pre_read"], prepared * PRE + 1)
                pe.wait_ge(s["u_done"], K * 2 + (n + 3))
                for k in range(NH):
                    mm = pe.matmul(aside[:, :], w_out[:, k, :], cv[:, k, b, cut(n)], start=(k == 0), stop=(k == NH - 1))
                mm.then_inc(s["out_ready"], 1)

            def b_row(K, si, b, n):
                if si == 0 and n == 0:
                    pe.wait_ge(s["bc_ready"], K * 2 + 2)
                pe.wait_ge(s["b_copied"], (K * STATE + si) * 2 + (n + 1))
                pe.matmul(p_b[:, :], sel[:, si, :], bcp[:, b, cut(n)], start=True, stop=True).then_inc(s["b_ready"], 1)

            def c_rows(K, si, b):
                pe.wait_ge(s["prod_done"], (K * STATE + si) * 2 + 2)
                for n in range(2):
                    mm = pe.matmul(p_c[:, cut(n)], sel[:, STATE + si, :], bcp[:, b, cut(n)], start=True, stop=True)
                mm.then_inc(s["c_ready"], 1)

            def start_y(K, b, h):
                pe.wait_ge(s["xd_done"], K + 1)
                pe.wait_ge(s["yg_done"], K * NH + (h + 1))
                for n in range(2):
                    pe.matmul(y[:, h, cut(n)], ident[:, :], cv[:, h, b, cut(n)], start=True, stop=True,
                              skip_group_check=True)

            def add_y(U, h):
                pe.wait_ge(s["prod_done"], U + 3)
                for n in range(2):
                    mm = pe.matmul(y[:, h, cut(n)], ident[:, :], prod[:, h, cut(n)], start=False, stop=True, skip_group_check=True)
                mm.then_inc(s["y_done"], 1)

            def first():
                for i in range(PRE):
                    prepare(0, 0, i)
                for q in range(B_LEAD):
                    b_row(0, q // 2, 0, q % 2)

            def one(l, b, following, before):
                K = l * BATCH + b
                for p in range(UNITS):
                    si, h = p // 2, p % 2
                    if h == 0:
                        c_rows(K, si, b)
                    if before or p > 0:
                        add_y(K * UNITS + (p - 1), 1 - h)
                    if p < NH:
                        start_y(K, b, p)
                    q = p + B_LEAD
                    if q < UNITS:
                        b_row(K, q // 2, b, q % 2)
                    elif following:
                        b_row(K + 1, (q - UNITS) // 2, following[1], q % 2)
                    if before and p in (2, 3):
                        output(before[0], before[1], p - 2, K + 1)
                    if following:
                        for i, at in enumerate(PE_AT):
                            if p == at:
                                prepare(following[0], following[1], i)

            pe.sem_inc(s["y_done"], 2)
            pe.wait_ge(s["sel_loaded"], 16)
            passes(pe, first, one)
            K = LAYERS * BATCH - 1
            add_y(K * UNITS + UNITS - 1, 1)
            for n in range(2):
                output(LAYERS - 1, 1, n, K + 1)

        @block.scalar
        def _(act):
            def read(l, b, i):
                K = l * BATCH + b
                act.wait_ge(s["pre_ready"], K * PRE + (i + 1))
                if i < 4:
                    m, n = i // 2, i % 2
                    at = TAPS - 1 + n * HALF
                    act.activation(pad[:, m, at:at + HALF], aside[:, :], ACT.Copy).then_inc(s["pre_read"], 1)
                    if n == 1:
                        act.wait_ge(s["pad_zero"], 1)
                        act.wait_ge(s["pre_read"], K * PRE + (i + 2))
                        act.activation(cv[:, m, b, :], pad[:, m, 0:SEQ], ACT.Identity,
                                       scale=cols[:, m, 0:1], bias=cols[:, m, BIAS_COL:BIAS_COL + 1]).then_inc(s["tap0"], 1)
                elif i < 8:
                    m, n = (i - 4) // 2, i % 2
                    act.activation(zs[:, m, b, cut(n)], aside[:, :], ACT.Copy).then_inc(s["pre_read"], 1)
                elif i < 10:
                    n = i - 8
                    act.activation(dts[X_ROWS - RANK:X_ROWS, cut(n)], aside[X_ROWS - RANK:X_ROWS, :], ACT.Copy)
                    act.activation(bcp[:, b, cut(n)], aside[0:6 * STATE, :], ACT.Copy).then_inc(s["bc0"], 1)
                else:
                    h, n = (i - 10) % 2, (i - 10) // 2
                    bias = cols[:, h, DT_COL:DT_COL + 1]
                    act.activation(cv[:, h, b, cut(n)], aside[:, :], ACT.Identity, bias=bias)
                    act.activation(delta[:, h, b, cut(n)], aside[:, :], ACT.Abs, bias=bias).then_inc(s["pre_read"], 1)

            def gates(l, b, K):
                act.wait_ge(s["pre_read"], K * PRE + 9)
                act.activation(zs[:, :, b, :], zs[:, :, b, :], ACT.Silu).then_inc(s["zs_done"], 1)

            def rest(l, b, p):
                K = l * BATCH + b
                if p == 17:
                    act.wait_ge(s["taps"], K * 6 + 6)
                    act.activation(xc[:, :, b, :], cv[:, :, b, :], ACT.Silu).then_inc(s["xc_done"], 1)
                if p == 23:
                    act.wait_ge(s["pre_read"], K * PRE + 11)
                    act.activation(bcq[:, :], bcr[:, :], ACT.Copy).then_inc(s["bc1"], 1)
                if p == 25 and b == 0:
                    act.activation(a_pos[:, :, :], cols[:, :, A_COL:A_COL + STATE], ACT.Exp).then_inc(s["a_exp"], 1)
                if p == 28:
                    act.wait_ge(s["pre_read"], K * PRE + (PRE + 1))
                    act.activation(delta[:, :, b, :], delta[:, :, b, :], ACT.Exp, scale=-1.0).then_inc(s["dl_exp"], 1)
                if p == 29:
                    act.wait_ge(s["dl_exp"], K + 1)
                    act.activation(delta[:, :, b, :], delta[:, :, b, :], ACT.Ln, bias=1.0).then_inc(s["dl_ln"], 1)
                if p == 30:
                    act.wait_ge(s["delta"], K + 1)
                    for h in range(NH):
                        x_d = act.activation(cv[:, h, b, :], xc[:, h, b, :], ACT.Copy, scale=cols[:, h, D_COL:D_COL + 1])
                    x_d.then_inc(s["xd_done"], 1)

            def copy_b(K, si, n):
                S = K * STATE + si
                act.wait_ge(s["b_ready"], S * 2 + (n + 1))
                act.wait_ge(s["drive_done"], S * 2 + 1)
                act.sem_inc(s["act_begun"], 1)
                act.activation(b_sb[:, si % 4, cut(n)], p_b[:, :], ACT.Copy).then_inc(s["b_copied"], 1)

            def first():
                for p in range(UNITS):
                    for i, at in enumerate(PE_AT):
                        if p == at + LAG:
                            read(0, 0, i)
                    rest(0, 0, p)

            def one(l, b, following, before):
                K = l * BATCH + b
                for p in range(UNITS):
                    si, h = p // 2, p % 2
                    if p == 0:
                        act.wait_ge(s["delta"], K + 1)
                        act.wait_ge(s["a_neg"], l + 1)
                    act.wait_ge(s["scan_done"], K * UNITS + (p + 1))
                    act.sem_inc(s["act_begun"], 1)
                    act.activation(decay[p % 4], delta[:, h, b, :], ACT.Exp,
                                   scale=neg_a[:, bass.ds(l % 2, 1), h * STATE + si:h * STATE + si + 1].rearrange("p o a -> p (o a)")).then_inc(s["exp_done"], 1)
                    copy_b(K, si, h)
                    if before and p in (6, 7):
                        pK, n = before[0] * BATCH + before[1], p - 6
                        act.wait_ge(s["out_ready"], pK * 2 + (n + 1))
                        act.sem_inc(s["act_begun"], 1)
                        at = before[1] * SEQ + n * HALF
                        act.activation(u[:, at:at + HALF], aside[:, :], ACT.Copy).then_inc(s["u_done"], 1)
                    if following:
                        for i, at in enumerate(PE_AT):
                            if p == at + LAG:
                                read(following[0], following[1], i)
                        rest(following[0], following[1], p)
                    if p == 17:
                        gates(l, b, K)

            act.sem_inc(s["exp_done"], 1)
            act.sem_inc(s["u_done"], 3)
            act.sem_inc(s["b_copied"], 1)
            act.sem_inc(s["pre_read"], 1)
            passes(act, first, one)
            K = LAYERS * BATCH - 1
            for n in range(2):
                act.wait_ge(s["out_ready"], K * 2 + (n + 1))
                act.activation(u[:, SEQ + n * HALF:SEQ + (n + 1) * HALF], aside[:, :], ACT.Copy).then_inc(s["u_done"], 1)

        @block.gpsimd
        def _(pool):
            def first():
                pool.memset(pad[:, :, 0:TAPS - 1], 0.0).then_inc(s["pad_zero"], 1)
                pool.sem_inc(s["drive_done"], 7)

            def one(l, b, following, before):
                K = l * BATCH + b
                pool.wait_ge(s["du_done"], K + 1)
                pool.sem_inc(s["begun"], 1)
                for p in range(UNITS):
                    si, h = p // 2, p % 2
                    if h == 0:
                        pool.wait_ge(s["b_copied"], (K * STATE + si) * 2 + 3)
                    pool.wait_ge(s["scan_done"], K * UNITS + (p + 3))
                    pool.sem_inc(s["begun"], 1)
                    pool.tensor_tensor(drive[:, h, :], du[:, h, b, :], b_sb[:, si % 4, :], ALU.mult).then_inc(s["drive_done"], 1)

            passes(pool, first, one)

        @block.vector
        def _(dve):
            def prepare(l, b, p):
                K = l * BATCH + b
                if 8 <= p < 14:
                    h, j = (p - 8) // 3, (p - 8) % 3 + 1
                    if j == 1:
                        dve.wait_ge(s["tap0"], K * NH + (h + 1))
                    else:
                        dve.wait_ge(s["taps"], K * 6 + (3 * h + j - 1))
                    dve.scalar_tensor_tensor(out=cv[:, h, b, :], in0=pad[:, h, j:j + SEQ], scalar=cols[:, h, j:j + 1], in1=cv[:, h, b, :],
                                             op0=ALU.mult, op1=ALU.add).then_inc(s["taps"], 1)
                if p in (16, 19):
                    n = (p - 16) // 3
                    dve.wait_ge(s["bc0"], K * 2 + (n + 1))
                    dve.tensor_tensor(bcr[:, cut(n)], aside[0:6 * STATE, :], bcp[:, b, cut(n)], ALU.subtract).then_inc(s["pre_read"], 1)
                if p == 22:
                    dve.wait_ge(s["bc1"], K + 1)
                    dve.tensor_copy(bcp[32:64, b, :], bcq[32:64, :]).then_inc(s["bc_ready"], 1)
                    dve.tensor_tensor(bcp[64:96, b, :], bcr[64:96, :], bcq[64:96, :], ALU.subtract).then_inc(s["bc_ready"], 1)
                if p == 24 and b == 0:
                    dve.wait_ge(s["a_exp"], l + 1)
                    dve.tensor_scalar(neg_a[:, bass.ds(l % 2, 1), :].rearrange("p o a -> p (o a)"),
                                      a_pos[:, :, :].rearrange("p h a -> p (h a)"), -1.0, None, ALU.mult).then_inc(s["a_neg"], 1)
                if p == 27:
                    dve.wait_ge(s["dl_ln"], K + 1)
                    dve.scalar_tensor_tensor(out=delta[:, :, b, :], in0=cv[:, :, b, :], scalar=0.0, in1=delta[:, :, b, :],
                                             op0=ALU.max, op1=ALU.add).then_inc(s["delta"], 1)
                if p == 28:
                    dve.wait_ge(s["delta"], K + 1)
                    dve.tensor_tensor(du[:, :, b, :], delta[:, :, b, :], xc[:, :, b, :], ALU.mult).then_inc(s["du_done"], 1)

            def gate_y(l, b, h):
                K = l * BATCH + b
                dve.wait_ge(s["y_done"], K * UNITS + (UNITS + 1 + h))
                dve.wait_ge(s["zs_done"], K + 1)
                dve.tensor_tensor(cv[:, h, b, :], y[:, h, :], zs[:, h, b, :], ALU.mult).then_inc(s["yg_done"], 1)

            def first():
                for p in range(UNITS):
                    prepare(0, 0, p)

            def one(l, b, following, before):
                K = l * BATCH + b
                for p in range(UNITS):
                    U, h = K * UNITS + p, p % 2
                    dve.wait_ge(s["exp_done"], U + 2)
                    dve.wait_ge(s["drive_done"], U + 8)
                    dve.wait_ge(s["prod_done"], U + 1)
                    dve.tensor_tensor_scan(state[:, h, :], decay[p % 4], drive[:, h, :], 0.0, ALU.mult, ALU.add).then_inc(s["scan_done"], 1)
                    if before and p < NH:
                        gate_y(before[0], before[1], p)
                    dve.wait_ge(s["scan_done"], U + 5)
                    dve.wait_ge(s["c_ready"], K * STATE + (p // 2 + 1))
                    dve.wait_ge(s["y_done"], U + 1)
                    dve.tensor_tensor(prod[:, h, :], state[:, h, :], p_c[:, :], ALU.mult).then_inc(s["prod_done"], 1)
                    if following:
                        prepare(following[0], following[1], p)

            dve.sem_inc(s["scan_done"], 4)
            dve.sem_inc(s["prod_done"], 2)
            dve.sem_inc(s["yg_done"], 2)
            passes(dve, first, one)
            for h in range(NH):
                gate_y(LAYERS - 1, 1, h)


def finish(nc, whole, d, ident, x, gate, u, out):
    turned, mixed, added, stored = (whole.sem(f"f_{n}") for n in ("turned", "mixed", "added", "stored"))
    out = out.rearrange("b (t p) c -> p (b t) c", p=P)
    with ExitStack() as st:
        c = Core(nc, st)
        res = c.sb("f_res", [P, TILES, DIM])
        pt = c.ps("f_pt", [P, TILES, P])
        block = st.enter_context(nc.Block())

        @block.tensor
        def _(pe):
            for t in range(TILES):
                pe.transpose(pt[:, t, :], u[:, t * P:(t + 1) * P], ident[:, :]).then_inc(turned, 1)

        @block.vector
        def _(dve):
            for n in range(TILES // 4):
                tt = slice(4 * n, 4 * n + 4)
                dve.wait_ge(turned, 4 * n + 4)
                dve.tensor_tensor(res[:, tt, :], pt[:, tt, :], gate[:, tt, :], ALU.mult).then_inc(mixed, 1)
                dve.wait_ge(mixed, n + 1)
                dve.tensor_tensor(res[:, tt, :], res[:, tt, :], x[:, tt, :], ALU.add).then_inc(added, 1)

        @block.sync
        def _(sp):
            for n in range(TILES // 4):
                tt = slice(4 * n, 4 * n + 4)
                sp.wait_ge(added, n + 1)
                sp.dma_start(out[:, tt, :], res[:, tt, :]).then_inc(stored, 16)
            sp.wait_ge(stored, 16 * (TILES // 4))


def program(nc, d, out, debug=None):
    with ExitStack() as stack:
        whole = Core(nc, stack)
        dram = lambda name, shape, dt=F32: nc.dram_tensor(name, shape, dt, kind="Internal").ap()
        parts_scr = dram("parts_scr", (2, 3, BATCH, DIM, SEQ), BF16)
        bias_scr = dram("bias_scr", (3, GROUPS, HEADS_PER_GROUP, BIAS_R, SEQ), BF16)
        x = whole.sb("x", [P, TILES, DIM])
        xn = whole.sb("xn", [P, TILES, DIM])
        xnT = whole.sb("xnT", [P, TOK])
        ident = whole.sb("ident", [P, P])

        layer_norm(nc, whole, "a", x, xn, xnT, ident,
                   [(x[:, :, :], d["x"].rearrange("(t p) c -> p t c", p=P)), (ident[:, :], d["ident"])])
        with ExitStack() as st:
            c = Core(nc, st)
            o_all = c.sb("o_all", [P, GROUPS, SEQ])
            with ExitStack() as st2:
                c = Core(nc, st2)
                v_all = c.sb("v_all", [P, GROUPS, QT, 32])
                tri_all = c.sb("tri_all", [P, HEADS, P])
                s8 = c.sb("s8", [P, HEADS])
                w_ffn = c.sb("w_ffn", [P, 3, HIDDEN])
                stored = whole.sem("stored")
                project_qkv(nc, whole, d, xnT, ident, v_all, tri_all, s8, w_ffn, parts_scr, bias_scr, stored)
                attention(nc, whole, d, ident, v_all, tri_all, s8, parts_scr, bias_scr, o_all, xnT, w_ffn, xn, stored)
            if debug == "attention":
                dump(nc, whole, out, o_all[:, 0, :])
                return
            project_and_mix(nc, whole, d, ident, o_all, x, xn)
        layer_norm(nc, whole, "n", x, xn, xnT, ident, [])
        if debug == "ffn":
            dump(nc, whole, out, x[:, :, :])
            return
        gate = whole.sb("gate", [P, TILES, DIM])
        experts(nc, whole, d, ident, xn, xnT, gate)
        if debug == "experts":
            dump(nc, whole, out, gate[:, :, :])
            return
        mamba(nc, whole, d, ident, xnT, xn[:, :, :].rearrange("p t c -> p (t c)").rearrange("p (h t) -> p h t", h=2))
        if debug == "mamba":
            dump(nc, whole, out, xnT[:, :])
            return
        finish(nc, whole, d, ident, x, gate, xnT, out)


def dump(nc, whole, out, src):
    done = whole.sem("dumped")
    with nc.Block() as block:
        @block.sync
        def _(sp):
            sp.dma_start(out, src).then_inc(done, 16)
            sp.wait_ge(done, 16)


def layout(a):
    import numpy as np

    f32 = np.float32
    w = np.asarray(a["L0_attn_qkv_w"])
    swap = np.arange(DIM).reshape(HEADS, 2, HEAD_DIM // 2)[:, ::-1].reshape(DIM)
    q, k, v = w[0:DIM], w[DIM:2 * DIM], w[2 * DIM:]
    m = {"x": np.asarray(a["L0_attn_x"]).reshape(TOK, DIM),
         "w_qkv": np.ascontiguousarray(np.stack([q, q[swap], k, k[swap], v]).transpose(2, 0, 1)),
         "slopes": np.asarray(a["L0_attn_slopes"]),
         "slopes_rows": np.ascontiguousarray(np.repeat(np.asarray(a["L0_attn_slopes"]).reshape(2, 8), BIAS_R, axis=1).T)}
    inv = f32(1.0) / np.power(f32(10000.0), np.arange(0, HEAD_DIM, 2, dtype=f32) / f32(HEAD_DIM)).astype(f32)
    ang = (np.arange(SEQ, dtype=f32)[:, None] * inv[None, :]).astype(f32).astype(np.float64)
    cos = np.tile(np.cos(ang).T, (2 * HEADS, 1))
    sin = np.tile(np.concatenate([-np.sin(ang).T, np.sin(ang).T]), (HEADS, 1))
    scale = HEAD_DIM ** -0.5
    m["rotation"] = np.ascontiguousarray(np.stack([cos * scale, sin * scale, cos, sin], axis=1).astype(f32))
    m["ident"] = np.eye(P, dtype=f32)

    bf = mybir.dt.np(BF16)
    m["ident_bf16"] = np.eye(P).astype(bf)
    i = np.arange(P)
    m["tri_qk"] = np.minimum(i[None, :] - i[:, None], 0).astype(f32)
    m["tri_kq"] = np.ascontiguousarray(m["tri_qk"].T)
    pos = np.arange(SEQ)
    rows_k, rows_q = [], []
    for b in range(1, QT):
        rows_k.append(np.where(pos < P * b, pos - P * b, 0))
        rows_q.append(pos // P == b)
    for b in range(1, QT):
        rows_k.append(np.where(pos < P * b, -1, 0))
        rows_q.append(np.where(pos // P == b, pos % P, 0))
    m["bias_keys"] = np.tile(np.stack(rows_k).astype(f32), (8, 1))
    m["bias_queries"] = np.ascontiguousarray(np.repeat(np.tile(np.stack(rows_q).astype(f32), (3, 1))[:, None, :], HEADS_PER_GROUP, axis=1)).astype(bf)
    m["ones_rows"] = np.ones((3, HEADS_PER_GROUP, SEQ), bf)
    down = np.asarray(a["L0_ffn_w_down"]).T.reshape(HIDDEN // P, P, DIM).transpose(1, 0, 2).reshape(P, HIDDEN)
    m["w_ffn"] = np.ascontiguousarray(np.stack([np.asarray(a["L0_ffn_w_gate"]).T, np.asarray(a["L0_ffn_w_up"]).T, down], axis=1))
    m["w_proj"] = np.ascontiguousarray(np.asarray(a["L0_attn_proj_w"]).T)
    m["proj_b"] = np.asarray(a["L0_attn_proj_b"])
    g = {n: np.asarray(a["L1_ffn_" + n]) for n in ("sW1", "sb1", "sW2", "sb2", "rW1", "rb1", "rW2", "rb2", "gW", "gb")}
    m["experts_w1"] = np.concatenate([g["rW1"], g["sW1"].reshape(DIM, 2, EXP_HID).transpose(1, 0, 2)])
    w2 = np.concatenate([g["rW2"], g["sW2"].reshape(2, EXP_HID, DIM)])
    m["experts_w2"] = np.ascontiguousarray(w2.reshape(ALL_EXPERTS, 2, P, DIM).transpose(0, 2, 1, 3))
    b1 = np.concatenate([g["rb1"], g["sb1"].reshape(2, EXP_HID)])
    m["experts_b1"] = np.ascontiguousarray(b1.reshape(ALL_EXPERTS, 2, P).transpose(2, 0, 1))
    m["experts_b2"] = np.concatenate([g["rb2"], g["sb2"], np.zeros((1, DIM), f32)])
    m["gate_w"], m["gate_b"] = g["gW"], g["gb"]
    restart = np.ones((P, TILES, EXPERTS), f32)
    restart[:, :, 0] = 0
    m["restart"] = restart
    t = {n: np.asarray(a["L1_attn_" + n]) for n in ("in_proj_w", "conv_w", "conv_b", "x_proj_w", "dt_proj_w", "dt_proj_b", "A_log", "D", "out_proj_w")}
    halves = lambda v: v.reshape(LAYERS, NH, P, -1).transpose(0, 2, 1, 3)
    w_x = t["x_proj_w"].transpose(0, 2, 1)
    bc, dt = w_x[:, :, RANK:], w_x[:, :, :RANK]
    m["mamba_w"] = np.ascontiguousarray(np.concatenate(
        [t["in_proj_w"].transpose(0, 2, 1)]
        + [halves(np.concatenate([bc, bc, bc, dt], axis=2)).reshape(LAYERS, P, -1)]
        + [halves(np.concatenate([t["conv_w"], t["conv_b"][:, :, None], t["dt_proj_b"][:, :, None], t["A_log"], t["D"][:, :, None]],
                                 axis=2)).reshape(LAYERS, P, -1)], axis=2))
    m["mamba_w_dt"] = np.ascontiguousarray(t["dt_proj_w"].transpose(0, 2, 1))
    m["mamba_w_out"] = np.ascontiguousarray(halves(t["out_proj_w"].transpose(0, 2, 1)))
    m["select"] = np.ascontiguousarray(np.tile(np.repeat(np.eye(2 * STATE)[:, :, None], P, axis=2), (3, 1, 1))).astype(bf)
    return m


_OUT = (BATCH, SEQ, DIM)


def kernel(**inputs):
    import concourse.bacc as bacc
    import numpy as np
    from concourse.bass_utils import run_bass_kernel_spmd

    nc = bacc.Bacc("TRN2", target_bir_lowering=False, num_devices=1)
    arrays = {f"in_{n}": np.ascontiguousarray(v) for n, v in layout(inputs).items()}
    d = {n[3:]: nc.dram_tensor(n, v.shape, mybir.dt.from_np(v.dtype), kind="ExternalInput").ap() for n, v in arrays.items()}
    out = nc.dram_tensor("out", _OUT, F32, kind="ExternalOutput").ap()
    program(nc, d, out)
    r = run_bass_kernel_spmd(nc, [arrays], core_ids=[0])
    return r.results[0]["out"]
```

```python
from contextlib import ExitStack

import concourse.bass as bass
from concourse import mybir

F32 = mybir.dt.float32
BF16 = mybir.dt.bfloat16
I32 = mybir.dt.int32
ALU = mybir.AluOpType
ACT = mybir.ActivationFunctionType
AX = mybir.AxisListType

P = 128
BATCH, SEQ, DIM = 2, 1024, 128
TOK = BATCH * SEQ
TILES = TOK // P
HALF = 512
HEADS, HEAD_DIM = 16, 8
HEADS_PER_GROUP = 4
HEAD_GROUPS = HEADS // HEADS_PER_GROUP
GROUPS = BATCH * HEAD_GROUPS
QT = SEQ // P
PAIR_ROWS = 9 * HEAD_DIM
BIAS_R = 2 * (QT - 1)
BIAS_ROWS = 3 * BIAS_R
MAX_ROW = PAIR_ROWS + BIAS_ROWS
PACK_ROWS = MAX_ROW + 3
RING = 4
MAX_BIAS = 8.0
LN_EPS = 1e-5
HIDDEN = 384
QSCALE = 1.0 / 127.0
EXPERTS = 15
TOP_K = 3


STORES = 3 * BATCH * (2 + 2)


class Core:

    def __init__(self, nc, stack):
        self.nc, self.stack = nc, stack

    def sb(self, name, shape, dt=F32):
        return self.stack.enter_context(self.nc.sbuf_tensor(name, shape, dt))

    def ps(self, name, shape, dt=F32):
        return self.stack.enter_context(self.nc.psum_tensor(name, shape, dt))

    def sem(self, name):
        return self.stack.enter_context(self.nc.semaphore(name))


def load_ahead(sp, loads):
    for dst, src, loaded in loads:
        sp.dma_start(dst, src).then_inc(loaded, 16)


def layer_norm(nc, whole, tag, x, xn, xnT, ident, loads, ahead=()):
    loaded, stats_done, mv_done, var_done = (whole.sem(f"{tag}_{n}") for n in ("loaded", "stats_done", "mv_done", "var_done"))
    rstd_done, norm_done, turned, copied = (whole.sem(f"{tag}_{n}") for n in ("rstd_done", "norm_done", "turned", "copied"))
    with ExitStack() as st:
        c = Core(nc, st)
        stats = c.sb(f"{tag}_stats", [P, TILES, 6])
        mv = c.sb(f"{tag}_mv", [P, TILES, 2])
        var = c.sb(f"{tag}_var", [P, TILES])
        power = c.sb(f"{tag}_power", [P, TILES])
        rstd = c.sb(f"{tag}_rstd", [P, TILES])
        psT = c.ps(f"{tag}_psT", [P, TOK])
        block = st.enter_context(nc.Block())

        @block.sync
        def _(sp):
            for dst, src in loads:
                sp.dma_start(dst, src).then_inc(loaded, 16)
            load_ahead(sp, ahead)

        @block.gpsimd
        def _(pool):
            pool.memset(power[:, :], -0.5).then_inc(var_done, 1)
            pool.wait_ge(var_done, 2)
            pool.tensor_tensor(rstd[:, :], var[:, :], power[:, :], ALU.pow).then_inc(rstd_done, 1)

        @block.vector
        def _(dve):
            if loads:
                dve.wait_ge(loaded, 16 * len(loads))
            for t in range(TILES):
                dve.bn_stats(stats[:, t, :], x[:, t, :]).then_inc(stats_done, 1)
            for t in range(TILES):
                dve.wait_ge(stats_done, t + 1)
                dve.bn_aggr(mv[:, t, :], stats[:, t, :]).then_inc(mv_done, 1)
            dve.wait_ge(mv_done, TILES)
            dve.tensor_scalar(var[:, :], mv[:, :, 1], LN_EPS, None, ALU.add).then_inc(var_done, 1)
            dve.wait_ge(rstd_done, 1)
            for t in range(TILES):
                dve.tensor_scalar(xn[:, t, :], x[:, t, :], mv[:, t, 0:1], rstd[:, t:t + 1],
                                  ALU.subtract, ALU.mult).then_inc(norm_done, 1)

        @block.tensor
        def _(pe):
            if loads:
                pe.wait_ge(loaded, 16 * len(loads))
            for t in range(TILES):
                pe.wait_ge(norm_done, t + 1)
                pe.transpose(psT[:, t * P:(t + 1) * P], xn[:, t, :], ident[:, :]).then_inc(turned, 1)

        @block.scalar
        def _(act):
            for n in range(TOK // HALF):
                act.wait_ge(turned, 4 * (n + 1))
                act.activation(xnT[:, n * HALF:(n + 1) * HALF], psT[:, n * HALF:(n + 1) * HALF],
                               ACT.Copy).then_inc(copied, 1)


def qkv_constants(whole, c, d):
    kb_rows = 8 * BIAS_R
    t = {"loaded": whole.sem("b_loaded"), "int_loaded": whole.sem("b_int_loaded"),
         "w": c.sb("b_w", [P, 5, P]),
         "cs": c.sb("b_cs", [P, 4, SEQ]),
         "triT": c.sb("b_triT", [P, P]), "slopes": c.sb("b_slopes", [P, HEADS]),
         "kc": c.sb("b_kc", [kb_rows, SEQ]), "ks": c.sb("b_ks", [kb_rows, 2]),
         "w_int": c.sb("b_w_int", [P, 3, HIDDEN], I32)}
    loads = [(t["w"][:, :, :], d["w_qkv"], t["loaded"]), (t["slopes"][:, :], d["slopes"].partition_broadcast(P), t["loaded"]),
             (t["kc"][:, :], d["bias_keys"], t["loaded"]), (t["ks"][:, :], d["slopes_rows"], t["loaded"]),
             (t["cs"][:, :, :], d["rotation"], t["loaded"]), (t["triT"][:, :], d["tri_kq"], t["loaded"]),
             (t["w_int"][:, :, :], d["w_ffn"], t["int_loaded"])]
    return t, loads


def project_qkv(nc, whole, d, xnT, ident, v_all, tri_all, s8, w_ffn, parts_scr, bias_scr, stored, consts):
    loaded, int_loaded = consts["loaded"], consts["int_loaded"]
    proj_done, rot_cos, rot_sin, rot_add = (whole.sem(n) for n in ("b_proj_done", "b_rot_cos", "b_rot_sin", "b_rot_add"))
    part0, rest0, part1, part2 = (whole.sem(n) for n in ("b_part0", "b_rest0", "b_part1", "b_part2"))
    v_done, v_copied, kb_full, kb_part0, kb_rest, kb_part1, kb_part2 = (
        whole.sem(n) for n in ("b_v_done", "b_v_copied", "b_kb_full", "b_kb_part0", "b_kb_rest", "b_kb_part1", "b_kb_part2"))
    tri_done, s8_done = whole.sem("b_tri_done"), whole.sem("b_s8_done")
    w_cast, w_scaled = whole.sem("b_w_cast"), whole.sem("b_w_scaled")
    with ExitStack() as st:
        c = Core(nc, st)
        kb_rows = 8 * BIAS_R
        parts = c.sb("b_parts", [P, 2, 3, TOK], BF16)
        kbp = c.sb("b_kbp", [kb_rows, 3, 2, SEQ], BF16)
        w, cs, triT, slopes, kc, ks, w_int = (consts[n] for n in ("w", "cs", "triT", "slopes", "kc", "ks", "w_int"))
        f = c.sb("b_f", [P, 2, TOK])
        sin_part = c.sb("b_sin_part", [P, 2, HALF])
        kb = c.sb("b_kb", [kb_rows, 2, SEQ])
        pq = c.ps("b_pq", [P, 2, 2, HALF])
        pv = c.ps("b_pv", [P, TILES, P])
        block = st.enter_context(nc.Block())
        N = TOK // HALF

        @block.sync
        def _(sp):
            for i, ready in enumerate((kb_part0, kb_part1, kb_part2)):
                sp.wait_ge(ready, 1)
                for hh in range(2):
                    for b in range(BATCH):
                        g0 = b * HEAD_GROUPS + 2 * hh
                        sp.dma_start(bias_scr[i, g0:g0 + 2].rearrange("g h r k -> (g h r) k"),
                                     kbp[:, i, hh, :]).then_inc(stored, 16)
            for z in range(2):
                for i, ready in enumerate((part0, part1, part2)):
                    sp.wait_ge(ready, z + 1)
                    for b in range(BATCH):
                        sp.dma_start(parts_scr[z, i, b], parts[:, z, i, b * SEQ:(b + 1) * SEQ]).then_inc(stored, 16)

        @block.tensor
        def _(pe):
            pe.wait_ge(loaded, 96)
            for s in range(2 * N):
                z, n = s // N, s % N
                if s >= 2:
                    pe.wait_ge(rot_sin, s - 1)
                for j in range(2):
                    mm = pe.matmul(pq[:, s % 2, j, :], w[:, 2 * z + j, :], xnT[:, n * HALF:(n + 1) * HALF],
                                   start=True, stop=True)
                mm.then_inc(proj_done, 1)
                for t in range(2 * s, 2 * s + 2):
                    mm = pe.matmul(pv[:, t, :], xnT[:, t * P:(t + 1) * P], w[:, 4, :], start=True, stop=True)
                mm.then_inc(v_done, 1)

        @block.vector
        def _(dve):
            dve.wait_ge(loaded, 96)
            dve.tensor_scalar(s8[:, :], slopes[:, :], MAX_BIAS, None, ALU.mult).then_inc(s8_done, 1)
            for hh in range(2):
                dve.tensor_scalar(kb[:, hh, :], kc[:, :], ks[:, hh:hh + 1], MAX_BIAS,
                                  ALU.mult, ALU.mult).then_inc(kb_full, 1)
            def rotate(s):
                z, n = s // N, s % N
                at = slice((n % 2) * HALF, (n % 2 + 1) * HALF)
                dst = f[:, z, n * HALF:(n + 1) * HALF]
                dve.wait_ge(proj_done, s + 1)
                dve.tensor_tensor(dst, pq[:, s % 2, 0, :], cs[:, 2 * z, at], ALU.mult).then_inc(rot_cos, 1)
                if s >= 2:
                    dve.wait_ge(rot_add, s - 1)
                dve.tensor_tensor(sin_part[:, s % 2, :], pq[:, s % 2, 1, :], cs[:, 2 * z + 1, at],
                                  ALU.mult).then_inc(rot_sin, 1)
                dve.wait_ge(rot_cos, s + 1)
                dve.wait_ge(rot_sin, s + 1)
                dve.tensor_tensor(dst, dst, sin_part[:, s % 2, :], ALU.add).then_inc(rot_add, 1)

            def first_rest(z):
                dve.wait_ge(part0, z + 1)
                dve.tensor_tensor(f[:, z, :], f[:, z, :], parts[:, z, 0, :], ALU.subtract).then_inc(rest0, 1)

            def last_part(z):
                dve.wait_ge(part1, z + 1)
                dve.wait_ge(rest0, z + 1)
                dve.tensor_tensor(parts[:, z, 2, :], f[:, z, :], parts[:, z, 1, :], ALU.subtract).then_inc(part2, 1)

            for s in range(N + 1):
                rotate(s)
            first_rest(0)
            for s in range(N + 1, 2 * N):
                rotate(s)
            last_part(0)
            first_rest(1)
            last_part(1)

        @block.scalar
        def _(act):
            act.wait_ge(kb_full, 2)
            act.activation(kbp[:, 0, :, :], kb[:, :, :], ACT.Copy).then_inc(kb_part0, 1)
            act.wait_ge(kb_rest, 1)
            act.activation(kbp[:, 1, :, :], kb[:, :, :], ACT.Copy).then_inc(kb_part1, 1)
            def first_part(z):
                act.wait_ge(rot_add, N * (z + 1))
                act.activation(parts[:, z, 0, :], f[:, z, :], ACT.Copy).then_inc(part0, 1)

            def second_part(z):
                act.wait_ge(rest0, z + 1)
                act.activation(parts[:, z, 1, :], f[:, z, :], ACT.Copy).then_inc(part1, 1)

            def copy_v(n):
                act.wait_ge(v_done, 2 * (n + 1))
                b, k0 = 4 * n // QT, 4 * n % QT
                act.activation(v_all[:, b * HEAD_GROUPS:(b + 1) * HEAD_GROUPS, k0:k0 + 4, :].rearrange("p g k x -> p k g x"),
                               pv[:, 4 * n:4 * n + 4, :].rearrange("p k (g x) -> p k g x", g=HEAD_GROUPS),
                               ACT.Copy).then_inc(v_copied, 1)

            copy_v(0)
            copy_v(1)
            first_part(0)
            second_part(0)
            copy_v(2)
            copy_v(3)
            first_part(1)
            second_part(1)

        @block.gpsimd
        def _(pool):
            pool.wait_ge(loaded, 96)
            pool.wait_ge(s8_done, 1)
            pool.wait_ge(kb_part0, 1)
            pool.tensor_tensor(kb[:, :, :], kb[:, :, :], kbp[:, 0, :, :], ALU.subtract).then_inc(kb_rest, 1)
            pool.wait_ge(kb_part1, 1)
            pool.tensor_tensor(kbp[:, 2, :, :], kb[:, :, :], kbp[:, 1, :, :], ALU.subtract).then_inc(kb_part2, 1)
            for h in range(HEADS):
                pool.tensor_scalar(tri_all[:, h, :], triT[:, :], s8[:, h:h + 1], None, ALU.mult).then_inc(tri_done, 1)
            pool.wait_ge(int_loaded, 16)
            pool.tensor_copy(w_ffn[:, :, :], w_int[:, :, :]).then_inc(w_cast, 1)
            pool.wait_ge(w_cast, 1)
            pool.tensor_scalar(w_ffn[:, :, :], w_ffn[:, :, :], QSCALE, None, ALU.mult).then_inc(w_scaled, 1)


def attention(nc, whole, d, ident, v_all, tri_all, s8, parts_scr, bias_scr, o_all, xnT, w_ffn, mix_gate, stored, ahead):
    names = ("pack_loaded", "ones_loaded", "scores_ready", "exp_done", "pv_done", "o_copied", "v_ready", "v_fixed",
             "maxs_ready", "maxs_free", "center_done", "max_done", "neg_done", "mp0", "mr0", "mp1", "mr1", "mp2", "m_turned",
             "m_copied", "m_stored", "w_zero", "gtri_loaded", "begun", "sp_begun",
             "gu_ready", "silu_done", "gu_read", "down_ready", "gate_done")
    s = {n: whole.sem("c_" + n) for n in names}
    with ExitStack() as st:
        c = Core(nc, st)
        qpack = c.sb("c_qpack", [PACK_ROWS, RING, HEADS_PER_GROUP, SEQ], BF16)
        kpack = c.sb("c_kpack", [PACK_ROWS, RING, HEADS_PER_GROUP, SEQ], BF16)
        probs = c.sb("c_probs", [P, 8, SEQ])
        v_cur = c.sb("c_v_cur", [P, QT, HEADS_PER_GROUP, 32])
        window = c.sb("c_window", [P, HEADS_PER_GROUP, 7 * P])
        tri = c.sb("c_tri", [P, P])
        identb = c.sb("c_identb", [P, P], BF16)
        junk = c.sb("c_junk", [P, 2, HALF], BF16)
        mx = c.sb("c_mx", [P, 32, 2])
        neg = c.sb("c_neg", [P, 32])
        negp = c.sb("c_negp", [P, 3, 32], BF16)
        neg_rows = c.sb("c_neg_rows", [96, P], BF16)
        pst = c.ps("c_pst", [P, 2, SEQ])
        pmax = c.ps("c_pmax", [P, 2, HALF])
        po = c.ps("c_po", [P, SEQ])
        block = st.enter_context(nc.Block())
        KH = HIDDEN // P
        N = TOK // HALF
        hT = probs[:, 0:2 * KH, :].rearrange("p (m b) t -> p m (b t)", m=KH)
        act_gate = probs[:, 2 * KH, :].rearrange("p (i c) -> p i c", i=2)
        pgu = pst[:, :, :].rearrange("p i (j c) -> p i j c", j=2)
        pdown = po[:, :].rearrange("p (i c) -> p i c", i=2)

        LOADS = 9 + 9 + 3
        WEIGH_AT = (5, 7)
        LEAD = 30

        def load_group(q, g, ring):
            for z, pack in enumerate((qpack, kpack)):
                for i in range(3):
                    for j in range(3):
                        src = parts_scr[z, (i, j)[z]].rearrange("b (g h d) t -> (b g) d h t", g=HEAD_GROUPS, d=HEAD_DIM)
                        r0 = HEAD_DIM * (3 * i + j)
                        src = src[bass.ds(g, 1)].rearrange("o d h t -> (o d) h t")
                        dst = pack[r0:r0 + HEAD_DIM, bass.ds(ring, 1)].rearrange("d o h t -> d (o h) t")
                        q.dma_start(dst, src).then_inc(s["pack_loaded"], 16)
            for i in range(3):
                r0 = PAIR_ROWS + BIAS_R * i
                src = bias_scr[i][bass.ds(g, 1)].rearrange("o h r k -> r (o h) k")
                q.dma_start(kpack[r0:r0 + BIAS_R, bass.ds(ring, 1)].rearrange("r o h k -> r (o h) k"),
                            src).then_inc(s["pack_loaded"], 16)
            q.wait_ge(s["pack_loaded"], (g + 1) * (16 * LOADS))
            q.sem_inc(s["sp_begun"], 1)

        @block.sync
        def _(sp):
            sp.sem_inc(s["m_stored"], 16)
            sp.dma_start(tri[:, :], d["tri_qk"]).then_inc(s["gtri_loaded"], 16)
            sp.dma_start(identb[:, :], d["ident_bf16"]).then_inc(s["gtri_loaded"], 16)
            sp.wait_ge(stored, 16 * STORES)
            for r in range(RING):
                sp.dma_start(qpack[PAIR_ROWS:MAX_ROW, r], d["bias_queries"]).then_inc(s["ones_loaded"], 16)
                sp.dma_start(kpack[MAX_ROW:PACK_ROWS, r], d["ones_rows"]).then_inc(s["ones_loaded"], 16)
            for g in range(RING):
                load_group(sp, g, g)
            load_ahead(sp, ahead)

            def store_max(g):
                sp.wait_ge(s["m_copied"], g + 1)
                sp.sem_inc(s["sp_begun"], 1)
                for i in range(3):
                    dst = qpack[MAX_ROW + i:MAX_ROW + i + 1, bass.ds(g % RING, 1)].rearrange("r o h (t q) -> r (o h t) q", q=P)
                    sp.dma_start(dst, neg_rows[32 * i:32 * i + 32, :]).then_inc(s["m_stored"], 16)

            store_max(0)
            with sp.Fori(0, GROUPS - RING) as g:
                store_max(g + 1)
                sp.wait_ge(s["pv_done"], (g + 1) * QT + 1)
                sp.sem_inc(s["sp_begun"], 1)
                load_group(sp, g + RING, g)
            with sp.Fori(GROUPS - RING, GROUPS - 1) as g:
                store_max(g + 1)
            sp.wait_ge(s["m_stored"], 48 * GROUPS + 16)

        @block.gpsimd
        def _(pool):
            pool.memset(window[:, :, :], 0.0).then_inc(s["w_zero"], 1)
            pool.memset(v_cur[:, :, :, :], 0.0).then_inc(s["v_fixed"], 1)
            pool.wait_ge(s["v_fixed"], 1)
            pool.memset(v_cur[:, :, :, HEAD_DIM:HEAD_DIM + 1], 1.0).then_inc(s["v_fixed"], 1)
            pool.wait_ge(s["v_fixed"], 2)
            with pool.Fori(0, GROUPS) as g:
                pool.wait_ge(s["pv_done"], g * QT + 1)
                pool.tensor_copy(v_cur[:, :, :, 0:HEAD_DIM],
                                 v_all[:, bass.ds(g, 1)].rearrange("p o k (h x) -> p (o k) h x", x=HEAD_DIM)).then_inc(s["v_ready"], 1)

        def max_tiles(pe, g, n0, n1, first):
            for n in range(n0, n1):
                h, qt, half = n // 16, n // 2 % 8, n % 2
                if not (first and n < 2):
                    pe.wait_ge(s["maxs_free"], g * 65 + max(n - 1, 0))
                ring = g % RING
                q = qpack[0:MAX_ROW, bass.ds(ring, 1), h, qt * P:(qt + 1) * P].rearrange("r o q -> r (o q)")
                k = kpack[0:MAX_ROW, bass.ds(ring, 1), h, half * HALF:(half + 1) * HALF].rearrange("r o k -> r (o k)")
                pe.matmul(pmax[:, n % 2, :], q, k, start=True, stop=True).then_inc(s["maxs_ready"], 1)

        def turn_max(pe, g):
            pe.wait_ge(s["mp2"], g + 1)
            pe.transpose(pmax[0:96, 0, 0:P // 2].bitcast(BF16), negp[:, :, :].rearrange("p i x -> p (i x)"),
                         identb[:, :]).then_inc(s["m_turned"], 1)

        def second_pass(pe, g, with_next):
            ring = g % RING
            pe.wait_ge(s["m_stored"], (g + 1) * 48 + 16)
            if with_next:
                pe.wait_ge(s["pack_loaded"], (g + 2) * (16 * LOADS))
            for j in range(32):
                kt, h = j // 4, j % 4
                pe.wait_ge(s["exp_done"], g * 32 + (j + 1))
                k = kpack[:, bass.ds(ring, 1), h, kt * P:(kt + 1) * P].rearrange("r o k -> r (o k)")
                n0, n1 = (64 * j // LEAD, 64 * (j + 1) // LEAD) if with_next and j < LEAD else (0, 0)
                for half in range(2):
                    q = qpack[:, bass.ds(ring, 1), h, half * HALF:(half + 1) * HALF].rearrange("r o q -> r (o q)")
                    diag = kt // 4 == half
                    mm = pe.matmul(pst[:, j % 2, half * HALF:(half + 1) * HALF], k, q, start=True, stop=True,
                                   skip_group_check=diag)
                    if diag:
                        t = tri_all[:, bass.ds((g % HEAD_GROUPS) * HEADS_PER_GROUP + h, 1), :].rearrange("p o q -> p (o q)")
                        mm = pe.matmul(pst[:, j % 2, kt * P:(kt + 1) * P], ident[:, :], t, start=False, stop=True,
                                       skip_group_check=True)
                    if half == 0:
                        max_tiles(pe, g + 1, n0, min(n0 + 1, n1), False)
                mm.then_inc(s["scores_ready"], 1)
                max_tiles(pe, g + 1, n0 + 1, n1, False)
                for half, at in enumerate(WEIGH_AT):
                    if j >= at and (j - at) % 4 == 0:
                        weigh(pe, g, (j - at) // 4, half)
                if with_next and j == 31:
                    turn_max(pe, g + 1)
            for half in range(2):
                if 4 * (QT - 1) + WEIGH_AT[half] >= 4 * QT:
                    weigh(pe, g, QT - 1, half)

        def weigh(pe, g, kt, half):
            if half == 0:
                pe.wait_ge(s["exp_done"], g * 32 + (4 * kt + 6))
            if kt == 0 and half == 0:
                pe.wait_ge(s["v_ready"], g + 1)
                pe.wait_ge(s["o_copied"], g + 1)
            for h in range(HEADS_PER_GROUP):
                mm = pe.matmul(po[32 * h:32 * h + 32, half * HALF:(half + 1) * HALF], v_cur[:, kt, h, :],
                               probs[:, 4 * (kt % 2) + h, half * HALF:(half + 1) * HALF],
                               start=(kt == 0), stop=(kt == QT - 1))
            if half == 1:
                mm.then_inc(s["pv_done"], 1)

        @block.tensor
        def _(pe):
            pe.sem_inc(s["pv_done"], 1)
            for r in range(KH * N):
                n, m = r // KH, r % KH
                if r >= 2:
                    pe.wait_ge(s["gu_read"], r - 1)
                for j in range(2):
                    mm = pe.matmul(pgu[:, r % 2, j, :], w_ffn[:, j, m * P:(m + 1) * P], xnT[:, n * HALF:(n + 1) * HALF],
                                   start=True, stop=True)
                mm.then_inc(s["gu_ready"], 1)
            pe.wait_ge(s["gtri_loaded"], 32)
            pe.wait_ge(s["ones_loaded"], 16 * 2 * RING)
            pe.wait_ge(s["pack_loaded"], 16 * LOADS)
            for t in range(TILES):
                n = t // 4
                if t % 4 == 0:
                    pe.wait_ge(s["gu_read"], KH * (n + 1))
                    if n >= 2:
                        pe.wait_ge(s["gate_done"], n - 1)
                max_tiles(pe, 0, 4 * t, 4 * t + 4, True)
                for k in range(KH):
                    mm = pe.matmul(pdown[:, n % 2, t % 4 * P:(t % 4 + 1) * P], hT[:, k, t * P:(t + 1) * P],
                                   w_ffn[:, 2, k * P:(k + 1) * P], start=(k == 0), stop=(k == KH - 1))
                if t % 4 == 3:
                    mm.then_inc(s["down_ready"], 1)
            turn_max(pe, 0)
            with pe.Fori(0, GROUPS - 1) as g:
                second_pass(pe, g, True)
            second_pass(pe, GROUPS - 1, False)

        @block.scalar
        def _(act):
            act.sem_inc(s["o_copied"], 1)
            for r in range(KH * N):
                act.wait_ge(s["gu_ready"], r + 1)
                if r >= 2:
                    act.wait_ge(s["gu_read"], r - 1)
                act.activation(act_gate[:, r % 2, :], pgu[:, r % 2, 0, :], ACT.Silu).then_inc(s["silu_done"], 1)
            for n in range(N):
                act.wait_ge(s["down_ready"], n + 1)
                act.activation(mix_gate[:, 4 * n:4 * n + 4, :], pdown[:, n % 2, :].rearrange("p (t c) -> p t c", t=4),
                               ACT.Silu).then_inc(s["gate_done"], 1)
            act.sem_inc(s["exp_done"], 2)
            with act.Fori(0, GROUPS) as g:
                for j in range(32):
                    kt = j // 4
                    act.wait_ge(s["scores_ready"], g * 32 + (j + 1))
                    if j % 4 == 0:
                        if kt >= 2:
                            act.wait_ge(s["pv_done"], g * QT + kt)
                    act.activation(probs[:, j % 8, :], pst[:, j % 2, :], ACT.Exp).then_inc(s["exp_done"], 1)
                act.wait_ge(s["pv_done"], (g + 1) * QT + 1)
                act.activation(o_all[:, bass.ds(g, 1), :].rearrange("p o q -> p (o q)"), po[:, :], ACT.Copy).then_inc(s["o_copied"], 1)

        def maxima(dve, g):
            for h in range(HEADS_PER_GROUP):
                dve.tensor_scalar(window[:, h, 3 * P:4 * P], tri[:, :],
                                  s8[:, bass.ds((g % HEAD_GROUPS) * HEADS_PER_GROUP + h, 1)], None, ALU.mult).then_inc(s["center_done"], 1)
            dve.wait_ge(s["center_done"], (g + 1) * 4)
            for n in range(64):
                h, qt, half = n // 16, n // 2 % 8, n % 2
                dve.wait_ge(s["maxs_ready"], g * 64 + (n + 1))
                if qt // 4 == half:
                    if n >= 2:
                        dve.wait_ge(s["maxs_free"], g * 65 + (n - 1))
                    dve.sem_inc(s["begun"], 1)
                    o = 3 * P - P * (qt % 4)
                    dve.tensor_tensor_reduce(junk[:, half, :], pmax[:, n % 2, :], window[:, h, o:o + HALF], 1.0, -3e38,
                                             ALU.add, ALU.max, mx[:, n // 2, half:half + 1]).then_inc(s["maxs_free"], 1)
                else:
                    dve.tensor_reduce(mx[:, n // 2, half:half + 1], pmax[:, n % 2, :], AX.X, ALU.max).then_inc(s["maxs_free"], 1)
            dve.wait_ge(s["maxs_free"], g * 65 + 64)
            dve.tensor_reduce(neg[:, :], mx[:, :, :], AX.X, ALU.max, negate=True).then_inc(s["neg_done"], 1)
            dve.wait_ge(s["neg_done"], g + 1)
            dve.tensor_copy(negp[:, 0, :], neg[:, :]).then_inc(s["mp0"], 1)
            dve.wait_ge(s["mp0"], g + 1)
            dve.tensor_tensor(neg[:, :], neg[:, :], negp[:, 0, :], ALU.subtract).then_inc(s["mr0"], 1)
            dve.wait_ge(s["mr0"], g + 1)
            dve.tensor_copy(negp[:, 1, :], neg[:, :]).then_inc(s["mp1"], 1)
            dve.wait_ge(s["mp1"], g + 1)
            dve.tensor_tensor(negp[:, 2, :], neg[:, :], negp[:, 1, :], ALU.subtract).then_inc(s["mp2"], 1)
            dve.wait_ge(s["m_turned"], g + 1)
            dve.wait_ge(s["m_stored"], g * 48 + 16)
            dve.tensor_copy(neg_rows[:, :], pmax[0:96, 0, 0:P // 2].bitcast(BF16)).then_inc(s["m_copied"], 1)
            dve.wait_ge(s["m_copied"], g + 1)
            dve.sem_inc(s["maxs_free"], 1)

        @block.vector
        def _(dve):
            for r in range(KH * N):
                n, m = r // KH, r % KH
                dve.wait_ge(s["silu_done"], r + 1)
                dve.tensor_tensor(hT[:, m, n * HALF:(n + 1) * HALF], act_gate[:, r % 2, :], pgu[:, r % 2, 1, :],
                                  ALU.mult).then_inc(s["gu_read"], 1)
            dve.wait_ge(s["w_zero"], 1)
            dve.wait_ge(s["gtri_loaded"], 32)
            with dve.Fori(0, GROUPS) as g:
                maxima(dve, g)


def project_and_mix(nc, whole, d, ident, o_all, x, mix_gate, w_proj, bias, loaded):
    names = ("turned", "recip", "o_read", "o_turned", "oT_copied", "proj_ready", "proj_read", "mul_done", "x_done")
    s = {n: whole.sem("d_" + n) for n in names}
    N = TOK // HALF
    with ExitStack() as st:
        c = Core(nc, st)
        recip = c.sb("d_recip", [P, TILES, HEADS])
        o_tok = c.sb("d_o_tok", [P, TILES, DIM])
        oT = c.sb("d_oT", [P, TOK])
        mix = c.sb("d_mix", [P, TILES, DIM])
        pturn = c.ps("d_pturn", [P, 4, HALF])
        pturn2 = c.ps("d_pturn2", [P, 2, HALF])
        prow = c.ps("d_prow", [P, 2, HALF])
        block = st.enter_context(nc.Block())

        @block.tensor
        def _(pe):
            def rows_of(n):
                pe.wait_ge(s["o_read"], 4 * n + 4)
                if n >= 2:
                    pe.wait_ge(s["oT_copied"], n - 1)
                for t in range(4 * n, 4 * n + 4):
                    mm = pe.transpose(pturn2[:, n % 2, t % 4 * P:(t % 4 + 1) * P], o_tok[:, t, :], ident[:, :])
                mm.then_inc(s["o_turned"], 1)

            def project(n):
                pe.wait_ge(loaded, 32)
                pe.wait_ge(s["oT_copied"], n + 1)
                if n >= 2:
                    pe.wait_ge(s["proj_read"], n - 1)
                for t in range(4 * n, 4 * n + 4):
                    mm = pe.matmul(prow[:, n % 2, t % 4 * P:(t % 4 + 1) * P], oT[:, t * P:(t + 1) * P], w_proj[:, :],
                                   start=True, stop=True)
                mm.then_inc(s["proj_ready"], 1)

            for t in range(TILES):
                b, qt = t // QT, t % QT
                if t >= 4:
                    pe.wait_ge(s["o_read"], t - 3)
                for hg in range(HEAD_GROUPS):
                    mm = pe.transpose(pturn[:, t % 4, hg * P:(hg + 1) * P],
                                      o_all[:, b * HEAD_GROUPS + hg, qt * P:(qt + 1) * P], ident[:, :])
                mm.then_inc(s["turned"], 1)
                if t >= 7 and t % 4 == 3:
                    rows_of(t // 4 - 1)
                    if t >= 11:
                        project(t // 4 - 2)
            rows_of(N - 1)
            project(N - 2)
            project(N - 1)

        @block.scalar
        def _(act):
            for n in range(N):
                act.wait_ge(s["o_turned"], n + 1)
                act.activation(oT[:, n * HALF:(n + 1) * HALF], pturn2[:, n % 2, :], ACT.Copy).then_inc(s["oT_copied"], 1)

        @block.gpsimd
        def _(pool):
            for n in range(N):
                tt = slice(4 * n, 4 * n + 4)
                pool.wait_ge(s["mul_done"], n + 1)
                pool.tensor_tensor(x[:, tt, :], x[:, tt, :], mix[:, tt, :], ALU.add).then_inc(s["x_done"], 1)

        @block.vector
        def _(dve):
            def mixed(n):
                tt = slice(4 * n, 4 * n + 4)
                dve.wait_ge(s["proj_ready"], n + 1)
                dve.wait_ge(loaded, 32)
                dve.tensor_tensor(mix[:, tt, :], prow[:, n % 2, :].rearrange("p (t c) -> p t c", t=4),
                                  bias[:, :].unsqueeze(1).to_broadcast([P, 4, DIM]), ALU.add).then_inc(s["proj_read"], 1)
                dve.wait_ge(s["proj_read"], n + 1)
                dve.tensor_tensor(mix[:, tt, :], mix[:, tt, :], mix_gate[:, tt, :], ALU.mult).then_inc(s["mul_done"], 1)

            for t in range(TILES):
                v = pturn[:, t % 4, :].rearrange("p (h x) -> p h x", h=HEADS)
                dve.wait_ge(s["turned"], t + 1)
                dve.reciprocal(recip[:, t, :], v[:, :, HEAD_DIM]).then_inc(s["recip"], 1)
                dve.wait_ge(s["recip"], t + 1)
                dve.tensor_tensor(o_tok[:, t, :].rearrange("p (h x) -> p h x", h=HEADS), v[:, :, 0:HEAD_DIM],
                                  recip[:, t, :].unsqueeze(2).to_broadcast([P, HEADS, HEAD_DIM]), ALU.mult).then_inc(s["o_read"], 1)
            for n in range(N):
                mixed(n)


ALL_EXPERTS = EXPERTS + 2
EXP_HID = 256


def expert_constants(whole, c, d):
    t = {"gate_loaded": whole.sem("e_gate_loaded"), "b_loaded": whole.sem("e_b_loaded"),
         "w1_loaded": [whole.sem(f"e_w1_loaded{i}") for i in range(2)],
         "w2_loaded": [whole.sem(f"e_w2_loaded{i}") for i in range(2)],
         "w_gate": c.sb("e_w_gate", [P, EXPERTS]), "b_gate": c.sb("e_b_gate", [P, EXPERTS]),
         "restart": c.sb("e_restart", [P, TILES, EXPERTS]),
         "b1": c.sb("e_b1", [P, ALL_EXPERTS, 2]), "b2": c.sb("e_b2", [ALL_EXPERTS, DIM]),
         "w1": c.sb("e_w1", [P, 2, EXP_HID]), "w2": c.sb("e_w2", [P, 2, 2, DIM])}
    loads = [(t["w_gate"][:, :], d["gate_w"], t["gate_loaded"]),
             (t["b_gate"][:, :], d["gate_b"].partition_broadcast(P), t["gate_loaded"]),
             (t["restart"][:, :, :], d["restart"], t["gate_loaded"]),
             (t["b1"][:, :, :], d["experts_b1"], t["b_loaded"]), (t["b2"][:, :], d["experts_b2"], t["b_loaded"])]
    for par in range(2):
        loads += [(t["w1"][:, par, :], d["experts_w1"][par], t["w1_loaded"][par]),
                  (t["w2"][:, par, :, :], d["experts_w2"][par], t["w2_loaded"][par])]
    return t, loads


def experts(nc, whole, d, ident, xn, xnT, gate_out, consts, ahead):
    names = ("logit_ready", "logit", "top", "shift", "expo", "total", "inv", "weight", "best", "gt", "eq", "ngt", "room",
             "cum", "allow", "both", "pick", "ones", "gated", "g_turned", "g_copied", "b2_ready", "acc_ready", "h_ready", "h_done",
             "y_ready", "y_read", "silu_done", "begun")
    s = {n: whole.sem("e_" + n) for n in names}
    s["gate_loaded"], s["b_loaded"] = consts["gate_loaded"], consts["b_loaded"]
    w1_loaded, w2_loaded = consts["w1_loaded"], consts["w2_loaded"]
    w_gate, b_gate, restart, b1, b2, w1, w2 = (consts[n] for n in ("w_gate", "b_gate", "restart", "b1", "b2", "w1", "w2"))
    E, A = EXPERTS, ALL_EXPERTS
    with ExitStack() as st:
        c = Core(nc, st)
        hT = c.sb("e_hT", [P, 2, 2, TOK])
        wt = c.sb("e_wt", [P, TILES, E])
        small = c.sb("e_small", [P, 5, TILES])
        best = c.sb("e_best", [P, TILES, 8])
        gt = c.sb("e_gt", [P, TILES, E])
        eq = c.sb("e_eq", [P, TILES, E])
        cum = c.sb("e_cum", [P, TILES, E])
        gates = c.sb("e_gates", [P, A, TILES])
        gates_tok = c.sb("e_gates_tok", [P, TILES, A])
        gT = c.sb("e_gT", [A, TOK])
        ph = c.ps("e_ph", [P, 2, SEQ])
        py = c.ps("e_py", [P, 2, HALF])
        pg = c.ps("e_pg", [P, 2, HALF])
        block = st.enter_context(nc.Block())
        wide = lambda v: v.unsqueeze(2).to_broadcast([P, TILES, E])

        def load_w1(sp, e, par):
            sp.dma_start(w1[:, par, :], d["experts_w1"][bass.ds(e, 1)].rearrange("o c f -> (o c) f")).then_inc(w1_loaded[par], 16)

        def load_w2(sp, e, par):
            sp.dma_start(w2[:, par, :, :], d["experts_w2"][bass.ds(e, 1)].rearrange("o f k c -> (o f) k c")).then_inc(w2_loaded[par], 16)

        @block.sync
        def _(sp):
            load_ahead(sp, ahead)
            with sp.Fori(0, (A - 3) // 2) as i:
                for par in range(2):
                    sp.wait_ge(s["h_ready"], i * 8 + 4 * (par + 1))
                    load_w1(sp, i * 2 + (par + 2), par)
                    sp.wait_ge(s["y_ready"], i * 8 + 4 * (par + 1))
                    load_w2(sp, i * 2 + (par + 2), par)
            sp.wait_ge(s["h_ready"], 4 * (A - 2))
            load_w1(sp, A - 1, 0)
            sp.wait_ge(s["y_ready"], 4 * (A - 2))
            load_w2(sp, A - 1, 0)

        def hidden(pe, e, par, uses):
            pe.wait_ge(w1_loaded[par], uses * 16)
            for u in range(4):
                m, half = u // 2, u % 2
                pe.wait_ge(s["h_done"], e * 4 + (u + 1))
                for j in range(2):
                    at = half * SEQ + j * HALF
                    mm = pe.matmul(ph[:, u % 2, j * HALF:(j + 1) * HALF], w1[:, par, m * P:(m + 1) * P], xnT[:, at:at + HALF],
                                   start=True, stop=True)
                mm.then_inc(s["h_ready"], 1)

        def output(pe, e, par, uses):
            pe.wait_ge(w2_loaded[par], uses * 16)
            pe.wait_ge(s["h_done"], e * 4 + 6)
            for r in range(4):
                pe.wait_ge(s["y_read"], e * 16 + (4 * r + 12))
                for t in range(4 * r, 4 * r + 4):
                    for k in range(2):
                        mm = pe.matmul(py[:, r % 2, t % 4 * P:(t % 4 + 1) * P], hT[:, par, k, t * P:(t + 1) * P],
                                       w2[:, par, k, :], start=(k == 0), stop=(k == 1))
                mm.then_inc(s["y_ready"], 1)

        @block.tensor
        def _(pe):
            pe.wait_ge(s["gate_loaded"], 48)
            for t in range(TILES):
                mm = pe.matmul(pg[:, 0, t * 16:t * 16 + E], xnT[:, t * P:(t + 1) * P], w_gate[:, :], start=True, stop=True)
            mm.then_inc(s["logit_ready"], 1)
            hidden(pe, 0, 0, 1)
            pe.wait_ge(s["gated"], 1)
            for n in range(TILES // 4):
                if n >= 1:
                    pe.wait_ge(s["g_copied"], n)
                for t in range(4 * n, 4 * n + 4):
                    mm = pe.transpose(pg[0:A, 1, t % 4 * P:(t % 4 + 1) * P], gates_tok[:, t, :], ident[:, :])
                mm.then_inc(s["g_turned"], 1)
            pe.wait_ge(s["g_copied"], TILES // 4)
            pe.wait_ge(s["b_loaded"], 32)
            for n in range(TILES // 4):
                if n >= 1:
                    pe.wait_ge(s["acc_ready"], n)
                for t in range(4 * n, 4 * n + 4):
                    mm = pe.matmul(pg[:, 0, t % 4 * P:(t % 4 + 1) * P], gT[:, t * P:(t + 1) * P], b2[:, :], start=True, stop=True)
                mm.then_inc(s["b2_ready"], 1)
            with pe.Fori(0, (A - 1) // 2) as i:
                hidden(pe, i * 2 + 1, 1, i + 1)
                output(pe, i * 2, 0, i + 1)
                hidden(pe, i * 2 + 2, 0, i + 2)
                output(pe, i * 2 + 1, 1, i + 1)
            output(pe, A - 1, 0, (A + 1) // 2)

        @block.scalar
        def _(act):
            act.sem_inc(s["h_done"], 2)
            act.wait_ge(s["shift"], 1)
            act.activation(wt[:, :, :], wt[:, :, :], ACT.Exp).then_inc(s["expo"], 1)
            act.wait_ge(s["b_loaded"], 32)

            def transposed():
                for n in range(TILES // 4):
                    act.wait_ge(s["g_turned"], n + 1)
                    act.activation(gT[:, n * HALF:(n + 1) * HALF], pg[0:A, 1, :], ACT.Copy).then_inc(s["g_copied"], 1)

            def first(e, par):
                for u in range(4):
                    m, half = u // 2, u % 2
                    act.wait_ge(s["h_ready"], e * 4 + u + 1)
                    act.activation(hT[:, par, m, half * SEQ:(half + 1) * SEQ], ph[:, u % 2, :], ACT.Gelu,
                                   bias=b1[:, e, m:m + 1]).then_inc(s["h_done"], 1)

            first(0, 0)
            transposed()
            first(1, 1)
            with act.Fori(1, (A - 1) // 2) as i:
                for par in range(2):
                    for u in range(4):
                        m, half = u // 2, u % 2
                        if u == 0:
                            act.wait_ge(s["y_ready"], i * 8 + 4 * (par - 1))
                        act.wait_ge(s["h_ready"], i * 8 + (4 * par + u + 1))
                        act.sem_inc(s["begun"], 1)
                        bias = b1[:, bass.ds(i * 2 + par, 1), m:m + 1].rearrange("p o m -> p (o m)")
                        act.activation(hT[:, par, m, half * SEQ:(half + 1) * SEQ], ph[:, u % 2, :], ACT.Gelu,
                                       bias=bias).then_inc(s["h_done"], 1)
            act.wait_ge(s["y_ready"], 4 * (A - 2))
            first(A - 1, 0)
            for n in range(4):
                act.wait_ge(s["y_read"], TILES * A + 4 * n + 4)
                act.activation(gate_out[:, 4 * n:4 * n + 4, :], gate_out[:, 4 * n:4 * n + 4, :], ACT.Silu).then_inc(s["silu_done"], 1)

        @block.vector
        def _(dve):
            inc = lambda ins, name: (ins.then_inc(s[name], 1), dve.wait_ge(s[name], 1))
            dve.wait_ge(s["gate_loaded"], 48)
            dve.wait_ge(s["logit_ready"], 1)
            mx, total, inv, ngt, room = (small[:, n, :] for n in range(5))
            inc(dve.tensor_tensor(wt[:, :, :], pg[:, 0, 0:16 * TILES].rearrange("p (t e) -> p t e", e=16)[:, :, 0:E],
                                  b_gate[:, :].unsqueeze(1).to_broadcast([P, TILES, E]), ALU.add), "logit")
            inc(dve.tensor_reduce(mx, wt[:, :, :], AX.X, ALU.max), "top")
            dve.tensor_tensor(wt[:, :, :], wt[:, :, :], wide(mx), ALU.subtract).then_inc(s["shift"], 1)
            dve.wait_ge(s["expo"], 1)
            inc(dve.tensor_reduce(total, wt[:, :, :], AX.X, ALU.add), "total")
            inc(dve.reciprocal(inv, total), "inv")
            inc(dve.tensor_tensor(wt[:, :, :], wt[:, :, :], wide(inv), ALU.mult), "weight")
            for t in range(TILES):
                dve.max(best[:, t, :], wt[:, t, :]).then_inc(s["best"], 1)
            dve.wait_ge(s["best"], TILES)
            third = wide(best[:, :, TOP_K - 1])
            inc(dve.tensor_tensor(gt[:, :, :], wt[:, :, :], third, ALU.is_gt), "gt")
            inc(dve.tensor_tensor(eq[:, :, :], wt[:, :, :], third, ALU.is_equal), "eq")
            inc(dve.tensor_reduce(ngt, gt[:, :, :], AX.X, ALU.add), "ngt")
            inc(dve.tensor_scalar(room, ngt, -1.0, float(TOP_K), ALU.mult, ALU.add), "room")
            inc(dve.tensor_tensor_scan(cum[:, :, :].rearrange("p t e -> p (t e)"), restart[:, :, :].rearrange("p t e -> p (t e)"),
                                       eq[:, :, :].rearrange("p t e -> p (t e)"), 0.0, ALU.mult, ALU.add), "cum")
            inc(dve.tensor_tensor(cum[:, :, :], cum[:, :, :], wide(room), ALU.is_le), "allow")
            inc(dve.tensor_tensor(eq[:, :, :], eq[:, :, :], cum[:, :, :], ALU.mult), "both")
            inc(dve.tensor_tensor(gt[:, :, :], gt[:, :, :], eq[:, :, :], ALU.add), "pick")
            dve.memset(gates_tok[:, :, E:A], 1.0).then_inc(s["ones"], 1)
            dve.memset(gates[:, E:A, :], 1.0).then_inc(s["ones"], 1)
            dve.tensor_tensor(gates[:, 0:E, :].rearrange("p e t -> p t e"), wt[:, :, :], gt[:, :, :], ALU.mult).then_inc(s["ones"], 1)
            dve.wait_ge(s["ones"], 3)
            dve.tensor_tensor(gates_tok[:, :, 0:E], wt[:, :, :], gt[:, :, :], ALU.mult).then_inc(s["gated"], 1)
            for n in range(TILES // 4):
                dve.wait_ge(s["b2_ready"], n + 1)
                dve.tensor_tensor(gate_out[:, 4 * n:4 * n + 4, :], pg[:, 0, :].rearrange("p (t c) -> p t c", t=4),
                                  xn[:, 4 * n:4 * n + 4, :], ALU.add).then_inc(s["acc_ready"], 1)
            dve.wait_ge(s["acc_ready"], TILES // 4)
            dve.sem_inc(s["y_read"], TILES)

            with dve.Fori(0, A) as e:
                for t in range(TILES):
                    if t % 4 == 0:
                        dve.wait_ge(s["y_ready"], e * 4 + (t // 4 + 1))
                        dve.wait_ge(s["y_read"], e * 16 + (t + 4))
                    dve.scalar_tensor_tensor(out=gate_out[:, t, :], in0=py[:, t // 4 % 2, t % 4 * P:(t % 4 + 1) * P],
                                             scalar=gates[:, bass.ds(e, 1), t:t + 1].rearrange("p o t -> p (o t)"),
                                             in1=gate_out[:, t, :], op0=ALU.mult, op1=ALU.add).then_inc(s["y_read"], 1)


LAYERS, INNER, STATE, RANK, TAPS = 4, 256, 16, 8, 4
NH = INNER // P
COLS = TAPS + 1 + 1 + STATE + 1
X_ROWS = 3 * 2 * STATE + RANK


def mamba_weights(whole, c, d):
    t = {"w_loaded": whole.sem("m_w_loaded"), "wo_loaded": whole.sem("m_wo_loaded"), "sel_loaded": whole.sem("m_sel_loaded"),
         "sel": c.sb("m_sel", [6 * STATE, 2 * STATE, P], BF16),
         "w": c.sb("m_w", [P, 2 * INNER + NH * X_ROWS + NH * COLS]),
         "w_dt": c.sb("m_w_dt", [X_ROWS, INNER]), "w_out": c.sb("m_w_out", [P, NH, DIM])}
    loads = [(t["w"][:, :], d["mamba_w"][0], t["w_loaded"]),
             (t["w_dt"][X_ROWS - RANK:X_ROWS, :], d["mamba_w_dt"][0], t["w_loaded"]),
             (t["sel"][:, :, :], d["select"], t["sel_loaded"]), (t["w_out"][:, :, :], d["mamba_w_out"][0], t["wo_loaded"])]
    return t, loads


def mamba(nc, whole, d, ident, u, decay_xn, weights_of):
    names = ("pad_zero", "pre_ready", "pre_read", "tap0", "taps", "xc_done", "zs_done", "bc0",
             "bc1", "bc_ready", "dl_exp", "dl_ln", "delta", "du_done", "a_exp", "a_neg", "xd_done",
             "b_ready", "b_copied", "c_ready", "exp_done", "drive_done", "scan_done", "prod_done", "y_done",
             "yg_done", "out_ready", "u_done", "begun", "act_begun", "sp_begun")
    s = {n: whole.sem("m_" + n) for n in names}
    with ExitStack() as st:
        c = Core(nc, st)
        s["w_loaded"], s["wo_loaded"], s["sel_loaded"], sel, w, w_dt, w_out = (
            weights_of[n] for n in ("w_loaded", "wo_loaded", "sel_loaded", "sel", "w", "w_dt", "w_out"))
        w_in = w[:, 0:2 * INNER]
        w_x = w[:, 2 * INNER:2 * INNER + NH * X_ROWS].rearrange("p (k r) -> p k r", k=NH)
        cols = w[:, 2 * INNER + NH * X_ROWS:].rearrange("p (k r) -> p k r", k=NH)
        pad = c.sb("m_pad", [P, NH, TAPS - 1 + SEQ])
        zs = c.sb("m_zs", [P, NH, BATCH, SEQ])
        cv = c.sb("m_cv", [P, NH, BATCH, SEQ])
        xc = c.sb("m_xc", [P, NH, BATCH, SEQ])
        delta = c.sb("m_delta", [P, NH, BATCH, SEQ])
        du = c.sb("m_du", [P, NH, BATCH, SEQ])
        bcp = c.sb("m_bcp", [6 * STATE, BATCH, SEQ], BF16)
        bcq = c.sb("m_bcq", [6 * STATE, SEQ], BF16)
        bcr = c.sb("m_bcr", [6 * STATE, SEQ])
        dts = c.sb("m_dts", [X_ROWS, SEQ])
        a_pos = c.sb("m_a_pos", [P, NH, STATE])
        neg_a = c.sb("m_neg_a", [P, 2, NH * STATE])
        b_sb = c.sb("m_b_sb", [P, 4, SEQ])
        decay_more = c.sb("m_decay_more", [P, 2, SEQ])
        decay = (decay_xn[:, 0, :], decay_xn[:, 1, :], decay_more[:, 0, :], decay_more[:, 1, :])
        drive = c.sb("m_drive", [P, 2, SEQ])
        state = c.sb("m_state", [P, 2, SEQ])
        prod = c.sb("m_prod", [P, 2, SEQ])
        y = c.ps("m_y", [P, NH, SEQ])
        p_c = c.ps("m_p_c", [P, SEQ])
        p_b = c.ps("m_p_b", [P, HALF])
        aside = c.ps("m_aside", [P, HALF])
        block = st.enter_context(nc.Block())
        UNITS = 2 * STATE
        PRE = 14
        PE_AT = (5, 6, 7, 8, 9, 10, 11, 12, 14, 16, 20, 21, 22, 23)
        OUT_AT = (1, 4)
        XD_AT = (26, 28)
        LAG = 4
        B_LEAD = 4
        BIAS_COL, DT_COL, A_COL, D_COL = TAPS, TAPS + 1, TAPS + 2, COLS - 1
        cut = lambda n: slice(n * HALF, (n + 1) * HALF)

        def bank_of(i, alone):
            if not alone:
                return aside[:, :]
            return (y[:, 0, cut(0)], y[:, 0, cut(1)], y[:, 1, cut(0)], y[:, 1, cut(1)],
                    p_c[:, cut(0)], p_c[:, cut(1)], p_b[:, :], aside[:, :])[i % 8]

        def passes(e, first, one):
            first()
            one(0, 0, (0, 1), None)
            with e.Fori(0, LAYERS - 1) as l:
                one(l, 1, (l + 1, 0), (l, 0))
                one(l + 1, 0, (l + 1, 1), (l, 1))
            one(LAYERS - 1, 1, None, (LAYERS - 1, 0))

        @block.sync
        def _(sp):
            def weights(l):
                sp.dma_start(w[:, :], d["mamba_w"][bass.ds(l, 1)].rearrange("o p f -> (o p) f")).then_inc(s["w_loaded"], 16)
                sp.dma_start(w_dt[X_ROWS - RANK:X_ROWS, :], d["mamba_w_dt"][bass.ds(l, 1)].rearrange("o r f -> (o r) f")).then_inc(s["w_loaded"], 16)

            def out_weights(l):
                sp.dma_start(w_out[:, :, :], d["mamba_w_out"][bass.ds(l, 1)].rearrange("o p k f -> (o p) k f")).then_inc(s["wo_loaded"], 16)

            with sp.Fori(0, LAYERS - 1) as l:
                sp.wait_ge(s["xd_done"], l * BATCH + 2)
                sp.wait_ge(s["pre_read"], (l * BATCH + 2) * PRE + 1)
                sp.sem_inc(s["sp_begun"], 1)
                weights(l + 1)
                sp.wait_ge(s["u_done"], (l * BATCH + 2) * 2 + 3)
                sp.sem_inc(s["sp_begun"], 1)
                out_weights(l + 1)

        @block.tensor
        def _(pe):
            def prepare(l, b, i, alone=False):
                K = l * BATCH + b
                bank = bank_of(i, alone)
                if i == 0:
                    pe.wait_ge(s["w_loaded"], l * 32 + 32)
                    pe.wait_ge(s["u_done"], K * 2 + 1)
                if not alone or i in (8, 10):
                    pe.wait_ge(s["pre_read"], K * PRE + (i + 1))
                if i < 8:
                    m, n = i // 2, i % 2
                    mm = pe.matmul(bank[:, :], w_in[:, m * P:(m + 1) * P], u[:, b * SEQ + n * HALF:b * SEQ + (n + 1) * HALF],
                                   start=True, stop=True)
                elif i < 10:
                    n = i - 8
                    pe.wait_ge(s["xc_done"], K + 1)
                    for k in range(NH):
                        mm = pe.matmul(bank[0:X_ROWS, :], w_x[:, k, :], xc[:, k, b, cut(n)], start=(k == 0), stop=(k == NH - 1))
                else:
                    h, n = (i - 10) % 2, (i - 10) // 2
                    pe.wait_ge(s["bc0"], K * 2 + 2)
                    mm = pe.matmul(bank[:, :], w_dt[X_ROWS - RANK:X_ROWS, h * P:(h + 1) * P], dts[X_ROWS - RANK:X_ROWS, cut(n)],
                                   start=True, stop=True)
                mm.then_inc(s["pre_ready"], 1)

            def output(l, b, n, prepared):
                K = l * BATCH + b
                if n == 0:
                    pe.wait_ge(s["yg_done"], K * NH + 4)
                    pe.wait_ge(s["wo_loaded"], l * 16 + 16)
                    pe.wait_ge(s["pre_read"], prepared * PRE + 1)
                pe.wait_ge(s["u_done"], K * 2 + (n + 3))
                for k in range(NH):
                    mm = pe.matmul(aside[:, :], w_out[:, k, :], cv[:, k, b, cut(n)], start=(k == 0), stop=(k == NH - 1))
                mm.then_inc(s["out_ready"], 1)

            def b_row(K, si, b, n):
                if si == 0 and n == 0:
                    pe.wait_ge(s["bc_ready"], K * 2 + 2)
                pe.wait_ge(s["b_copied"], (K * STATE + si) * 2 + (n + 1))
                pe.matmul(p_b[:, :], sel[:, si, :], bcp[:, b, cut(n)], start=True, stop=True).then_inc(s["b_ready"], 1)

            def c_rows(K, si, b):
                pe.wait_ge(s["prod_done"], (K * STATE + si) * 2 + 2)
                for n in range(2):
                    mm = pe.matmul(p_c[:, cut(n)], sel[:, STATE + si, :], bcp[:, b, cut(n)], start=True, stop=True)
                mm.then_inc(s["c_ready"], 1)

            def add_xd(K, b, h):
                pe.wait_ge(s["xd_done"], K + 1)
                for n in range(2):
                    pe.matmul(y[:, h, cut(n)], ident[:, :], cv[:, h, b, cut(n)], start=False, stop=True,
                              skip_group_check=True)

            def add_y(K, p):
                h = p % 2
                pe.wait_ge(s["prod_done"], K * UNITS + (p + 3))
                if p < NH:
                    pe.wait_ge(s["yg_done"], K * NH + (h + 1))
                for n in range(2):
                    mm = pe.matmul(y[:, h, cut(n)], ident[:, :], prod[:, h, cut(n)], start=(p < NH), stop=True, skip_group_check=True)
                mm.then_inc(s["y_done"], 1)

            def first():
                for i in range(PRE):
                    prepare(0, 0, i, True)
                for q in range(B_LEAD):
                    b_row(0, q // 2, 0, q % 2)

            def one(l, b, following, before):
                K = l * BATCH + b
                for p in range(UNITS):
                    si, h = p // 2, p % 2
                    if h == 0:
                        c_rows(K, si, b)
                    if p > 0:
                        add_y(K, p - 1)
                    elif before:
                        add_y(K - 1, UNITS - 1)
                    if p in XD_AT:
                        add_xd(K, b, XD_AT.index(p))
                    q = p + B_LEAD
                    if q < UNITS:
                        b_row(K, q // 2, b, q % 2)
                    elif following:
                        b_row(K + 1, (q - UNITS) // 2, following[1], q % 2)
                    if before and p in OUT_AT:
                        output(before[0], before[1], OUT_AT.index(p), K + 1)
                    if following:
                        for i, at in enumerate(PE_AT):
                            if p == at:
                                prepare(following[0], following[1], i)

            pe.sem_inc(s["y_done"], 2)
            pe.wait_ge(s["sel_loaded"], 16)
            passes(pe, first, one)
            K = LAYERS * BATCH - 1
            add_y(K, UNITS - 1)
            for n in range(2):
                output(LAYERS - 1, 1, n, K + 1)

        @block.scalar
        def _(act):
            def read(l, b, i, alone=False):
                K = l * BATCH + b
                bank = bank_of(i, alone)
                act.wait_ge(s["pre_ready"], K * PRE + (i + 1))
                if i < 4:
                    m, n = i // 2, i % 2
                    at = TAPS - 1 + n * HALF
                    act.activation(pad[:, m, at:at + HALF], bank[:, :], ACT.Copy).then_inc(s["pre_read"], 1)
                    if n == 1:
                        act.wait_ge(s["pad_zero"], 1)
                        act.wait_ge(s["pre_read"], K * PRE + (i + 2))
                        act.activation(cv[:, m, b, :], pad[:, m, 0:SEQ], ACT.Identity,
                                       scale=cols[:, m, 0:1], bias=cols[:, m, BIAS_COL:BIAS_COL + 1]).then_inc(s["tap0"], 1)
                elif i < 8:
                    m, n = (i - 4) // 2, i % 2
                    act.activation(zs[:, m, b, cut(n)], bank[:, :], ACT.Copy).then_inc(s["pre_read"], 1)
                elif i < 10:
                    n = i - 8
                    act.activation(dts[X_ROWS - RANK:X_ROWS, cut(n)], bank[X_ROWS - RANK:X_ROWS, :], ACT.Copy)
                    act.activation(bcp[:, b, cut(n)], bank[0:6 * STATE, :], ACT.Copy).then_inc(s["bc0"], 1)
                else:
                    h, n = (i - 10) % 2, (i - 10) // 2
                    bias = cols[:, h, DT_COL:DT_COL + 1]
                    act.activation(cv[:, h, b, cut(n)], bank[:, :], ACT.Identity, bias=bias)
                    act.activation(delta[:, h, b, cut(n)], bank[:, :], ACT.Abs, bias=bias).then_inc(s["pre_read"], 1)

            def gates(l, b):
                K = l * BATCH + b
                act.wait_ge(s["pre_read"], K * PRE + 9)
                act.activation(zs[:, :, b, :], zs[:, :, b, :], ACT.Silu).then_inc(s["zs_done"], 1)

            def rest(l, b, p):
                K = l * BATCH + b
                if p == 17:
                    act.wait_ge(s["taps"], K * 6 + 6)
                    act.activation(xc[:, :, b, :], cv[:, :, b, :], ACT.Silu).then_inc(s["xc_done"], 1)
                if p == 23:
                    act.wait_ge(s["pre_read"], K * PRE + 11)
                    act.activation(bcq[:, :], bcr[:, :], ACT.Copy).then_inc(s["bc1"], 1)
                if p == 25 and b == 0:
                    act.activation(a_pos[:, :, :], cols[:, :, A_COL:A_COL + STATE], ACT.Exp).then_inc(s["a_exp"], 1)
                if p == 28:
                    act.wait_ge(s["pre_read"], K * PRE + (PRE + 1))
                    act.activation(delta[:, :, b, :], delta[:, :, b, :], ACT.Exp, scale=-1.0).then_inc(s["dl_exp"], 1)
                if p == 29:
                    act.wait_ge(s["dl_exp"], K + 1)
                    act.activation(delta[:, :, b, :], delta[:, :, b, :], ACT.Ln, bias=1.0).then_inc(s["dl_ln"], 1)
                if p == 30:
                    act.wait_ge(s["delta"], K + 1)
                    for h in range(NH):
                        x_d = act.activation(cv[:, h, b, :], xc[:, h, b, :], ACT.Copy, scale=cols[:, h, D_COL:D_COL + 1])
                    x_d.then_inc(s["xd_done"], 1)

            def copy_b(K, si, n):
                S = K * STATE + si
                act.wait_ge(s["b_ready"], S * 2 + (n + 1))
                act.wait_ge(s["drive_done"], S * 2 + 1)
                act.sem_inc(s["act_begun"], 1)
                act.activation(b_sb[:, si % 4, cut(n)], p_b[:, :], ACT.Copy).then_inc(s["b_copied"], 1)

            def first():
                for p in range(UNITS):
                    for i, at in enumerate(PE_AT):
                        if p == at + LAG:
                            read(0, 0, i, True)
                    rest(0, 0, p)

            def one(l, b, following, before):
                K = l * BATCH + b
                for p in range(UNITS):
                    si, h = p // 2, p % 2
                    if p == 0:
                        act.wait_ge(s["delta"], K + 1)
                        act.wait_ge(s["a_neg"], l + 1)
                    act.wait_ge(s["scan_done"], K * UNITS + (p + 1))
                    act.sem_inc(s["act_begun"], 1)
                    act.activation(decay[p % 4], delta[:, h, b, :], ACT.Exp,
                                   scale=neg_a[:, bass.ds(l % 2, 1), h * STATE + si:h * STATE + si + 1].rearrange("p o a -> p (o a)")).then_inc(s["exp_done"], 1)
                    copy_b(K, si, h)
                    if before and p - LAG in OUT_AT:
                        pK, n = before[0] * BATCH + before[1], OUT_AT.index(p - LAG)
                        act.wait_ge(s["out_ready"], pK * 2 + (n + 1))
                        act.sem_inc(s["act_begun"], 1)
                        at = before[1] * SEQ + n * HALF
                        act.activation(u[:, at:at + HALF], aside[:, :], ACT.Copy).then_inc(s["u_done"], 1)
                    if following:
                        for i, at in enumerate(PE_AT):
                            if p == at + LAG:
                                read(following[0], following[1], i)
                        rest(following[0], following[1], p)
                    if p == 17:
                        gates(l, b)

            act.sem_inc(s["exp_done"], 1)
            act.sem_inc(s["u_done"], 3)
            act.sem_inc(s["b_copied"], 1)
            act.sem_inc(s["pre_read"], 1)
            passes(act, first, one)
            K = LAYERS * BATCH - 1
            for n in range(2):
                act.wait_ge(s["out_ready"], K * 2 + (n + 1))
                act.activation(u[:, SEQ + n * HALF:SEQ + (n + 1) * HALF], aside[:, :], ACT.Copy).then_inc(s["u_done"], 1)

        @block.gpsimd
        def _(pool):
            def first():
                pool.memset(pad[:, :, 0:TAPS - 1], 0.0).then_inc(s["pad_zero"], 1)
                pool.sem_inc(s["drive_done"], 7)

            def one(l, b, following, before):
                K = l * BATCH + b
                pool.wait_ge(s["du_done"], K + 1)
                pool.sem_inc(s["begun"], 1)
                for p in range(UNITS):
                    si, h = p // 2, p % 2
                    if h == 0:
                        pool.wait_ge(s["b_copied"], (K * STATE + si) * 2 + 3)
                    pool.wait_ge(s["scan_done"], K * UNITS + (p + 3))
                    pool.sem_inc(s["begun"], 1)
                    pool.tensor_tensor(drive[:, h, :], du[:, h, b, :], b_sb[:, si % 4, :], ALU.mult).then_inc(s["drive_done"], 1)

            passes(pool, first, one)

        @block.vector
        def _(dve):
            def prepare(l, b, p, alone=False):
                K = l * BATCH + b
                if 8 <= p < 14:
                    h, j = (p - 8) // 3, (p - 8) % 3 + 1
                    if j == 1:
                        dve.wait_ge(s["tap0"], K * NH + (h + 1))
                    else:
                        dve.wait_ge(s["taps"], K * 6 + (3 * h + j - 1))
                    dve.scalar_tensor_tensor(out=cv[:, h, b, :], in0=pad[:, h, j:j + SEQ], scalar=cols[:, h, j:j + 1], in1=cv[:, h, b, :],
                                             op0=ALU.mult, op1=ALU.add).then_inc(s["taps"], 1)
                if p in (16, 19):
                    n = (p - 16) // 3
                    dve.wait_ge(s["bc0"], K * 2 + (n + 1))
                    dve.tensor_tensor(bcr[:, cut(n)], bank_of(8 + n, alone)[0:6 * STATE, :], bcp[:, b, cut(n)], ALU.subtract).then_inc(s["pre_read"], 1)
                if p == 22:
                    dve.wait_ge(s["bc1"], K + 1)
                    dve.tensor_copy(bcp[32:64, b, :], bcq[32:64, :]).then_inc(s["bc_ready"], 1)
                    dve.tensor_tensor(bcp[64:96, b, :], bcr[64:96, :], bcq[64:96, :], ALU.subtract).then_inc(s["bc_ready"], 1)
                if p == 24 and b == 0:
                    dve.wait_ge(s["a_exp"], l + 1)
                    dve.tensor_scalar(neg_a[:, bass.ds(l % 2, 1), :].rearrange("p o a -> p (o a)"),
                                      a_pos[:, :, :].rearrange("p h a -> p (h a)"), -1.0, None, ALU.mult).then_inc(s["a_neg"], 1)
                if p == 27:
                    dve.wait_ge(s["dl_ln"], K + 1)
                    dve.scalar_tensor_tensor(out=delta[:, :, b, :], in0=cv[:, :, b, :], scalar=0.0, in1=delta[:, :, b, :],
                                             op0=ALU.max, op1=ALU.add).then_inc(s["delta"], 1)
                if p == 28:
                    dve.wait_ge(s["delta"], K + 1)
                    dve.tensor_tensor(du[:, :, b, :], delta[:, :, b, :], xc[:, :, b, :], ALU.mult).then_inc(s["du_done"], 1)

            def gate_y(l, b, h):
                K = l * BATCH + b
                dve.wait_ge(s["y_done"], K * UNITS + (UNITS + 1 + h))
                dve.wait_ge(s["zs_done"], K + 1)
                dve.tensor_tensor(cv[:, h, b, :], y[:, h, :], zs[:, h, b, :], ALU.mult).then_inc(s["yg_done"], 1)

            def first():
                for p in range(UNITS):
                    prepare(0, 0, p, True)

            def one(l, b, following, before):
                K = l * BATCH + b
                for p in range(UNITS):
                    U, h = K * UNITS + p, p % 2
                    dve.wait_ge(s["exp_done"], U + 2)
                    dve.wait_ge(s["drive_done"], U + 8)
                    dve.wait_ge(s["prod_done"], U + 1)
                    dve.tensor_tensor_scan(state[:, h, :], decay[p % 4], drive[:, h, :], 0.0, ALU.mult, ALU.add).then_inc(s["scan_done"], 1)
                    if before and p < NH:
                        gate_y(before[0], before[1], p)
                    if following:
                        prepare(following[0], following[1], p)
                    dve.wait_ge(s["scan_done"], U + 5)
                    dve.wait_ge(s["c_ready"], K * STATE + (p // 2 + 1))
                    dve.wait_ge(s["y_done"], U + 1)
                    dve.tensor_tensor(prod[:, h, :], state[:, h, :], p_c[:, :], ALU.mult).then_inc(s["prod_done"], 1)

            dve.sem_inc(s["scan_done"], 4)
            dve.sem_inc(s["prod_done"], 2)
            dve.sem_inc(s["yg_done"], 2)
            passes(dve, first, one)
            for h in range(NH):
                gate_y(LAYERS - 1, 1, h)


def finish(nc, whole, d, ident, x, gate, u, out):
    turned, mixed, added, stored = (whole.sem(f"f_{n}") for n in ("turned", "mixed", "added", "stored"))
    out = out.rearrange("b (t p) c -> p (b t) c", p=P)
    with ExitStack() as st:
        c = Core(nc, st)
        res = c.sb("f_res", [P, TILES, DIM])
        pt = c.ps("f_pt", [P, TILES, P])
        block = st.enter_context(nc.Block())

        @block.tensor
        def _(pe):
            for t in range(TILES):
                pe.transpose(pt[:, t, :], u[:, t * P:(t + 1) * P], ident[:, :]).then_inc(turned, 1)

        @block.vector
        def _(dve):
            for n in range(TILES // 4):
                tt = slice(4 * n, 4 * n + 4)
                dve.wait_ge(turned, 4 * n + 4)
                dve.tensor_tensor(res[:, tt, :], pt[:, tt, :], gate[:, tt, :], ALU.mult).then_inc(mixed, 1)
                dve.wait_ge(mixed, n + 1)
                dve.tensor_tensor(res[:, tt, :], res[:, tt, :], x[:, tt, :], ALU.add).then_inc(added, 1)

        @block.sync
        def _(sp):
            for n in range(TILES // 4):
                tt = slice(4 * n, 4 * n + 4)
                sp.wait_ge(added, n + 1)
                sp.dma_start(out[:, tt, :], res[:, tt, :]).then_inc(stored, 16)
            sp.wait_ge(stored, 16 * (TILES // 4))


def program(nc, d, out, debug=None):
    with ExitStack() as stack:
        whole = Core(nc, stack)
        dram = lambda name, shape, dt=F32: nc.dram_tensor(name, shape, dt, kind="Internal").ap()
        parts_scr = dram("parts_scr", (2, 3, BATCH, DIM, SEQ), BF16)
        bias_scr = dram("bias_scr", (3, GROUPS, HEADS_PER_GROUP, BIAS_R, SEQ), BF16)
        x = whole.sb("x", [P, TILES, DIM])
        xn = whole.sb("xn", [P, TILES, DIM])
        xnT = whole.sb("xnT", [P, TOK])
        ident = whole.sb("ident", [P, P])

        w_proj, bias, proj_loaded = whole.sb("d_w_proj", [P, DIM]), whole.sb("d_bias", [P, DIM]), whole.sem("d_loaded")
        proj_loads = [(w_proj[:, :], d["w_proj"], proj_loaded), (bias[:, :], d["proj_b"].partition_broadcast(P), proj_loaded)]
        expert_consts, expert_loads = expert_constants(whole, whole, d)

        with ExitStack() as st:
            c = Core(nc, st)
            o_all = c.sb("o_all", [P, GROUPS, SEQ])
            with ExitStack() as st2:
                c = Core(nc, st2)
                v_all = c.sb("v_all", [P, GROUPS, QT, 32])
                tri_all = c.sb("tri_all", [P, HEADS, P])
                s8 = c.sb("s8", [P, HEADS])
                w_ffn = c.sb("w_ffn", [P, 3, HIDDEN])
                stored = whole.sem("stored")
                with ExitStack() as st3:
                    qkv_consts, qkv_loads = qkv_constants(whole, Core(nc, st3), d)
                    layer_norm(nc, whole, "a", x, xn, xnT, ident,
                               [(x[:, :, :], d["x"].rearrange("(t p) c -> p t c", p=P)), (ident[:, :], d["ident"])], qkv_loads)
                    project_qkv(nc, whole, d, xnT, ident, v_all, tri_all, s8, w_ffn, parts_scr, bias_scr, stored, qkv_consts)
                attention(nc, whole, d, ident, v_all, tri_all, s8, parts_scr, bias_scr, o_all, xnT, w_ffn, xn, stored,
                          proj_loads + expert_loads)
            if debug == "attention":
                dump(nc, whole, out, o_all[:, 0, :])
                return
            project_and_mix(nc, whole, d, ident, o_all, x, xn, w_proj, bias, proj_loaded)
        layer_norm(nc, whole, "n", x, xn, xnT, ident, [])
        if debug == "ffn":
            dump(nc, whole, out, x[:, :, :])
            return
        gate = whole.sb("gate", [P, TILES, DIM])
        weights, weight_loads = mamba_weights(whole, whole, d)
        experts(nc, whole, d, ident, xn, xnT, gate, expert_consts, weight_loads)
        if debug == "experts":
            dump(nc, whole, out, gate[:, :, :])
            return
        mamba(nc, whole, d, ident, xnT, xn[:, :, :].rearrange("p t c -> p (t c)").rearrange("p (h t) -> p h t", h=2), weights)
        if debug == "mamba":
            dump(nc, whole, out, xnT[:, :])
            return
        finish(nc, whole, d, ident, x, gate, xnT, out)


def dump(nc, whole, out, src):
    done = whole.sem("dumped")
    with nc.Block() as block:
        @block.sync
        def _(sp):
            sp.dma_start(out, src).then_inc(done, 16)
            sp.wait_ge(done, 16)


def layout(a):
    import numpy as np

    f32 = np.float32
    w = np.asarray(a["L0_attn_qkv_w"])
    swap = np.arange(DIM).reshape(HEADS, 2, HEAD_DIM // 2)[:, ::-1].reshape(DIM)
    q, k, v = w[0:DIM], w[DIM:2 * DIM], w[2 * DIM:]
    m = {"x": np.asarray(a["L0_attn_x"]).reshape(TOK, DIM),
         "w_qkv": np.ascontiguousarray(np.stack([q, q[swap], k, k[swap], v]).transpose(2, 0, 1)),
         "slopes": np.asarray(a["L0_attn_slopes"]),
         "slopes_rows": np.ascontiguousarray(np.repeat(np.asarray(a["L0_attn_slopes"]).reshape(2, 8), BIAS_R, axis=1).T)}
    inv = f32(1.0) / np.power(f32(10000.0), np.arange(0, HEAD_DIM, 2, dtype=f32) / f32(HEAD_DIM)).astype(f32)
    ang = (np.arange(SEQ, dtype=f32)[:, None] * inv[None, :]).astype(f32).astype(np.float64)
    cos = np.tile(np.cos(ang).T, (2 * HEADS, 1))
    sin = np.tile(np.concatenate([-np.sin(ang).T, np.sin(ang).T]), (HEADS, 1))
    scale = HEAD_DIM ** -0.5
    m["rotation"] = np.ascontiguousarray(np.stack([cos * scale, sin * scale, cos, sin], axis=1).astype(f32))
    m["ident"] = np.eye(P, dtype=f32)

    bf = mybir.dt.np(BF16)
    m["ident_bf16"] = np.eye(P).astype(bf)
    i = np.arange(P)
    m["tri_qk"] = np.minimum(i[None, :] - i[:, None], 0).astype(f32)
    m["tri_kq"] = np.ascontiguousarray(m["tri_qk"].T)
    pos = np.arange(SEQ)
    rows_k, rows_q = [], []
    for b in range(1, QT):
        rows_k.append(np.where(pos < P * b, pos - P * b, 0))
        rows_q.append(pos // P == b)
    for b in range(1, QT):
        rows_k.append(np.where(pos < P * b, -1, 0))
        rows_q.append(np.where(pos // P == b, pos % P, 0))
    m["bias_keys"] = np.tile(np.stack(rows_k).astype(f32), (8, 1))
    m["bias_queries"] = np.ascontiguousarray(np.repeat(np.tile(np.stack(rows_q).astype(f32), (3, 1))[:, None, :], HEADS_PER_GROUP, axis=1)).astype(bf)
    m["ones_rows"] = np.ones((3, HEADS_PER_GROUP, SEQ), bf)
    down = np.asarray(a["L0_ffn_w_down"]).T.reshape(HIDDEN // P, P, DIM).transpose(1, 0, 2).reshape(P, HIDDEN)
    m["w_ffn"] = np.ascontiguousarray(np.stack([np.asarray(a["L0_ffn_w_gate"]).T, np.asarray(a["L0_ffn_w_up"]).T, down], axis=1))
    m["w_proj"] = np.ascontiguousarray(np.asarray(a["L0_attn_proj_w"]).T)
    m["proj_b"] = np.asarray(a["L0_attn_proj_b"])
    g = {n: np.asarray(a["L1_ffn_" + n]) for n in ("sW1", "sb1", "sW2", "sb2", "rW1", "rb1", "rW2", "rb2", "gW", "gb")}
    m["experts_w1"] = np.concatenate([g["rW1"], g["sW1"].reshape(DIM, 2, EXP_HID).transpose(1, 0, 2)])
    w2 = np.concatenate([g["rW2"], g["sW2"].reshape(2, EXP_HID, DIM)])
    m["experts_w2"] = np.ascontiguousarray(w2.reshape(ALL_EXPERTS, 2, P, DIM).transpose(0, 2, 1, 3))
    b1 = np.concatenate([g["rb1"], g["sb1"].reshape(2, EXP_HID)])
    m["experts_b1"] = np.ascontiguousarray(b1.reshape(ALL_EXPERTS, 2, P).transpose(2, 0, 1))
    m["experts_b2"] = np.concatenate([g["rb2"], g["sb2"], np.zeros((1, DIM), f32)])
    m["gate_w"], m["gate_b"] = g["gW"], g["gb"]
    restart = np.ones((P, TILES, EXPERTS), f32)
    restart[:, :, 0] = 0
    m["restart"] = restart
    t = {n: np.asarray(a["L1_attn_" + n]) for n in ("in_proj_w", "conv_w", "conv_b", "x_proj_w", "dt_proj_w", "dt_proj_b", "A_log", "D", "out_proj_w")}
    halves = lambda v: v.reshape(LAYERS, NH, P, -1).transpose(0, 2, 1, 3)
    w_x = t["x_proj_w"].transpose(0, 2, 1)
    bc, dt = w_x[:, :, RANK:], w_x[:, :, :RANK]
    m["mamba_w"] = np.ascontiguousarray(np.concatenate(
        [t["in_proj_w"].transpose(0, 2, 1)]
        + [halves(np.concatenate([bc, bc, bc, dt], axis=2)).reshape(LAYERS, P, -1)]
        + [halves(np.concatenate([t["conv_w"], t["conv_b"][:, :, None], t["dt_proj_b"][:, :, None], t["A_log"], t["D"][:, :, None]],
                                 axis=2)).reshape(LAYERS, P, -1)], axis=2))
    m["mamba_w_dt"] = np.ascontiguousarray(t["dt_proj_w"].transpose(0, 2, 1))
    m["mamba_w_out"] = np.ascontiguousarray(halves(t["out_proj_w"].transpose(0, 2, 1)))
    m["select"] = np.ascontiguousarray(np.tile(np.repeat(np.eye(2 * STATE)[:, :, None], P, axis=2), (3, 1, 1))).astype(bf)
    return m


_OUT = (BATCH, SEQ, DIM)


def kernel(**inputs):
    import concourse.bacc as bacc
    import numpy as np
    from concourse.bass_utils import run_bass_kernel_spmd

    nc = bacc.Bacc("TRN2", target_bir_lowering=False, num_devices=1)
    arrays = {f"in_{n}": np.ascontiguousarray(v) for n, v in layout(inputs).items()}
    d = {n[3:]: nc.dram_tensor(n, v.shape, mybir.dt.from_np(v.dtype), kind="ExternalInput").ap() for n, v in arrays.items()}
    out = nc.dram_tensor("out", _OUT, F32, kind="ExternalOutput").ap()
    program(nc, d, out)
    r = run_bass_kernel_spmd(nc, [arrays], core_ids=[0])
    return r.results[0]["out"]
```
